# Optimizing a Trainium2 kernel written in Bass

```python
import numpy as np
import jax
import jax.numpy as jnp

def _softmax(x, axis=-1):
    return jax.nn.softmax(x, axis=axis)

def _gelu(x):
    return jax.nn.gelu(x, approximate=True)

def _silu(x):
    return jax.nn.silu(x)

def _sigmoid(x):
    return jax.nn.sigmoid(x)

def _layernorm(x, axis=-1, eps=1e-05):
    m = jnp.mean(x, axis=axis, keepdims=True)
    v = jnp.var(x, axis=axis, keepdims=True)
    return (x - m) / jnp.sqrt(v + eps)

def _scatter_add(tgt, idx, src, axis=0):
    return tgt.at[idx].add(src)

def _segment_sum(src, seg, n):
    return jax.ops.segment_sum(src, seg, n)
kernel_name = 'mk_vit_tower_d1_tok_img1024_r4_9f3988'

def setup_inputs(seed: int=0):
    np.random.seed(seed)
    _w = jnp.asarray

    def _rec_inputs():
        import jax
        import jax.numpy as jnp
        _rk = jax.random.key(seed)
        x = -0.000125008 + 0.999885 * jax.random.normal(jax.random.fold_in(_rk, 1), (4, 512, 256, 4), jnp.float32)
        return x
    x = _rec_inputs()

    def _L0_tok_setup():
        import jax, jax.numpy as jnp
        import numpy as np
        key = jax.random.key(seed)
        k1, k2, k3 = jax.random.split(key, 3)
        B, H, I, O, Dp1 = (4, 512, 256, 256, 4)
        x = jax.random.normal(k1, (B, H, I, Dp1), dtype=jnp.float32)
        weight = 0.1 * jax.random.normal(k2, (O, Dp1), dtype=jnp.float32)
        weighted_sum = 0.1 * jax.random.normal(k3, (O, I), dtype=jnp.float32)
        return {'x': x, 'weight': weight, 'weighted_sum': weighted_sum}
    _L0_tok_all = _L0_tok_setup()
    _L0_tok_in = {k: v for k, v in _L0_tok_all.items() if k in ('weight', 'weighted_sum')}
    del _L0_tok_all

    def _L0_attn_setup():
        import jax, jax.numpy as jnp
        import numpy as np
        import math
        NUM_HEADS = 16

        def get_slopes(n):

            def pow2(n):
                start = 2 ** (-2 ** (-(math.log2(n) - 3)))
                return [start * start ** i for i in range(n)]
            if math.log2(n).is_integer():
                return pow2(n)
            c = 2 ** math.floor(math.log2(n))
            return pow2(c) + get_slopes(2 * c)[0::2][:n - c]
        key = jax.random.key(seed)
        ks = jax.random.split(key, 5)
        B, T, C = (2, 512, 256)
        return {'x': jax.random.normal(ks[0], (B, T, C), dtype=jnp.float32), 'W_qkv': jax.random.normal(ks[1], (C, 3 * C), dtype=jnp.float32) * 0.02, 'b_qkv': jax.random.normal(ks[2], (3 * C,), dtype=jnp.float32) * 0.02, 'W_proj': jax.random.normal(ks[3], (C, C), dtype=jnp.float32) * 0.02, 'b_proj': jax.random.normal(ks[4], (C,), dtype=jnp.float32) * 0.02}
    _L0_attn_all = _L0_attn_setup()
    _L0_attn_in = {k: v for k, v in _L0_attn_all.items() if k in ('W_qkv', 'b_qkv', 'W_proj', 'b_proj')}
    del _L0_attn_all

    def _L0_ffn_setup():
        import jax, jax.numpy as jnp
        import numpy as np
        E = 8
        K = 2
        CAP_FACTOR = 1.0
        key = jax.random.key(seed)
        ks = jax.random.split(key, 5)
        B, T, C, H = (4, 512, 256, 1024)
        x = jax.random.normal(ks[0], (B, T, C), dtype=jnp.float32)
        Wr = jax.random.normal(ks[1], (C, E), dtype=jnp.float32) * 0.02
        br = jnp.zeros((E,), jnp.float32)
        W1 = jax.random.normal(ks[2], (E, C, H), dtype=jnp.float32) * 0.02
        b1 = jnp.zeros((E, H), jnp.float32)
        W2 = jax.random.normal(ks[3], (E, H, C), dtype=jnp.float32) * 0.02
        b2 = jnp.zeros((E, C), jnp.float32)
        return {'x': x, 'Wr': Wr, 'br': br, 'W1': W1, 'b1': b1, 'W2': W2, 'b2': b2}
    _L0_ffn_all = _L0_ffn_setup()
    _L0_ffn_in = {k: v for k, v in _L0_ffn_all.items() if k in ('Wr', 'br', 'W1', 'b1', 'W2', 'b2')}
    del _L0_ffn_all
    return {'x': x, 'L0_tok_weight': _L0_tok_in['weight'], 'L0_tok_weighted_sum': _L0_tok_in['weighted_sum'], 'L0_attn_W_qkv': _L0_attn_in['W_qkv'], 'L0_attn_b_qkv': _L0_attn_in['b_qkv'], 'L0_attn_W_proj': _L0_attn_in['W_proj'], 'L0_attn_b_proj': _L0_attn_in['b_proj'], 'L0_ffn_Wr': _L0_ffn_in['Wr'], 'L0_ffn_br': _L0_ffn_in['br'], 'L0_ffn_W1': _L0_ffn_in['W1'], 'L0_ffn_b1': _L0_ffn_in['b1'], 'L0_ffn_W2': _L0_ffn_in['W2'], 'L0_ffn_b2': _L0_ffn_in['b2']}

def reference(x, L0_tok_weight, L0_tok_weighted_sum, L0_attn_W_qkv, L0_attn_b_qkv, L0_attn_W_proj, L0_attn_b_proj, L0_ffn_Wr, L0_ffn_br, L0_ffn_W1, L0_ffn_b1, L0_ffn_W2, L0_ffn_b2):
    import jax
    import jax.numpy as jnp

    def _L0_tok_ref(x, weight, weighted_sum):
        import jax, jax.numpy as jnp
        import numpy as np
        return jnp.einsum('bhid,oi,od->bho', x, weighted_sum, weight)

    def _L0_attn_ref(x, W_qkv, b_qkv, W_proj, b_proj):
        import jax, jax.numpy as jnp
        import numpy as np
        import math
        NUM_HEADS = 16

        def get_slopes(n):

            def pow2(n):
                start = 2 ** (-2 ** (-(math.log2(n) - 3)))
                return [start * start ** i for i in range(n)]
            if math.log2(n).is_integer():
                return pow2(n)
            c = 2 ** math.floor(math.log2(n))
            return pow2(c) + get_slopes(2 * c)[0::2][:n - c]
        B, T, C = x.shape
        H = NUM_HEADS
        D = C // H
        qkv = x @ W_qkv + b_qkv
        q, k, v = jnp.split(qkv, 3, axis=-1)
        q = q.reshape(B, T, H, D).transpose(0, 2, 1, 3)
        k = k.reshape(B, T, H, D).transpose(0, 2, 1, 3)
        v = v.reshape(B, T, H, D).transpose(0, 2, 1, 3)
        slopes = jnp.asarray(get_slopes(H), dtype=jnp.float32)
        idx = jnp.arange(T)
        alibi = jnp.minimum(idx[None, :] - idx[:, None], 0).astype(jnp.float32)
        bias = slopes[:, None, None] * alibi
        scale = 1.0 / math.sqrt(D)
        scores = jnp.einsum('bhtd,bhsd->bhts', q, k) * scale + bias[None]
        w = jax.nn.softmax(scores, axis=-1)
        y = jnp.einsum('bhts,bhsd->bhtd', w, v)
        y = y.transpose(0, 2, 1, 3).reshape(B, T, C)
        return y @ W_proj + b_proj

    def _L0_ffn_ref(x, Wr, br, W1, b1, W2, b2):
        import jax, jax.numpy as jnp
        import numpy as np
        E = 8
        K = 2
        CAP_FACTOR = 1.0
        B, T, C = x.shape
        N = B * T
        xf = x.reshape(N, C)
        logits = xf @ Wr + br
        topv, topi = jax.lax.top_k(logits, K)
        gates = jax.nn.softmax(topv, axis=-1)
        rw = jnp.zeros((N, E), xf.dtype).at[jnp.arange(N)[:, None], topi].set(gates)
        cap = int(N * K / E * CAP_FACTOR)
        sel = jax.nn.one_hot(topi, E, dtype=jnp.int32).sum(1)
        rank = jnp.cumsum(sel, axis=0) - sel
        keep = (sel > 0) & (rank < cap)
        tok = jnp.broadcast_to(jnp.arange(N, dtype=jnp.int32)[:, None], (N, E))
        eid = jnp.broadcast_to(jnp.arange(E, dtype=jnp.int32)[None, :], (N, E))
        rank_c = jnp.where(keep, rank, cap)
        buf = jnp.full((E, cap), N, dtype=jnp.int32)
        buf = buf.at[eid, rank_c].set(tok, mode='drop')
        xpad = jnp.concatenate([xf, jnp.zeros((1, C), xf.dtype)], axis=0)
        xg = xpad[buf]
        h = jax.nn.gelu(jnp.einsum('ecd,edh->ech', xg, W1) + b1[:, None, :], approximate=False)
        out = jnp.einsum('ech,ehd->ecd', h, W2) + b2[:, None, :]
        rw_pad = jnp.concatenate([rw, jnp.zeros((1, E), rw.dtype)], axis=0)
        w = rw_pad[buf, jnp.arange(E, dtype=jnp.int32)[:, None]]
        weighted = out * w[..., None]
        final = jnp.zeros((N + 1, C), xf.dtype).at[buf.reshape(-1)].add(weighted.reshape(-1, C))
        return final[:N].reshape(B, T, C)
    h = _L0_tok_ref(x, L0_tok_weight, L0_tok_weighted_sum)
    h = h + _L0_attn_ref(_layernorm(h, axis=-1), L0_attn_W_qkv, L0_attn_b_qkv, L0_attn_W_proj, L0_attn_b_proj)
    h = h + _L0_ffn_ref(_layernorm(h, axis=-1), L0_ffn_Wr, L0_ffn_br, L0_ffn_W1, L0_ffn_b1, L0_ffn_W2, L0_ffn_b2)
    return h

_drawn_inputs = setup_inputs


def setup_inputs(seed=0):
    import zlib

    import numpy as np

    out = dict(_drawn_inputs(seed))
    spreads = {'L0_ffn_br': (0.0, 0.1), 'L0_ffn_b1': (0.0, 0.1), 'L0_ffn_b2': (0.0, 0.1)}
    factors = {}
    for name, (base, spread) in spreads.items():
        noise = np.random.default_rng([zlib.crc32(name.encode()), seed]).standard_normal(out[name].shape)
        drawn = base * np.exp(spread * noise) if base else spread * noise
        out[name] = jnp.asarray(drawn.astype(out[name].dtype))
    for name, factor in factors.items():
        out[name] = (out[name] * factor).astype(out[name].dtype)
    return out
```

```python
import math
from contextlib import ExitStack

import concourse.bass as bass
from concourse import mybir

F32 = mybir.dt.float32
F32R = mybir.dt.float32r
BF16 = mybir.dt.bfloat16
U32 = mybir.dt.uint32
ALU = mybir.AluOpType
ACT = mybir.ActivationFunctionType
AX = mybir.AxisListType

P = 128
NB, T, C = 4, 512, 256
XD = 4
NT = T // P
CH = C // P
H, D = 16, 16
NG, GH = 4, 4
N = NB * T
E, CAP, HID = 8, 512, 1024
KH = HID // P
NS = CAP // P
ROW = C + 4
TOKEN, FIRST, GATE1, GATE2 = C, C + 1, C + 2, C + 3
EPS = 1e-5
LOWEST = -3.0e38

SPLIT, MROW, BROW = 4 * D, 4 * D, 4 * D + 2
STACK = 4 * D + 8
Q_PARTS, K_PARTS = (0, 1, 0, 1), (0, 0, 1, 1)
LEAD = 28
NA = NG * NT * GH
NU = NG * 2 * GH


A_EMBED, A_VALUE, A_MAX, A_PROJ, A_ROUTE, A_RANK = 0, NT, 2 * NT, 2 * NT + NA, 3 * NT + NA, 3 * NT + NA + 1
A_USES = A_RANK + 1
B_EMBED, B_NORM, B_QK, B_SCORE, B_HEADS, B_NORM2 = 0, NT, NT + 2, NT + 4, NT + 4 + NU, NT + 5 + NU
B_USES = B_NORM2 + 1
EA_USES, EB_USES = 2 * NS, 2 * (1 + KH // 2)
assert A_USES % 2 == B_USES % 2 == EA_USES % 2 == EB_USES % 2 == 0


def slopes():
    start = 2.0 ** (-(2.0 ** -(math.log2(H) - 3)))
    return [start * start**i for i in range(H)]


class Signal:

    def __init__(self, semaphore, per, by=1):
        self.sem, self.per, self.by = semaphore, per, by
        self.credit = per * by

    def at(self, turn, use):
        assert -self.per <= use < self.per
        return turn * self.credit + (self.credit + self.by * (use + 1))


def attention_steps():
    steps = [("max", a) for a in range(18)] + [("rows", 0)] + [("max", a) for a in range(18, LEAD)]
    for u in range(NU):
        for a in (LEAD + 2 * u, LEAD + 2 * u + 1):
            if a < NA:
                steps.append(("max", a))
        if u % 8 == 2 and u // 8 + 1 < NG:
            steps.append(("rows", u // 8 + 1))
        steps.append(("scores", u))
        if u % 4 == 1 and u > 4:
            steps.append(("values", u // 4 - 1))
        if u % 8 == 3 and u > 8:
            steps.append(("heads", u // 8 - 1))
    return steps + [("values", NU // 4 - 1), ("heads", NG - 1)]


def tower(nc, x, tok_weight, tok_sum, w_qkv, b_qkv, w_proj, b_proj, w_router, b_router, w1, b1, w2, b2,
          identity, earlier, relative, relative_block, stack_rows, q_scale, expert_numbers, token_numbers,
          empty_numbers, out):
    slope = slopes()
    x_tiles = x.rearrange("b (t p) i d -> (b t) p (i d)", p=P)
    out_tiles = out.rearrange("(n p) c -> n p c", p=P)
    steps = attention_steps()
    m_order = [s for s in steps if s[0] in ("rows", "heads")]

    def heads_before(step):
        return sum(s[0] == "heads" for s in m_order[:m_order.index(step)])

    def rows_before(step):
        return sum(s[0] == "rows" for s in m_order[:m_order.index(step)])

    with ExitStack() as whole:
        def sb(name, shape, dt, scope=whole):
            return scope.enter_context(nc.sbuf_tensor(name, shape, dt))

        def sem(name):
            return whole.enter_context(nc.semaphore(name))

        def signal(name, per, by=1):
            return Signal(sem(name), per, by)

        slots = nc.dram_tensor("slots", [E * CAP, ROW], F32, kind="Internal").ap()
        parts = nc.dram_tensor("parts", [2, 2, H * D, T], F32, kind="Internal").ap()

        psA = [whole.enter_context(nc.psum_tensor(f"psA{i}", [P, 512], F32)) for i in range(2)]
        psB = [whole.enter_context(nc.psum_tensor(f"psB{i}", [P, 2, 512], F32)) for i in range(2)]
        psO = whole.enter_context(nc.psum_tensor("psO", [P, 512], F32))
        psM = whole.enter_context(nc.psum_tensor("psM", [P, 512], F32))

        ident = sb("ident", [P, P], F32)
        b1T = sb("b1T", [P, E * KH], F32)
        tokens = whole.enter_context(ExitStack())

        def tk(name, shape, dt):
            return sb(name, shape, dt, tokens)

        wtok = tk("wtok", [P, XD, CH, C], F32)
        wqkv = tk("wqkv", [P, CH, 3 * C], F32)
        wproj = tk("wproj", [P, CH, C], F32)
        wr = tk("wr", [P, CH, E], F32)
        br_all = tk("br_all", [P, E], F32)
        bv_all = tk("bv_all", [P, C], F32)
        bp_all = tk("bp_all", [P, C], F32)
        bqk = tk("bqk", [P, 4], F32)
        qscale = tk("qscale", [P, 2], F32)
        bq_scaled = tk("bq_scaled", [P, 2], F32)
        before = tk("before", [P, P], BF16)
        ones = tk("ones", [P, P], BF16)
        ident16 = tk("ident16", [P, P], BF16)
        rel = tk("rel", [P, 2 * T - P], F32)
        rel_block = tk("rel_block", [P, P], BF16)
        numbers = tk("numbers", [P, E], F32)
        token_id = tk("token_id", [P, NT], F32)
        power = tk("power", [P, 1], F32)
        run = tk("run", [P, E], BF16)
        k_stack = tk("k_stack", [P, NG, GH, T], F32R)
        q_stack = tk("q_stack", [P, NG, GH, T], F32R)
        v_aug = tk("v_aug", [P, NT, H, 2 * D], F32)

        VEC, POOL = 2 * NT + NG + 14, 2 * NT + 4 + NG
        a_full, a_done = signal("a_full", A_USES), signal("a_done", A_USES)
        b_full, b_done = signal("b_full", B_USES), signal("b_done", B_USES)
        vec, pool_step = signal("vec", VEC), signal("pool_step", POOL)
        idle = sem("idle")
        x_loaded = [signal(f"x_loaded{i}", NT // 2, 16) for i in range(2)]
        moments_ready = signal("moments_ready", 2 * NT)
        rstd_ready = signal("rstd_ready", 2 * NT)
        ln_ready = signal("ln_ready", NT)
        split_ready = signal("split_ready", 4)
        parts_stored = [signal(f"parts_stored{j}", 1, 32) for j in range(4)]
        stack_loaded = [signal(f"stack_loaded{g}", 1, 16 * 8) for g in range(NG)]
        hb_ready = signal("hb_ready", 1)
        m_full = signal("m_full", 2 * NG)
        rows_out = signal("rows_out", NG)
        m_split = signal("m_split", NG)
        m_loaded = signal("m_loaded", NG, 16 * GH)
        values_done = signal("values_done", 2 * NG)
        heads_out = signal("heads_out", NG)
        y_ready = signal("y_ready", NG)
        row_ready = signal("row_ready", NT)
        sel_ready = signal("sel_ready", 1)
        gap_ready, gap_done = signal("gap_ready", 1), signal("gap_done", 1)
        slot_ready = signal("slot_ready", 1)
        h_stored = signal("h_stored", NT, 16)
        scattered = sem("scattered")
        rows_free = signal("rows_free", 1)

        with ExitStack() as first:
            ws = sb("ws", [P, CH, C], F32, first)
            wd = sb("wd", [P, C, XD], F32, first)
            b1_rows = sb("b1_rows", [E * KH, P], F32, first)
            before32 = sb("before32", [P, P], F32, first)
            rel_block32 = sb("rel_block32", [P, P], F32, first)
            rows32 = sb("rows32", [8, 2, T], F32, first)
            empty = sb("empty", [P, NS, ROW], F32, first)
            empty_id = sb("empty_id", [P, NS], F32, first)
            setup_loaded = sem("setup_loaded")
            rows_placed = sem("rows_placed")
            empty_ready = sem("empty_ready")
            slots_cleared = sem("slots_cleared")
            first_full = sem("first_full")
            first_step = sem("first_step")

            loads = [
                (ws[:, :, :], tok_sum.rearrange("(h p) i -> p h i", p=P)),
                (wd[:, :, :], tok_weight.partition_broadcast(P)),
                (ident[:, :], identity),
                (b1_rows[:, :], b1.rearrange("e (k p) -> (e k) p", p=P)),
                (before32[:, :], earlier),
                (rel_block32[:, :], relative_block),
                (rel[:, :], relative),
                (rows32[:, :, :], stack_rows),
                (empty_id[:, :], empty_numbers),
                (wqkv[:, :, :], w_qkv.rearrange("(h p) n -> p h n", p=P)),
                (wproj[:, :, :], w_proj.rearrange("(h p) n -> p h n", p=P)),
                (wr[:, :, :], w_router.rearrange("(h p) n -> p h n", p=P)),
                (bv_all[:, :], b_qkv[2 * C:3 * C].partition_broadcast(P)),
                (bp_all[:, :], b_proj.partition_broadcast(P)),
                (br_all[:, :], b_router.partition_broadcast(P)),
                (bqk[:, :], b_qkv[0:2 * C].rearrange("(j p) -> p j", p=P)),
                (qscale[:, :], q_scale),
                (numbers[:, :], expert_numbers.partition_broadcast(P)),
                (token_id[:, :], token_numbers),
            ]
            n_loads = 16 * len(loads)

            with nc.Block() as block:
                @block.sync
                def _(sp):
                    with nc.allow_non_contiguous_dma("biases by partition"):
                        for dst, src in loads:
                            sp.dma_start(dst, src).then_inc(setup_loaded, 16)
                    for s in [*x_loaded, *parts_stored, *stack_loaded, m_loaded, h_stored]:
                        sp.sem_inc(s.sem, s.credit)
                    sp.wait_ge(setup_loaded, n_loads)
                    for g in range(NG):
                        for h in range(GH):
                            for half, stack in ((0, q_stack), (1, k_stack)):
                                sp.dma_start(stack[SPLIT:STACK, g, h, :].bitcast(F32),
                                             rows32[:, half, :]).then_inc(rows_placed, 16)
                    sp.wait_ge(rows_placed, 16 * 2 * H)

                @block.gpsimd
                def _(pool):
                    for s in (pool_step, rstd_ready, split_ready, hb_ready, m_split, rows_free):
                        pool.sem_inc(s.sem, s.credit)
                    pool.wait_ge(empty_ready, 2)
                    for e in range(E):
                        dst = slots[e * CAP:(e + 1) * CAP, :].rearrange("(s p) c -> p s c", p=P)
                        pool.dma_start(dst, empty[:, :, :]).then_inc(slots_cleared, 16)
                    for s in range(NS):
                        pool.dma_start(out_tiles[NB * NT + s], empty[:, s, 0:C]).then_inc(slots_cleared, 16)
                    pool.wait_ge(slots_cleared, 16 * (E + NS))

                @block.tensor
                def _(pe):
                    for s in (a_full, b_full, m_full, values_done):
                        pe.sem_inc(s.sem, s.credit)
                    pe.wait_ge(setup_loaded, n_loads)
                    for ih in range(CH):
                        for oh in range(CH):
                            at = ih * C + oh * P
                            last = pe.transpose(psA[0][:, at:at + P], ws[:, oh, ih * P:(ih + 1) * P], ident[:, :])
                    last.then_inc(first_full, 1)
                    pe.transpose(psA[1][:, 0:E * KH], b1_rows[:, :],
                                 ident[0:E * KH, 0:E * KH]).then_inc(first_full, 1)

                @block.vector
                def _(dve):
                    for s in (a_done, vec, moments_ready, ln_ready, y_ready, row_ready, sel_ready, gap_ready,
                              slot_ready):
                        dve.sem_inc(s.sem, s.credit)
                    dve.memset(empty[:, :, :], 0.0).then_inc(empty_ready, 1)
                    dve.memset(v_aug[:, :, :, :], 0.0).then_inc(first_step, 1)
                    dve.memset(ones[:, :], 1.0)
                    dve.memset(run[:, :], 0.0)
                    dve.memset(power[:, :], -0.5)
                    dve.wait_ge(first_step, 1)
                    dve.memset(v_aug[:, :, :, D:D + 1], 1.0)
                    dve.wait_ge(setup_loaded, n_loads)
                    dve.wait_ge(empty_ready, 1)
                    dve.tensor_copy(empty[:, :, :].bitcast(U32)[:, :, TOKEN], empty_id[:, :]).then_inc(empty_ready, 1)
                    dve.tensor_copy(before[:, :], before32[:, :])
                    dve.tensor_copy(ident16[:, :], ident[:, :])
                    dve.tensor_copy(rel_block[:, :], rel_block32[:, :])
                    dve.tensor_tensor(bq_scaled[:, :], bqk[:, 0:2], qscale[:, :], ALU.mult)
                    dve.wait_ge(first_full, 1)
                    turned = psA[0][:, :].rearrange("p (i o) -> p i o", i=CH)
                    for d in range(XD):
                        by = wd[:, :, d].unsqueeze(1).to_broadcast([P, CH, C])
                        dve.tensor_tensor(wtok[:, d, :, :], turned, by, ALU.mult)
                    dve.wait_ge(first_full, 2)
                    dve.tensor_copy(b1T[:, :], psA[1][:, 0:E * KH])

                @block.scalar
                def _(act):
                    for s in (b_done, rows_out, heads_out, gap_done):
                        act.sem_inc(s.sem, s.credit)

        x_tile = [tk(f"x_tile{i}", [P, C * XD], F32) for i in range(2)]
        xT = [tk(f"xT{i}", [P, XD * CH, P], F32) for i in range(2)]
        h = tk("h", [P, NT, C], F32)
        h_bias = tk("h_bias", [P, NT, C], F32)
        stats = tk("stats", [P, NT, 6], F32)
        moments = tk("moments", [P, NT, 2], F32)
        var_eps = tk("var_eps", [P, NT], F32)
        rstd = tk("rstd", [P, NT], F32)
        ln = tk("ln", [P, NT, C], F32)
        y = ln
        lnT = tk("lnT", [P, CH, T], F32)
        qk_raw = tk("qk_raw", [P, 2, T], F32)
        qk_high = tk("qk_high", [P, 4, T], F32R)
        qk_low = tk("qk_low", [P, 4, T], F32R)
        masked = [tk(f"masked{i}", [P, T], BF16) for i in range(2)]
        top_score = [tk(f"top_score{i}", [P, NT, GH], F32) for i in range(2)]
        m_raw = tk("m_raw", [GH, T], F32)
        m_rows = tk("m_rows", [GH, 2, T], F32R)
        probs = [tk(f"probs{i}", [P, GH, 2, T], F32) for i in range(2)]
        heads_t = tk("heads_t", [P, T], F32)
        denom = tk("denom", [P, NT, GH], F32)
        yT = lnT
        rows = tk("rows", [P, NT, ROW], F32)
        logits = tk("logits", [P, NT, E], F32)
        top8 = tk("top8", [P, NT, 8], F32)
        top_at = tk("top_at", [P, NT, 8], U32)
        top_expert = tk("top_expert", [P, NT, 8], F32)
        hot = [tk(f"hot{i}", [P, NT, E], F32) for i in range(2)]
        sel = tk("sel", [P, NT, E], BF16)
        sel_sum = tk("sel_sum", [P, E], F32)
        gap = tk("gap", [P, NT], F32)
        gap_exp = tk("gap_exp", [P, NT], F32)
        gap_sum = tk("gap_sum", [P, NT], F32)
        picked = [tk(f"picked{i}", [P, NT, E], F32) for i in range(2)]
        rank = tk("rank", [P, 2, NT], F32)
        dropped = tk("dropped", [P, 2, NT], F32)
        slot = tk("slot", [P, 2, NT], F32)
        slot_at = tk("slot_at", [P, 2, NT], U32)

        with nc.Block() as block:
            @block.sync
            def _(sp):
                with sp.Fori(0, NB) as b:
                    for t in range(NT):
                        use = B_EMBED + t - 2 if t >= 2 else B_EMBED + t - 2 + NT - B_USES
                        sp.wait_ge(b_full.sem, b_full.at(b, use))
                        sp.dma_start(x_tile[t % 2][:, :], x_tiles[b * NT + t]).then_inc(x_loaded[t % 2].sem, 16)
                    for j in range(4):
                        for g in range(2 * (j % 2), 2 * (j % 2) + 2):
                            sp.wait_ge(stack_loaded[g].sem, stack_loaded[g].at(b, -1))
                            sp.sem_inc(idle, 1)
                        sp.wait_ge(split_ready.sem, split_ready.at(b, j))
                        sp.sem_inc(idle, 1)
                        for part, src in enumerate((qk_high, qk_low)):
                            dst = parts[j // 2, part, (j % 2) * P:(j % 2 + 1) * P, :]
                            sp.dma_start(dst, src[:, j, :].bitcast(F32)).then_inc(parts_stored[j].sem, 16)
                    for g in range(NG):
                        for j in (g // 2, 2 + g // 2):
                            sp.wait_ge(parts_stored[j].sem, parts_stored[j].at(b, 0))
                            sp.sem_inc(idle, 1)
                        sp.wait_ge(b_full.sem, b_full.at(b, B_SCORE + 8 * g + 7 - B_USES))
                        for which, stack, order in ((0, q_stack, Q_PARTS), (1, k_stack, K_PARTS)):
                            for n, part in enumerate(order):
                                src = parts[which, part, g * GH * D:(g + 1) * GH * D, :]
                                sp.dma_start(stack[n * D:(n + 1) * D, g, :, :].bitcast(F32),
                                             src.rearrange("(h d) t -> d h t", d=D)
                                             ).then_inc(stack_loaded[g].sem, 16)
                    for g in range(NG):
                        sp.wait_ge(m_split.sem, m_split.at(b, g))
                        for hd in range(GH):
                            sp.dma_start(q_stack[MROW:MROW + 2, g, hd, :].bitcast(F32),
                                         m_rows[hd:hd + 1, :, :].bitcast(F32)).then_inc(m_loaded.sem, 16)
                    for t in range(NT):
                        sp.wait_ge(row_ready.sem, row_ready.at(b, t))
                        sp.dma_start(out_tiles[b * NT + t], h[:, t, :]).then_inc(h_stored.sem, 16)
                sp.wait_ge(h_stored.sem, h_stored.at(NB - 1, NT - 1))

            @block.tensor
            def _(pe):
                with pe.Fori(0, NB) as b:
                    def ring_a(use):
                        pe.wait_ge(a_done.sem, a_done.at(b, use - 2))
                        return psA[use % 2]

                    def ring_b(use):
                        pe.wait_ge(b_done.sem, b_done.at(b, use - 2))
                        return psB[use % 2]

                    def turn_x(t):
                        pe.wait_ge(x_loaded[t % 2].sem, x_loaded[t % 2].at(b, t // 2))
                        bank = ring_b(B_EMBED + t)
                        xv = x_tile[t % 2][:, :].rearrange("p (i d) -> p i d", d=XD)
                        for k in range(XD * CH):
                            d, ih = k // CH, k % CH
                            last = pe.transpose(bank[:, k // 4, (k % 4) * P:(k % 4 + 1) * P],
                                                xv[:, ih * P:(ih + 1) * P, d], ident[:, :])
                        last.then_inc(b_full.sem, 1)

                    turn_x(0)
                    for t in range(NT):
                        if t + 1 < NT:
                            turn_x(t + 1)
                        pe.wait_ge(b_done.sem, b_done.at(b, B_EMBED + t))
                        bank = ring_a(A_EMBED + t)
                        for k in range(XD * CH):
                            last = pe.matmul(bank[:, 0:C], xT[t % 2][:, k, :], wtok[:, k // CH, k % CH, :],
                                             start=(k == 0), stop=(k == XD * CH - 1))
                        last.then_inc(a_full.sem, 1)

                    for t in range(NT):
                        if t % 2 == 0:
                            bank = ring_b(B_NORM + t // 2)
                        pe.wait_ge(ln_ready.sem, ln_ready.at(b, t))
                        for c in range(CH):
                            last = pe.transpose(bank[:, c, (t % 2) * P:(t % 2 + 1) * P],
                                                ln[:, t, c * P:(c + 1) * P], ident[:, :])
                        if t % 2:
                            last.then_inc(b_full.sem, 1)
                    pe.wait_ge(b_done.sem, b_done.at(b, B_NORM + 1))

                    for j in range(4):
                        if j % 2 == 0:
                            bank = ring_b(B_QK + j // 2)
                        for c in range(CH):
                            last = pe.matmul(bank[:, j % 2, :], wqkv[:, c, j * P:(j + 1) * P], lnT[:, c, :],
                                             start=(c == 0), stop=(c == CH - 1))
                        if j % 2:
                            last.then_inc(b_full.sem, 1)
                    for t in range(NT):
                        bank = ring_a(A_VALUE + t)
                        for c in range(CH):
                            last = pe.matmul(bank[:, 0:C], lnT[:, c, t * P:(t + 1) * P], wqkv[:, c, 2 * C:3 * C],
                                             start=(c == 0), stop=(c == CH - 1))
                        last.then_inc(a_full.sem, 1)

                    def psM_free(step):
                        pe.wait_ge(rows_out.sem, rows_out.at(b, rows_before(step) - 1))
                        pe.wait_ge(y_ready.sem, y_ready.at(b, heads_before(step) - 1))

                    for what, n in steps:
                        if what == "max":
                            g, t, hd = n // 16, n % 16 // GH, n % GH
                            if n % 16 == 0:
                                pe.wait_ge(stack_loaded[g].sem, stack_loaded[g].at(b, 0))
                            bank = ring_a(A_MAX + n)
                            pe.matmul(bank[:, :], q_stack[0:SPLIT, g, hd, t * P:(t + 1) * P],
                                      k_stack[0:SPLIT, g, hd, :], start=True, stop=True).then_inc(a_full.sem, 1)
                        elif what == "rows":
                            pe.wait_ge(a_done.sem, a_done.at(b, A_MAX + 16 * n + 15))
                            psM_free((what, n))
                            for t in range(NT):
                                last = pe.transpose(psM[0:GH, t * P:(t + 1) * P], top_score[n % 2][:, t, :],
                                                    ident[:, :])
                            last.then_inc(m_full.sem, 1)
                        elif what == "scores":
                            g, half, hd = n // 8, n % 8 // GH, n % GH
                            if n % 8 == 0:
                                pe.wait_ge(m_loaded.sem, m_loaded.at(b, g))
                            bank = ring_b(B_SCORE + n)
                            for i in range(2):
                                s = 2 * half + i
                                pe.matmul(bank[:, i, s * P:(s + 1) * P], ident16[:, :], rel_block[:, :],
                                          start=True, stop=True)
                                last = pe.matmul(bank[:, i, :], k_stack[0:STACK, g, hd, s * P:(s + 1) * P],
                                                 q_stack[0:STACK, g, hd, :], start=False, stop=True,
                                                 skip_group_check=True)
                            last.then_inc(b_full.sem, 1)
                        elif what == "values":
                            g, half = n // 2, n % 2
                            pe.wait_ge(b_done.sem, b_done.at(b, B_SCORE + 4 * n + 3))
                            if n == 0:
                                pe.wait_ge(a_done.sem, a_done.at(b, A_VALUE + NT - 1))
                            if half == 0:
                                pe.wait_ge(heads_out.sem, heads_out.at(b, g - 1))
                            for i in range(2):
                                s = 2 * half + i
                                for hd in range(GH):
                                    last = pe.matmul(psO[32 * hd:32 * hd + 32, :], v_aug[:, s, g * GH + hd, :],
                                                     probs[n % 2][:, hd, i, :], start=(s == 0), stop=(s == NT - 1),
                                                     tile_position=(0, 32 * hd))
                            last.then_inc(values_done.sem, 1)
                        elif what == "heads":
                            pe.wait_ge(heads_out.sem, heads_out.at(b, n))
                            psM_free((what, n))
                            for t in range(NT):
                                last = pe.transpose(psM[:, t * P:(t + 1) * P], heads_t[:, t * P:(t + 1) * P],
                                                    ident[:, :])
                            last.then_inc(m_full.sem, 1)

                    bank = ring_b(B_HEADS)
                    pe.wait_ge(y_ready.sem, y_ready.at(b, NG - 1))
                    for t in range(NT):
                        for c in range(CH):
                            last = pe.transpose(bank[:, c, t * P:(t + 1) * P], y[:, t, c * P:(c + 1) * P],
                                                ident[:, :])
                    last.then_inc(b_full.sem, 1)
                    pe.wait_ge(b_done.sem, b_done.at(b, B_HEADS))
                    for t in range(NT):
                        bank = ring_a(A_PROJ + t)
                        for c in range(CH):
                            last = pe.matmul(bank[:, 0:C], yT[:, c, t * P:(t + 1) * P], wproj[:, c, :],
                                             start=(c == 0), stop=(c == CH - 1))
                        last.then_inc(a_full.sem, 1)

                    bank = ring_b(B_NORM2)
                    for t in range(NT):
                        pe.wait_ge(row_ready.sem, row_ready.at(b, t))
                        for c in range(CH):
                            last = pe.transpose(bank[:, c, t * P:(t + 1) * P], rows[:, t, c * P:(c + 1) * P],
                                                ident[:, :])
                    last.then_inc(b_full.sem, 1)
                    pe.wait_ge(b_done.sem, b_done.at(b, B_NORM2))
                    bank = ring_a(A_ROUTE)
                    for t in range(NT):
                        for c in range(CH):
                            last = pe.matmul(bank[:, t * E:(t + 1) * E], lnT[:, c, t * P:(t + 1) * P], wr[:, c, :],
                                             start=(c == 0), stop=(c == CH - 1))
                    last.then_inc(a_full.sem, 1)
                    bank = ring_a(A_RANK)
                    pe.wait_ge(sel_ready.sem, sel_ready.at(b, 0))
                    for t in range(NT):
                        o = bank[:, t * E:(t + 1) * E]
                        pe.matmul(o, before[:, :], sel[:, t, :], start=True, stop=False)
                        for t0 in range(t):
                            pe.matmul(o, ones[:, :], sel[:, t0, :], start=False, stop=False)
                        last = pe.matmul(o, ones[:, :], run[:, :], start=False, stop=True)
                    last.then_inc(a_full.sem, 1)

            @block.scalar
            def _(act):
                with act.Fori(0, NB) as b:
                    def ring_b(use):
                        act.wait_ge(b_full.sem, b_full.at(b, use))
                        return psB[use % 2]

                    for t in range(NT):
                        bank = ring_b(B_EMBED + t)
                        use = A_EMBED + t - 2 if t >= 2 else A_EMBED + t - 2 + NT - A_USES
                        act.wait_ge(a_full.sem, a_full.at(b, use))
                        act.activation(xT[t % 2][:, :, :].rearrange("p k n -> p (k n)"),
                                       bank[:, :, :].rearrange("p a n -> p (a n)"), ACT.Copy).then_inc(b_done.sem, 1)
                    for i in range(NT // 2):
                        bank = ring_b(B_NORM + i)
                        act.activation(lnT[:, :, 2 * i * P:2 * (i + 1) * P], bank[:, :, 0:2 * P],
                                       ACT.Copy).then_inc(b_done.sem, 1)
                    for i in range(2):
                        bank = ring_b(B_QK + i)
                        act.wait_ge(split_ready.sem, split_ready.at(b, 2 * i - 1))
                        for j in range(2):
                            scale = qscale[:, j:j + 1] if i == 0 else 1.0
                            bias = bq_scaled[:, j:j + 1] if i == 0 else bqk[:, 2 + j:3 + j]
                            last = act.activation(qk_raw[:, j, :], bank[:, j, :], ACT.Identity, bias=bias, scale=scale)
                        last.then_inc(b_done.sem, 1)
                    for what, n in steps:
                        if what == "rows":
                            act.wait_ge(m_full.sem, m_full.at(b, m_order.index((what, n))))
                            act.wait_ge(m_split.sem, m_split.at(b, n - 1))
                            act.activation(m_raw[:, :], psM[0:GH, :], ACT.Copy).then_inc(rows_out.sem, 1)
                        elif what == "scores":
                            g, half, hd = n // 8, n % 8 // GH, n % GH
                            bank = ring_b(B_SCORE + n)
                            if hd == 0:
                                act.wait_ge(values_done.sem, values_done.at(b, n // GH - 2))
                            act.activation(probs[n // GH % 2][:, hd, :, :], bank[:, :, :], ACT.Exp,
                                           scale=slope[g * GH + hd]).then_inc(b_done.sem, 1)
                        elif what == "heads":
                            act.wait_ge(values_done.sem, values_done.at(b, 2 * n + 1))
                            use = m_order.index((what, n - 1)) if n else 2 * NG - 1 - 2 * NG
                            act.wait_ge(m_full.sem, m_full.at(b, use))
                            act.activation(heads_t[:, :], psO[:, :], ACT.Copy).then_inc(heads_out.sem, 1)
                    for use, dst in ((B_HEADS, yT), (B_NORM2, lnT)):
                        bank = ring_b(use)
                        act.activation(dst[:, :, :], bank[:, :, :], ACT.Copy).then_inc(b_done.sem, 1)
                    act.wait_ge(gap_ready.sem, gap_ready.at(b, 0))
                    act.activation(gap_exp[:, :], gap[:, :], ACT.Exp).then_inc(gap_done.sem, 1)

            @block.vector
            def _(dve):
                with dve.Fori(0, NB) as b:
                    own = [0]

                    def ring_a(use):
                        dve.wait_ge(a_full.sem, a_full.at(b, use))
                        return psA[use % 2]

                    def settle(instruction):
                        instruction.then_inc(vec.sem, 1)
                        dve.wait_ge(vec.sem, vec.at(b, own[0]))
                        own[0] += 1

                    def normalise(t, dst, done, turn):
                        settle(dve.bn_stats(stats[:, t, :], h[:, t, :]))
                        dve.sem_inc(idle, 1)
                        dve.bn_aggr(moments[:, t, :], stats[:, t, :]).then_inc(moments_ready.sem, 1)
                        dve.wait_ge(rstd_ready.sem, rstd_ready.at(b, turn))
                        dve.tensor_scalar(dst, h[:, t, :], moments[:, t, 0:1], rstd[:, t:t + 1],
                                          ALU.subtract, ALU.mult).then_inc(done.sem, 1)

                    dve.wait_ge(h_stored.sem, h_stored.at(b, -1))
                    for t in range(NT):
                        bank = ring_a(A_EMBED + t)
                        dve.tensor_copy(h[:, t, :], bank[:, 0:C]).then_inc(a_done.sem, 1)
                        dve.wait_ge(a_done.sem, a_done.at(b, A_EMBED + t))
                        normalise(t, ln[:, t, :], ln_ready, t)
                    for t in range(NT):
                        bank = ring_a(A_VALUE + t)
                        dve.tensor_tensor(v_aug[:, t, :, 0:D], bank[:, 0:C].rearrange("p (h d) -> p h d", d=D),
                                          bv_all[:, :].rearrange("p (h d) -> p h d", d=D),
                                          ALU.add).then_inc(a_done.sem, 1)
                    for what, n in steps:
                        if what == "max":
                            g, t, hd = n // 16, n % 16 // GH, n % GH
                            bank = ring_a(A_MAX + n)
                            if n % 16 == 0:
                                use = m_order.index(("rows", g - 2)) if g >= 2 else m_order.index(("rows", g + 2)) - 2 * NG
                                dve.wait_ge(m_full.sem, m_full.at(b, use))
                            first = T - P - t * P
                            dve.sem_inc(idle, 1)
                            dve.tensor_tensor_reduce(masked[n % 2][:, :], bank[:, :], rel[:, first:first + T], 1.0, LOWEST,
                                                     ALU.add, ALU.max,
                                                     top_score[g % 2][:, t, hd:hd + 1]).then_inc(a_done.sem, 1)
                        elif what == "heads":
                            dve.wait_ge(m_full.sem, m_full.at(b, m_order.index((what, n))))
                            o = psM[:, :].rearrange("p (t h d) -> p t h d", t=NT, h=GH)
                            settle(dve.reciprocal(denom[:, :, :], o[:, :, :, D]))
                            dve.tensor_tensor(
                                y[:, :, n * GH * D:(n + 1) * GH * D].rearrange("p t (h d) -> p t h d", d=D),
                                o[:, :, :, 0:D], denom[:, :, :].unsqueeze(3).to_broadcast([P, NT, GH, D]),
                                ALU.mult).then_inc(y_ready.sem, 1)
                    dve.wait_ge(hb_ready.sem, hb_ready.at(b, 0))
                    dve.wait_ge(rows_free.sem, rows_free.at(b, -1))
                    for t in range(NT):
                        bank = ring_a(A_PROJ + t)
                        dve.tensor_tensor(h[:, t, :], bank[:, 0:C], h_bias[:, t, :], ALU.add).then_inc(a_done.sem, 1)
                        dve.wait_ge(a_done.sem, a_done.at(b, A_PROJ + t))
                        normalise(t, rows[:, t, 0:C], row_ready, NT + t)

                    bank = ring_a(A_ROUTE)
                    dve.tensor_tensor(logits[:, :, :], bank[:, 0:NT * E].rearrange("p (t e) -> p t e", e=E),
                                      br_all[:, :].unsqueeze(1).to_broadcast([P, NT, E]), ALU.add).then_inc(a_done.sem, 1)
                    dve.wait_ge(a_done.sem, a_done.at(b, A_ROUTE))
                    dve.sem_inc(idle, 1)
                    for t in range(NT):
                        last = dve.max(top8[:, t, :], logits[:, t, :])
                    settle(last)
                    dve.sem_inc(idle, 1)
                    for t in range(NT):
                        last = dve.max_index(top_at[:, t, :], top8[:, t, :], logits[:, t, :])
                    settle(last)
                    settle(dve.tensor_copy(top_expert[:, :, :], top_at[:, :, :]))
                    for i in range(2):
                        last = dve.tensor_tensor(hot[i][:, :, :], numbers[:, :].unsqueeze(1).to_broadcast([P, NT, E]),
                                                 top_expert[:, :, i:i + 1].to_broadcast([P, NT, E]), ALU.is_equal)
                    settle(last)
                    dve.tensor_tensor(sel[:, :, :], hot[0][:, :, :], hot[1][:, :, :], ALU.add).then_inc(sel_ready.sem, 1)
                    dve.tensor_tensor(gap[:, :], top8[:, :, 1], top8[:, :, 0], ALU.subtract).then_inc(gap_ready.sem, 1)
                    dve.tensor_copy(rows[:, :, FIRST], top_expert[:, :, 0])
                    settle(dve.tensor_copy(rows[:, :, :].bitcast(U32)[:, :, TOKEN], token_id[:, :]))
                    dve.tensor_scalar(token_id[:, :], token_id[:, :], float(T), None, ALU.add)
                    dve.wait_ge(gap_done.sem, gap_done.at(b, 0))
                    settle(dve.tensor_scalar(gap_sum[:, :], gap_exp[:, :], 1.0, None, ALU.add))
                    settle(dve.reciprocal(rows[:, :, GATE1], gap_sum[:, :]))
                    dve.tensor_tensor(rows[:, :, GATE2], rows[:, :, GATE1], gap_exp[:, :], ALU.mult)
                    bank = ring_a(A_RANK)
                    ranks = bank[:, 0:NT * E].rearrange("p (t e) -> p t e", e=E)
                    dve.tensor_tensor(picked[0][:, :, :], ranks, hot[0][:, :, :], ALU.mult)
                    dve.tensor_tensor(picked[1][:, :, :], ranks, hot[1][:, :, :], ALU.mult).then_inc(a_done.sem, 1)
                    dve.wait_ge(a_done.sem, a_done.at(b, A_RANK))
                    for i in range(2):
                        last = dve.tensor_reduce(rank[:, i, :], picked[i][:, :, :], AX.X, ALU.add)
                    settle(last)
                    dve.tensor_scalar(dropped[:, :, :], rank[:, :, :], float(CAP), float(2 * E * CAP),
                                      ALU.is_ge, ALU.mult)
                    settle(dve.scalar_tensor_tensor(
                        out=slot[:, :, :], in0=top_expert[:, :, 0:2].rearrange("p t i -> p i t"), scalar=float(CAP),
                        in1=rank[:, :, :], op0=ALU.mult, op1=ALU.add))
                    dve.tensor_tensor(slot_at[:, :, :], slot[:, :, :], dropped[:, :, :], ALU.add).then_inc(slot_ready.sem, 1)
                    settle(dve.tensor_reduce(sel_sum[:, :], sel[:, :, :].rearrange("p t e -> p e t"), AX.X, ALU.add))
                    settle(dve.tensor_tensor(run[:, :], run[:, :], sel_sum[:, :], ALU.add))
                    assert own[0] <= VEC, own[0]
                    dve.sem_inc(vec.sem, VEC - own[0])

            @block.gpsimd
            def _(pool):
                with pool.Fori(0, NB) as b:
                    own = [0]

                    def settle(instruction):
                        instruction.then_inc(pool_step.sem, 1)
                        pool.wait_ge(pool_step.sem, pool_step.at(b, own[0]))
                        own[0] += 1

                    def deviation(t, turn):
                        pool.wait_ge(moments_ready.sem, moments_ready.at(b, turn))
                        pool.sem_inc(idle, 1)
                        settle(pool.tensor_scalar(var_eps[:, t:t + 1], moments[:, t, 1:2], EPS, None, ALU.add))
                        pool.tensor_tensor(rstd[:, t:t + 1], var_eps[:, t:t + 1], power[:, :],
                                           ALU.pow).then_inc(rstd_ready.sem, 1)

                    for t in range(NT):
                        deviation(t, t)
                    pool.wait_ge(a_done.sem, a_done.at(b, A_EMBED + NT - 1))
                    pool.tensor_tensor(h_bias[:, :, :], h[:, :, :], bp_all[:, :].unsqueeze(1).to_broadcast([P, NT, C]),
                                       ALU.add).then_inc(hb_ready.sem, 1)
                    for j in range(4):
                        pool.wait_ge(b_done.sem, b_done.at(b, B_QK + j // 2))
                        pool.wait_ge(parts_stored[j].sem, parts_stored[j].at(b, -1))
                        pool.sem_inc(idle, 1)
                        settle(pool.tensor_copy(qk_high[:, j, :], qk_raw[:, j % 2, :]))
                        pool.tensor_tensor(qk_low[:, j, :], qk_raw[:, j % 2, :], qk_high[:, j, :],
                                           ALU.subtract).then_inc(split_ready.sem, 1)
                    for g in range(NG):
                        pool.wait_ge(rows_out.sem, rows_out.at(b, g))
                        pool.wait_ge(m_loaded.sem, m_loaded.at(b, g - 1))
                        pool.sem_inc(idle, 1)
                        settle(pool.tensor_copy(m_rows[:, 0, :], m_raw[:, :]))
                        pool.tensor_tensor(m_rows[:, 1, :], m_raw[:, :], m_rows[:, 0, :],
                                           ALU.subtract).then_inc(m_split.sem, 1)
                    for t in range(NT):
                        deviation(t, NT + t)
                    pool.wait_ge(slot_ready.sem, slot_ready.at(b, 0))
                    pool.sem_inc(idle, 1)
                    for i in range(2):
                        for t in range(NT):
                            pool.indirect_dma_start(
                                out=slots[:, :], out_offset=bass.IndirectOffsetOnAxis(ap=slot_at[:, i, t:t + 1], axis=0),
                                in_=rows[:, t, :], in_offset=None, bounds_check=E * CAP - 1,
                                oob_is_err=False).then_inc(scattered, 16)
                    pool.wait_ge(scattered, b * (2 * NT * 16) + 2 * NT * 16)
                    pool.sem_inc(rows_free.sem, 1)
                    assert own[0] == POOL, own[0]
        tokens.close()

        w1_t = [sb(f"w1_t{i}", [P, CH, HID], F32) for i in range(2)]
        w2_t = [sb(f"w2_t{i}", [P, KH, C], F32) for i in range(2)]
        b2_t = [sb(f"b2_t{i}", [P, C], F32) for i in range(2)]
        taken = [sb(f"taken{i}", [P, NS, ROW], F32) for i in range(2)]
        takenT = [sb(f"takenT{i}", [P, CH, CAP], F32) for i in range(2)]
        hidden = [sb(f"hidden{i}", [P, KH, CAP], F32) for i in range(2)]
        given = [sb(f"given{i}", [P, NS, C], F32) for i in range(2)]
        number = sb("number", [P, 1], F32)
        gate_parts = [sb(f"gate_parts{i}", [P, NS], F32) for i in range(2)]
        gate = sb("gate", [P, NS], F32)
        NP = E // 2
        number_ready = sem("number_ready")

        w_loaded = [signal(f"w_loaded{i}", 1, 48) for i in range(2)]
        taken_loaded = [signal(f"taken_loaded{i}", 1, 16) for i in range(2)]
        ea_full, ea_done = signal("ea_full", EA_USES), signal("ea_done", EA_USES)
        eb_full, eb_done = signal("eb_full", EB_USES), signal("eb_done", EB_USES)
        e_step = signal("e_step", 4 + 2 * NS)
        given_ready = signal("given_ready", EA_USES)
        added = sem("added")
        given_free = signal("given_free", 2)
        B_E = EB_USES // 2

        with nc.Block() as block:
            @block.sync
            def _(sp):
                for s in (*w_loaded, *taken_loaded):
                    sp.sem_inc(s.sem, s.credit)
                with sp.Fori(0, NP) as pair:
                    for i in range(2):
                        sp.wait_ge(ea_full.sem, ea_full.at(pair, NS * i + NS - 1 - EA_USES))
                        sp.dma_start(w1_t[i][:, :, :], w1.rearrange("e (c p) n -> e p c n", p=P)[pair * 2 + i]
                                     ).then_inc(w_loaded[i].sem, 16)
                        sp.dma_start(w2_t[i][:, :, :], w2.rearrange("e (k p) n -> e p k n", p=P)[pair * 2 + i]
                                     ).then_inc(w_loaded[i].sem, 16)
                        sp.wait_ge(ea_done.sem, ea_done.at(pair, NS * i + NS - 1 - EA_USES))
                        sp.dma_start(b2_t[i][:, :], b2.rearrange("(e o) n -> e o n", o=1)[pair * 2 + i].to_broadcast([P, C])
                                     ).then_inc(w_loaded[i].sem, 16)
                        sp.wait_ge(given_free.sem, given_free.at(pair, i - 2))
                        sp.dma_start(taken[i][:, :, :], slots.rearrange("(e s p) c -> e p s c", p=P, s=NS)[pair * 2 + i]
                                     ).then_inc(taken_loaded[i].sem, 16)

            @block.tensor
            def _(pe):
                for s in (ea_full, eb_full):
                    pe.sem_inc(s.sem, s.credit)
                with pe.Fori(0, NP) as pair:
                    for i in range(2):
                        pe.wait_ge(taken_loaded[i].sem, taken_loaded[i].at(pair, 0))
                        pe.wait_ge(eb_done.sem, eb_done.at(pair, B_E * i - 2))
                        bank = psB[B_E * i % 2]
                        for s in range(NS):
                            for c in range(CH):
                                last = pe.transpose(bank[:, c, s * P:(s + 1) * P], taken[i][:, s, c * P:(c + 1) * P],
                                                    ident[:, :])
                        last.then_inc(eb_full.sem, 1)
                        pe.wait_ge(w_loaded[i].sem, w_loaded[i].at(pair, 0))
                        pe.wait_ge(eb_done.sem, eb_done.at(pair, B_E * i))
                        for k in range(KH):
                            use = B_E * i + 1 + k // 2
                            if k % 2 == 0:
                                pe.wait_ge(eb_done.sem, eb_done.at(pair, use - 2))
                            for c in range(CH):
                                last = pe.matmul(psB[use % 2][:, k % 2, :], w1_t[i][:, c, k * P:(k + 1) * P],
                                                 takenT[i][:, c, :], start=(c == 0), stop=(c == CH - 1))
                            if k % 2:
                                last.then_inc(eb_full.sem, 1)
                        for s in range(NS):
                            use = NS * i + s
                            pe.wait_ge(ea_done.sem, ea_done.at(pair, use - 2))
                            for k in range(KH):
                                if s == 0 and k % 2 == 0:
                                    pe.wait_ge(eb_done.sem, eb_done.at(pair, B_E * i + 1 + k // 2))
                                last = pe.matmul(psA[use % 2][:, 0:C], hidden[i][:, k, s * P:(s + 1) * P],
                                                 w2_t[i][:, k, :], start=(k == 0), stop=(k == KH - 1))
                            last.then_inc(ea_full.sem, 1)

            @block.scalar
            def _(act):
                act.sem_inc(eb_done.sem, eb_done.credit)
                with act.Fori(0, NP) as pair:
                    for i in range(2):
                        act.wait_ge(eb_full.sem, eb_full.at(pair, B_E * i))
                        act.activation(takenT[i][:, :, :], psB[B_E * i % 2][:, :, :], ACT.Copy).then_inc(eb_done.sem, 1)
                        act.wait_ge(ea_full.sem, ea_full.at(pair, NS * i + NS - 1 - EA_USES))
                        for k in range(KH):
                            use = B_E * i + 1 + k // 2
                            if k % 2 == 0:
                                act.wait_ge(eb_full.sem, eb_full.at(pair, use))
                            last = act.activation(hidden[i][:, k, :], psB[use % 2][:, k % 2, :], ACT.Gelu,
                                                  bias=b1T[:, bass.ds(pair * (2 * KH) + (i * KH + k), 1)])
                            if k % 2:
                                last.then_inc(eb_done.sem, 1)

            @block.vector
            def _(dve):
                for s in (ea_done, e_step, given_ready):
                    dve.sem_inc(s.sem, s.credit)
                dve.memset(number[:, :], 0.0).then_inc(number_ready, 1)
                dve.wait_ge(number_ready, 1)
                with dve.Fori(0, NP) as pair:
                    own = [0]

                    def settle(instruction):
                        instruction.then_inc(e_step.sem, 1)
                        dve.wait_ge(e_step.sem, e_step.at(pair, own[0]))
                        own[0] += 1

                    for i in range(2):
                        dve.wait_ge(taken_loaded[i].sem, taken_loaded[i].at(pair, 0))
                        for n, (column, test) in enumerate(((GATE1, ALU.is_equal), (GATE2, ALU.not_equal))):
                            last = dve.scalar_tensor_tensor(out=gate_parts[n][:, :], in0=taken[i][:, :, FIRST],
                                                            scalar=number[:, 0:1], in1=taken[i][:, :, column],
                                                            op0=test, op1=ALU.mult)
                        settle(last)
                        dve.tensor_scalar(number[:, :], number[:, :], 1.0, None, ALU.add)
                        settle(dve.tensor_tensor(gate[:, :], gate_parts[0][:, :], gate_parts[1][:, :], ALU.add))
                        dve.wait_ge(w_loaded[i].sem, w_loaded[i].at(pair, 0))
                        dve.wait_ge(given_free.sem, given_free.at(pair, i - 2))
                        for s in range(NS):
                            use = NS * i + s
                            dve.wait_ge(ea_full.sem, ea_full.at(pair, use))
                            dve.tensor_tensor(given[i][:, s, :], psA[use % 2][:, 0:C], b2_t[i][:, :],
                                              ALU.add).then_inc(ea_done.sem, 1)
                            dve.wait_ge(ea_done.sem, ea_done.at(pair, use))
                            dve.tensor_scalar(given[i][:, s, :], given[i][:, s, :], gate[:, s:s + 1], None,
                                              ALU.mult).then_inc(given_ready.sem, 1)
                    dve.sem_inc(e_step.sem, e_step.per - own[0])

            @block.gpsimd
            def _(pool):
                pool.sem_inc(given_free.sem, given_free.credit)
                with pool.Fori(0, NP) as pair:
                    for i in range(2):
                        for s in range(NS):
                            use = NS * i + s
                            pool.wait_ge(given_ready.sem, given_ready.at(pair, use))
                            pool.sem_inc(idle, 1)
                            pool.sem_inc(idle, 1)
                            pool.indirect_dma_start(
                                out=out[:, :],
                                out_offset=bass.IndirectOffsetOnAxis(ap=taken[i][:, s, TOKEN:TOKEN + 1].bitcast(U32), axis=0),
                                in_=given[i][:, s, :], in_offset=None, bounds_check=N + CAP - 1, oob_is_err=True,
                                compute_op=ALU.add).then_inc(added, 16)
                        pool.wait_ge(added, pair * (2 * NS * 16) + (i + 1) * NS * 16)
                        pool.sem_inc(given_free.sem, 1)


_INS = ["x", "L0_tok_weight", "L0_tok_weighted_sum", "L0_attn_W_qkv", "L0_attn_b_qkv", "L0_attn_W_proj",
        "L0_attn_b_proj", "L0_ffn_Wr", "L0_ffn_br", "L0_ffn_W1", "L0_ffn_b1", "L0_ffn_W2", "L0_ffn_b2"]


def constants():
    import numpy as np

    f = np.float32
    p, t = np.arange(P)[:, None], np.arange(T)
    later = [(t >= P * (s + 1)) for s in range(NT - 1)]
    inside = [(t // P == s) for s in range(NT - 1)]
    q_rows = [0 * t, 0 * t] + [w * (P * (s + 1) - t) for s, w in enumerate(later)] + [w * 1 for w in later]
    k_rows = [0 * t - 1, 0 * t - 1] + [w * 1 for w in inside] + [w * (t - P * (s + 1)) for s, w in enumerate(inside)]
    heads = 8 * np.arange(2)[None, :] + p // D
    return {
        "identity": np.eye(P, dtype=f),
        "earlier": (p < np.arange(P)[None, :]).astype(f),
        "relative": np.minimum(np.arange(2 * T - P)[None, :] - (T - P) - p, 0).astype(f),
        "relative_block": np.minimum(p - np.arange(P)[None, :], 0).astype(f),
        "stack_rows": np.stack([np.array(q_rows), np.array(k_rows)], 1).astype(f),
        "q_scale": (D**-0.5 / np.array(slopes(), f)[heads]).astype(f),
        "expert_numbers": np.arange(E, dtype=f),
        "token_numbers": (p + P * np.arange(NT)[None, :]).astype(f),
        "empty_numbers": (N + p + P * np.arange(NS)[None, :]).astype(f),
    }


def kernel(**inputs):
    import concourse.bacc as _bacc
    import numpy as _np
    from concourse.bass_utils import run_bass_kernel_spmd as _run

    nc = _bacc.Bacc("TRN2", target_bir_lowering=False, num_devices=1)
    arrays, args = {}, []
    for name, a in [*((k, inputs[k]) for k in _INS), *constants().items()]:
        a = _np.ascontiguousarray(a)
        arrays[f"in_{name}_dram"] = a
        args.append(nc.dram_tensor(f"in_{name}_dram", a.shape, mybir.dt.from_np(a.dtype), kind="ExternalInput").ap())
    args.append(nc.dram_tensor("out_0_dram", (N + CAP, C), F32, kind="ExternalOutput").ap())
    tower(nc, *args)
    r = _run(nc, [arrays], core_ids=[0])
    return _np.asarray(r.results[0]["out_0_dram"])[:N].reshape(NB, T, C)
```

```python
import math
from contextlib import ExitStack

import concourse.bass as bass
from concourse import mybir

F32 = mybir.dt.float32
F32R = mybir.dt.float32r
BF16 = mybir.dt.bfloat16
U32 = mybir.dt.uint32
ALU = mybir.AluOpType
ACT = mybir.ActivationFunctionType
AX = mybir.AxisListType

P = 128
NB, T, C = 4, 512, 256
XD = 4
NT = T // P
CH = C // P
H, D = 16, 16
NG, GH = 4, 4
N = NB * T
E, CAP, HID = 8, 512, 1024
KH = HID // P
NS = CAP // P
ROW = C + 4
TOKEN, FIRST, GATE1, GATE2 = C, C + 1, C + 2, C + 3
EPS = 1e-5
LOWEST = -3.0e38

SPLIT = 4 * D
ALIBI = 2 * (NT - 1)
MROW = P - 2
Q_PARTS, K_PARTS = (0, 1, 0, 1), (0, 0, 1, 1)
NA = NG * NT * GH
NU = NG * 2 * GH
LEAD = 26
MIDDLE = 16
CLEARS = E + NS


def slopes():
    start = 2.0 ** (-(2.0 ** -(math.log2(H) - 3)))
    return [start * start**i for i in range(H)]


class Signal:

    def __init__(self, semaphore, per, by=1):
        self.sem, self.per, self.by = semaphore, per, by
        self.credit = per * by

    def at(self, batch, event):
        assert -self.per <= event < self.per
        return batch * self.credit + (self.credit + self.by * (event + 1))


def embedding_steps(first, last):
    order = ["turn_x 0 new", "turn_ln 1 old", "turn_x 1 new", "embed 0 new", "qk 0 old", "turn_x 2 new",
             "embed 1 new", "norm 0 new", "qk 1 old", "store 0 old", "turn_x 3 new", "qk 2 old", "store 1 old",
             "embed 2 new", "norm 1 new", "qk 3 old", "store 2 old", "value 0 old", "norm 2 new", "embed 3 new",
             "store 3 old", "value 1 old", "turn_ln 0 new", "norm 3 new"]
    steps = []
    for step in order:
        what, n, batch = step.split()
        if not (first if batch == "old" else last):
            steps.append((what, int(n), int(batch == "new")))
        if last and what in ("qk", "value"):
            steps += [("max", len([s for s in steps if s[0] == "max"]) + i, 0) for i in range(3 if what == "qk" else 2)]
    return steps


def attention_steps(batch, start, end, first, last):
    steps = []
    after = {5: ("turn_y", 0), 6: ("turn_y", 1), 7: ("project", 0), 8: ("project", 1), 13: ("route", 0),
             15: ("rank", 0)}
    before = {8: ("stats", 0), 9: ("stats", 1), 10: ("norm", 0), 11: ("turn_rows", 0), 12: ("turn_rows", 1)}
    between = {10: ("norm", 1), 14: ("pick", 0)}
    ahead = {16: ("load", 0), 18: ("load", 1), 17: ("copy_v", 0), 20: ("copy_v", 1), 24: ("load", 2),
             28: ("copy_v", 2)}
    own = {1: ("load", 3), 5: ("copy_v", 3)}
    for u in range(start, end):
        if u in ahead and not last:
            steps.append((*ahead[u], batch + 1))
        if u in own and not first:
            steps.append((*own[u], batch))
        g, whose = (u // 8 - 1, batch) if u >= 8 else (u // 8 - 1 + NG, batch - 1)
        begun = u >= 8 or not first
        if u % 8 == 4 and begun:
            steps.append(("heads_out", g, whose))
        maxima = [("max", a, batch) if a < NA else ("max", a - NA, batch + 1)
                  for a in (LEAD + 2 * u, LEAD + 2 * u + 1) if a < NA or not last]
        if u in before and not first:
            steps.append((*before[u], batch - 1))
        steps += maxima[:1]
        if u in between and not first:
            steps.append((*between[u], batch - 1))
        steps += [("scores", u, batch)] + maxima[1:]
        if u % 8 == 3:
            if u // 8 + 1 < NG:
                steps.append(("rows", u // 8 + 1, batch))
            elif not last:
                steps.append(("rows", 0, batch + 1))
        if u >= 4:
            steps.append(("values", u - 4, batch))
        elif not first:
            steps.append(("values", u - 4 + NU, batch - 1))
        if u % 8 == 4 and begun:
            steps.append(("heads", g, whose))
        if u in after and not first:
            steps.append((*after[u], batch - 1))
        if u == 14 and not first:
            steps.append(("choose", 0, batch - 1))
    return steps


def attention_begin():
    steps = [("copy_v", 0, 0), ("rows", 0, 0)] + [("max", a, 0) for a in range(16, LEAD)]
    steps += [("copy_v", g, 0) for g in range(1, NG)]
    return steps + attention_steps(0, 0, MIDDLE, first=True, last=False)


def attention_round(batch):
    return (attention_steps(batch, MIDDLE, NU, first=False, last=False)
            + attention_steps(batch + 1, 0, MIDDLE, first=False, last=False))


def attention_end():
    last = NB - 1
    return (attention_steps(last, MIDDLE, NU, first=False, last=True) + [("weights", 0, 0)]
            + [("values", n, last) for n in range(NU - 4, NU)] + [("heads_out", NG - 1, last), ("heads", NG - 1, last),
               ("turn_y", 0, last), ("turn_y", 1, last), ("project", 0, last), ("project", 1, last),
               ("stats", 0, last), ("stats", 1, last), ("norm", 0, last), ("norm", 1, last),
               ("turn_rows", 0, last), ("turn_rows", 1, last), ("route", 0, last), ("pick", 0, last),
               ("choose", 0, last), ("rank", 0, last)])


def split_product(pe, out, left, right, start, stop):
    pe.matmul(out, left[0], right[0], start=start, stop=False)
    pe.matmul(out, left[0], right[1], start=False, stop=False)
    return pe.matmul(out, left[1], right[0], start=False, stop=stop)


def tower(nc, x, tok_weight, tok_sum, w_qkv, b_qkv, w_proj, b_proj, w_router, b_router, w1, b1, w2, b2,
          identity, earlier, relative, relative_block, stack_rows, q_scale, expert_numbers, token_numbers,
          empty_numbers, out):
    slope = slopes()
    x_tiles = x.rearrange("b (t p) i d -> (b t) p (i d)", p=P)
    out_tiles = out.rearrange("(n p) c -> n p c", p=P)

    with ExitStack() as whole:
        def sb(name, shape, dt, scope=whole):
            return scope.enter_context(nc.sbuf_tensor(name, shape, dt))

        def two(name, shape, dt, scope=whole):
            return [sb(f"{name}{i}", shape, dt, scope) for i in range(2)]

        def sem(name):
            return whole.enter_context(nc.semaphore(name))

        def signal(name, per, by=1):
            return Signal(sem(name), per, by)

        slots = nc.dram_tensor("slots", [E * CAP, ROW], F32, kind="Internal").ap()
        parts = nc.dram_tensor("parts", [NB, 2, 2, H * D, T], F32, kind="Internal").ap()

        bank = [whole.enter_context(nc.psum_tensor(f"bank{i}", [P, 512], F32)) for i in range(4)]
        wide = [whole.enter_context(nc.psum_tensor(f"wide{i}", [P, 2, 512], F32)) for i in range(2)]

        idle = sem("idle")
        scattered = sem("scattered")

        ident = sb("ident", [P, P], F32)
        b1T = sb("b1T", [P, E * KH], F32)
        x_tiles_in = sb("x_tiles_in", [P, 2, C * XD], F32)
        h_and_ln = sb("h_and_ln", [P, 2, NT, C], F32)
        w1_raw = x_tiles_in.rearrange("p i n -> p (i n)").rearrange("p (c n) -> p c n", c=CH)
        w2_raw = h_and_ln.rearrange("p i t c -> p (i t) c")
        q_stack = sb("q_stack", [P, NG, GH, T], F32R)
        quarter = q_stack.rearrange("p g h t -> p g (h t)")
        w1_first = [quarter[:, i, :].rearrange("p (c n) -> p c n", c=CH) for i in range(2)]
        w2_first = [quarter[:, 2 + i, :].rearrange("p (k n) -> p k n", n=C) for i in range(2)]
        tokens = whole.enter_context(ExitStack())

        def tk(name, shape, dt):
            return sb(name, shape, dt, tokens)

        masked = [tk(f"masked{i}", [P, T], BF16) for i in range(2)]
        top_score = [tk(f"top_score{i}", [P, NT, GH], F32) for i in range(2)]
        empty = tk("empty", [P, NS, ROW], F32)
        wproj = tk("wproj", [P, CH, C], F32)
        wr = tk("wr", [P, CH, E], F32)
        br_all = tk("br_all", [P, E], F32)
        before = tk("before", [P, P], BF16)
        ones = tk("ones", [P, P], BF16)
        ident16 = tk("ident16", [P, P], BF16)
        rel = tk("rel", [P, 2 * T - P], F32)
        rel_block = tk("rel_block", [P, P], BF16)
        numbers = tk("numbers", [P, E], F32)
        token_id = tk("token_id", [P, NT], F32)
        power = tk("power", [P, 1], F32)
        run = tk("run", [P, E], BF16)
        k_stack = tk("k_stack", [P, NG, GH, T], F32R)
        residual = tk("residual", [P, NB * NT, C], F32)
        v_all = tk("v_all", [P, NB * NT, C], F32)
        rows_placed = sem("rows_placed")
        cleared = [sem("q_cleared"), sem("k_cleared")]
        stack_loaded = [signal(f"stack_loaded{g}", 1, 16 * 8) for g in range(NG)]
        s_full, s_done = signal("s_full", NA), signal("s_done", NA)
        psS = bank[0:2]
        w_loaded = signal("w_loaded", 2, 32)
        w_high, w_split = signal("w_high", 2), signal("w_split", 2)

        def load_stacks(sp, b, g):
            for which, stack, order in ((0, q_stack, Q_PARTS), (1, k_stack, K_PARTS)):
                for i, part in enumerate(order):
                    src = parts[b, which, part, g * GH * D:(g + 1) * GH * D, :]
                    sp.dma_start(stack[i * D:(i + 1) * D, g, :, :].bitcast(F32),
                                 src.rearrange("(h d) t -> d h t", d=D)).then_inc(stack_loaded[g].sem, 16)

        def max_products(pe, b, n):
            g, t, hd = n // 16, n % 16 // GH, n % GH
            if n % 16 == 0:
                pe.wait_ge(stack_loaded[g].sem, stack_loaded[g].at(b, 0))
            pe.wait_ge(s_done.sem, s_done.at(b, n - 2))
            pe.matmul(psS[n % 2][:, :], q_stack[0:MROW, g, hd, t * P:(t + 1) * P],
                      k_stack[0:MROW, g, hd, :], start=True, stop=True).then_inc(s_full.sem, 1)

        def max_of_tile(dve, b, n):
            g, t, hd = n // 16, n % 16 // GH, n % GH
            dve.wait_ge(s_full.sem, s_full.at(b, n))
            dve.sem_inc(idle, 1)
            first = T - P - t * P
            dve.tensor_tensor_reduce(masked[n % 2][:, :], psS[n % 2][:, :], rel[:, first:first + T],
                                     1.0, LOWEST, ALU.add, ALU.max,
                                     top_score[g % 2][:, t, hd:hd + 1]).then_inc(s_done.sem, 1)

        def load_weights(sp, pair, i):
            sp.dma_start(w1_raw, w1.rearrange("e (c p) n -> e p c n", p=P)[pair * 2 + i]
                         ).then_inc(w_loaded.sem, 16)
            sp.dma_start(w2_raw, w2.rearrange("e (k p) n -> e p k n", p=P)[pair * 2 + i]
                         ).then_inc(w_loaded.sem, 16)

        def high_weights(dve, pair, i, w1_part, w2_part):
            dve.wait_ge(w_loaded.sem, w_loaded.at(pair, i))
            dve.tensor_copy(w1_part[0], w1_raw)
            dve.tensor_copy(w2_part[0], w2_raw).then_inc(w_high.sem, 1)

        def low_weights(pool, pair, i, w1_part, w2_part):
            pool.wait_ge(w_high.sem, w_high.at(pair, i))
            pool.tensor_tensor(w1_part[1], w1_raw, w1_part[0], ALU.subtract)
            pool.tensor_tensor(w2_part[1], w2_raw, w2_part[0], ALU.subtract).then_inc(w_split.sem, 1)

        with ExitStack() as embedding:
            def em(name, shape, dt):
                return sb(name, shape, dt, embedding)

            ws = em("ws", [P, CH, C], F32)
            b1_rows = em("b1_rows", [E * KH, P], F32)
            before32 = em("before32", [P, P], F32)
            rel_block32 = em("rel_block32", [P, P], F32)
            rows32 = em("rows32", [8, 2, T], F32)
            empty_id = em("empty_id", [P, NS], F32)
            wtok = two("wtok", [P, XD, CH, C], F32R, embedding)
            wtok32 = em("wtok32", [P, CH, C], F32)
            wqkv32 = em("wqkv32", [P, CH, 3 * C], F32)
            wqkv = two("wqkv", [P, CH, 3 * C], F32R, embedding)
            bv_all = em("bv_all", [P, C], F32)
            bp_all = em("bp_all", [P, C], F32)
            bqk = em("bqk", [P, 4], F32)
            qscale = em("qscale", [P, 2], F32)
            bq_scaled = em("bq_scaled", [P, 2], F32)
            x_tile = [x_tiles_in[:, i, :] for i in range(2)]
            xT = [two(f"xT{i}_", [P, XD * CH, P], F32R, embedding) for i in range(2)]
            h, ln = h_and_ln[:, 0, :, :], h_and_ln[:, 1, :, :]
            stats = em("stats", [P, NT, 6], F32)
            moments = em("moments", [P, NT, 2], F32)
            var_eps = em("var_eps", [P, NT], F32)
            rstd = em("rstd", [P, NT], F32)
            wd = ln.rearrange("p n c -> p (n c)").rearrange("p (c d) -> p c d", d=XD)
            lnT = two("lnT", [P, CH, T], F32R, embedding)
            qk_raw = em("qk_raw", [P, 2, T], F32)
            qk_part = two("qk_part", [P, 2, T], F32R, embedding)

            first_loaded = sem("first_loaded")
            later_loaded = sem("later_loaded")
            empty_ready = sem("empty_ready")
            turned = sem("turned")
            w_step = sem("w_step")
            wtok_ready = sem("wtok_ready")
            wqkv_ready = sem("wqkv_ready")
            x_loaded = [signal(f"x_loaded{i}", NT // 2, 16) for i in range(2)]
            xt_full = signal("xt_full", 2 * NT)
            xt_high = signal("xt_high", 2 * NT)
            xt_done = signal("xt_done", 2 * NT)
            em_full = signal("em_full", NT)
            em_done = signal("em_done", NT)
            stats_done = signal("stats_done", NT)
            moments_ready = signal("moments_ready", NT)
            var_ready = signal("var_ready", NT)
            rstd_ready = signal("rstd_ready", NT)
            ln_ready = signal("ln_ready", NT)
            residual_ready = signal("residual_ready", NT)
            lt_full = signal("lt_full", 2)
            lt_high = signal("lt_high", 2)
            lt_done = signal("lt_done", 2)
            qk_full = signal("qk_full", 4)
            qk_done = signal("qk_done", 4)
            low_ready = signal("low_ready", 4)
            part_stored = [signal(f"part_stored{i}", 2, 32) for i in range(2)]
            v_full = signal("v_full", NT // 2)
            v_done = signal("v_done", NT // 2)
            bank_x, bank_e, bank_q, bank_l, bank_v = bank[0:2], bank[2:4], wide[0], wide[1][:, 0, :], wide[1][:, 1, :]

            first_loads = [
                (ident[:, :], identity),
                (ws[:, :, :], tok_sum.rearrange("(h p) i -> p h i", p=P)),
                (wd[:, :, :], tok_weight.partition_broadcast(P)),
            ]
            later_loads = [
                (wqkv32[:, :, :], w_qkv.rearrange("(h p) n -> p h n", p=P)),
                (bqk[:, :], b_qkv[0:2 * C].rearrange("(j p) -> p j", p=P)),
                (qscale[:, :], q_scale),
                (bv_all[:, :], b_qkv[2 * C:3 * C].partition_broadcast(P)),
                (bp_all[:, :], b_proj.partition_broadcast(P)),
                (b1_rows[:, :], b1.rearrange("e (k p) -> (e k) p", p=P)),
                (before32[:, :], earlier),
                (rel_block32[:, :], relative_block),
                (rel[:, :], relative),
                (rows32[:, :, :], stack_rows),
                (empty_id[:, :], empty_numbers),
                (wproj[:, :, :], w_proj.rearrange("(h p) n -> p h n", p=P)),
                (wr[:, :, :], w_router.rearrange("(h p) n -> p h n", p=P)),
                (br_all[:, :], b_router.partition_broadcast(P)),
                (numbers[:, :], expert_numbers.partition_broadcast(P)),
                (token_id[:, :], token_numbers),
            ]

            def rounds(engine, body):
                body(-1, embedding_steps(first=True, last=False))
                with engine.Fori(0, NB - 1) as b:
                    body(b, embedding_steps(first=False, last=False))
                body(NB - 1, embedding_steps(first=False, last=True))

            with nc.Block() as block:
                @block.sync
                def _(sp):
                    for s in [*x_loaded, *stack_loaded]:
                        sp.sem_inc(s.sem, s.credit)
                    for dst, src in first_loads:
                        sp.dma_start(dst, src).then_inc(first_loaded, 16)

                    def body(b, steps):
                        for what, n, new in steps:
                            if what == "turn_x":
                                sp.wait_ge(xt_full.sem, xt_full.at(b + new, 2 * n - 3))
                                sp.dma_start(x_tile[n % 2], x_tiles[(b + new) * NT + n]
                                             ).then_inc(x_loaded[n % 2].sem, 16)

                    rounds(sp, body)
                    for stored in part_stored:
                        sp.wait_ge(stored.sem, stored.at(0, 1))
                    for g in range(NG):
                        load_stacks(sp, 0, g)

                @block.gpsimd
                def _(pool):
                    for s in (var_ready, rstd_ready, residual_ready, low_ready):
                        pool.sem_inc(s.sem, s.credit)
                    pool.memset(q_stack[SPLIT:P, :, :, :].bitcast(F32), 0.0).then_inc(cleared[0], 1)
                    pool.wait_ge(empty_ready, 2)
                    for e in range(E):
                        dst = slots[e * CAP:(e + 1) * CAP, :].rearrange("(s p) c -> p s c", p=P)
                        pool.dma_start(dst, empty[:, :, :]).then_inc(scattered, 16)
                    for s in range(NS):
                        pool.dma_start(out_tiles[NB * NT + s], empty[:, s, 0:C]).then_inc(scattered, 16)
                    pool.wait_ge(cleared[0], 1)
                    pool.wait_ge(wqkv_ready, 1)
                    pool.tensor_tensor(wqkv[1][:, :, :], wqkv32[:, :, :], wqkv[0][:, :, :],
                                       ALU.subtract).then_inc(wqkv_ready, 1)

                    def body(b, steps):
                        for what, n, new in steps:
                            if what == "embed":
                                e = b + new
                                pool.wait_ge(moments_ready.sem, moments_ready.at(e, n))
                                pool.sem_inc(idle, 1)
                                pool.tensor_scalar(var_eps[:, n:n + 1], moments[:, n, 1:2], EPS, None,
                                                   ALU.add).then_inc(var_ready.sem, 1)
                                pool.wait_ge(var_ready.sem, var_ready.at(e, n))
                                pool.tensor_tensor(rstd[:, n:n + 1], var_eps[:, n:n + 1], power[:, :],
                                                   ALU.pow).then_inc(rstd_ready.sem, 1)
                                pool.wait_ge(em_done.sem, em_done.at(e, n))
                                pool.tensor_tensor(residual[:, bass.ds(e * NT + n, 1), :].rearrange("p o c -> p (o c)"),
                                                   h[:, n, :], bp_all[:, :], ALU.add).then_inc(residual_ready.sem, 1)
                            elif what == "qk":
                                pool.wait_ge(qk_done.sem, qk_done.at(b, n))
                                pool.wait_ge(part_stored[n % 2].sem, part_stored[n % 2].at(b, n // 2 - 1))
                                pool.tensor_tensor(qk_part[1][:, n % 2, :], qk_raw[:, n % 2, :],
                                                   qk_part[0][:, n % 2, :], ALU.subtract).then_inc(low_ready.sem, 1)

                    rounds(pool, body)

                @block.tensor
                def _(pe):
                    for s in (xt_full, em_full, lt_full, qk_full, v_full, s_full):
                        pe.sem_inc(s.sem, s.credit)
                    pe.wait_ge(first_loaded, 16 * len(first_loads))
                    for ih in range(CH):
                        for oh in range(CH):
                            at = ih * C + oh * P
                            last = pe.transpose(bank[2][:, at:at + P], ws[:, oh, ih * P:(ih + 1) * P], ident[:, :])
                    last.then_inc(turned, 1)
                    pe.wait_ge(later_loaded, 16 * len(later_loads))
                    pe.transpose(bank[3][:, 0:E * KH], b1_rows[:, :],
                                 ident[0:E * KH, 0:E * KH]).then_inc(turned, 1)
                    pe.wait_ge(wtok_ready, 1)

                    def body(b, steps):
                        for what, n, new in steps:
                            e = b + new
                            if what == "turn_x":
                                pe.wait_ge(x_loaded[n % 2].sem, x_loaded[n % 2].at(e, n // 2))
                                xv = x_tile[n % 2].rearrange("p (i d) -> p i d", d=XD)
                                for half in range(2):
                                    pe.wait_ge(xt_done.sem, xt_done.at(e, 2 * n + half - 2))
                                    for k in range(4 * half, 4 * half + 4):
                                        d, ih = k // CH, k % CH
                                        last = pe.transpose(bank_x[half][:, (k % 4) * P:(k % 4 + 1) * P],
                                                            xv[:, ih * P:(ih + 1) * P, d], ident[:, :])
                                    last.then_inc(xt_full.sem, 1)
                            elif what == "embed":
                                pe.wait_ge(xt_done.sem, xt_done.at(e, 2 * n + 1))
                                pe.wait_ge(em_done.sem, em_done.at(e, n - 2))
                                for k in range(XD * CH):
                                    last = split_product(
                                        pe, bank_e[n % 2][:, 0:C], [xT[n % 2][i][:, k, :] for i in range(2)],
                                        [wtok[i][:, k // CH, k % CH, :] for i in range(2)],
                                        start=(k == 0), stop=(k == XD * CH - 1))
                                last.then_inc(em_full.sem, 1)
                            elif what == "turn_ln":
                                pe.wait_ge(lt_done.sem, lt_done.at(e, n - 1))
                                for t in (2 * n, 2 * n + 1):
                                    pe.wait_ge(ln_ready.sem, ln_ready.at(e, t))
                                    for c in range(CH):
                                        at = c * 2 * P + (t % 2) * P
                                        last = pe.transpose(bank_l[:, at:at + P], ln[:, t, c * P:(c + 1) * P],
                                                            ident[:, :])
                                last.then_inc(lt_full.sem, 1)
                            elif what == "qk":
                                pe.wait_ge(wqkv_ready, 2)
                                pe.wait_ge(lt_done.sem, lt_done.at(b, 1))
                                pe.wait_ge(qk_done.sem, qk_done.at(b, n - 2))
                                for c in range(CH):
                                    last = split_product(
                                        pe, bank_q[:, n % 2, :], [wqkv[i][:, c, n * P:(n + 1) * P] for i in range(2)],
                                        [lnT[i][:, c, :] for i in range(2)], start=(c == 0), stop=(c == CH - 1))
                                last.then_inc(qk_full.sem, 1)
                            elif what == "max":
                                if n == 0:
                                    pe.wait_ge(xt_done.sem, xt_done.at(NB - 1, 2 * NT - 1))
                                    pe.wait_ge(rows_placed, 4 * 16)
                                max_products(pe, 0, n)
                            elif what == "value":
                                pe.wait_ge(v_done.sem, v_done.at(b, n - 1))
                                for t in (2 * n, 2 * n + 1):
                                    for c in range(CH):
                                        last = split_product(
                                            pe, bank_v[:, (t % 2) * C:(t % 2 + 1) * C],
                                            [lnT[i][:, c, t * P:(t + 1) * P] for i in range(2)],
                                            [wqkv[i][:, c, 2 * C:3 * C] for i in range(2)],
                                            start=(c == 0), stop=(c == CH - 1))
                                last.then_inc(v_full.sem, 1)

                    rounds(pe, body)

                @block.scalar
                def _(act):
                    for s in (xt_high, lt_high, qk_done, *part_stored):
                        act.sem_inc(s.sem, s.credit)
                    with nc.allow_non_contiguous_dma("biases by partition"):
                        for dst, src in later_loads:
                            act.dma_start(dst, src).then_inc(later_loaded, 16)
                    act.wait_ge(later_loaded, 16 * len(later_loads))
                    for half, stack in ((0, q_stack), (1, k_stack)):
                        act.wait_ge(cleared[half], 1)
                        act.dma_start(stack[SPLIT:SPLIT + ALIBI, :, :, :].rearrange("p g h t -> p (g h) t")
                                      .bitcast(F32), rows32[0:ALIBI, half, :].unsqueeze(1).to_broadcast([ALIBI, H, T])
                                      ).then_inc(rows_placed, 16)
                        act.dma_start(stack[MROW:P, :, :, :].rearrange("p g h t -> p (g h) t").bitcast(F32),
                                      rows32[ALIBI:ALIBI + 2, half, :].unsqueeze(1).to_broadcast([2, H, T])
                                      ).then_inc(rows_placed, 16)

                    def body(b, steps):
                        for what, n, new in steps:
                            e = b + new
                            if what == "turn_x":
                                act.wait_ge(em_full.sem, em_full.at(e, n - 2))
                                for half in range(2):
                                    act.wait_ge(xt_full.sem, xt_full.at(e, 2 * n + half))
                                    act.activation(xT[n % 2][0][:, 4 * half:4 * half + 4, :],
                                                   bank_x[half][:, :].rearrange("p (k n) -> p k n", n=P),
                                                   ACT.Copy).then_inc(xt_high.sem, 1)
                            elif what == "turn_ln":
                                act.wait_ge(v_full.sem, v_full.at(e, -1))
                                act.wait_ge(lt_full.sem, lt_full.at(e, n))
                                act.activation(lnT[0][:, :, 2 * n * P:2 * (n + 1) * P],
                                               bank_l.rearrange("p (c n) -> p c n", c=CH),
                                               ACT.Copy).then_inc(lt_high.sem, 1)
                            elif what == "qk":
                                act.wait_ge(qk_full.sem, qk_full.at(b, n))
                                act.wait_ge(part_stored[n % 2].sem, part_stored[n % 2].at(b, n // 2 - 1))
                                scale = qscale[:, n:n + 1] if n < 2 else 1.0
                                bias = bq_scaled[:, n:n + 1] if n < 2 else bqk[:, n:n + 1]
                                act.activation(qk_part[0][:, n % 2, :], bank_q[:, n % 2, :], ACT.Identity, bias=bias,
                                               scale=scale)
                                act.activation(qk_raw[:, n % 2, :], bank_q[:, n % 2, :], ACT.Identity, bias=bias,
                                               scale=scale).then_inc(qk_done.sem, 1)

                            elif what == "store":
                                act.wait_ge(low_ready.sem, low_ready.at(b, n))
                                act.sem_inc(idle, 1)
                                for part in range(2):
                                    dst = parts[b, n // 2, part, (n % 2) * P:(n % 2 + 1) * P, :]
                                    act.dma_start(dst, qk_part[part][:, n % 2, :].bitcast(F32)
                                                  ).then_inc(part_stored[n % 2].sem, 16)

                    rounds(act, body)
                    for i in range(2):
                        act.wait_ge(part_stored[i].sem, part_stored[i].at(NB - 1, 1))
                    act.wait_ge(rows_placed, 4 * 16)

                @block.vector
                def _(dve):
                    for s in (xt_done, em_done, stats_done, moments_ready, ln_ready, lt_done, v_done, s_done):
                        dve.sem_inc(s.sem, s.credit)
                    dve.memset(empty[:, :, :], 0.0).then_inc(empty_ready, 1)
                    dve.memset(k_stack[SPLIT:P, :, :, :].bitcast(F32), 0.0).then_inc(cleared[1], 1)
                    dve.memset(ones[:, :], 1.0)
                    dve.memset(run[:, :], 0.0)
                    dve.memset(power[:, :], -0.5)
                    dve.wait_ge(turned, 1)
                    sums = bank[2][:, :].rearrange("p (i o) -> p i o", i=CH)
                    for d in range(XD):
                        by = wd[:, :, d].unsqueeze(1).to_broadcast([P, CH, C])
                        if d:
                            dve.wait_ge(w_step, 3 * d)
                        dve.tensor_tensor(wtok32[:, :, :], sums, by, ALU.mult).then_inc(w_step, 1)
                        dve.wait_ge(w_step, 3 * d + 1)
                        dve.tensor_copy(wtok[0][:, d, :, :], wtok32[:, :, :]).then_inc(w_step, 1)
                        dve.wait_ge(w_step, 3 * d + 2)
                        last = dve.tensor_tensor(wtok[1][:, d, :, :], wtok32[:, :, :], wtok[0][:, d, :, :],
                                                 ALU.subtract)
                        last.then_inc(w_step if d < XD - 1 else wtok_ready, 1)
                    dve.wait_ge(later_loaded, 16 * len(later_loads))
                    dve.tensor_copy(wqkv[0][:, :, :], wqkv32[:, :, :]).then_inc(wqkv_ready, 1)
                    dve.wait_ge(empty_ready, 1)
                    dve.tensor_copy(empty[:, :, :].bitcast(U32)[:, :, TOKEN], empty_id[:, :]).then_inc(empty_ready, 1)
                    dve.tensor_copy(before[:, :], before32[:, :])
                    dve.tensor_copy(ident16[:, :], ident[:, :])
                    dve.tensor_copy(rel_block[:, :], rel_block32[:, :])
                    dve.tensor_tensor(bq_scaled[:, :], bqk[:, 0:2], qscale[:, :], ALU.mult)
                    dve.wait_ge(turned, 2)
                    dve.tensor_copy(b1T[:, :], bank[3][:, 0:E * KH]).then_inc(w_step, 1)
                    dve.wait_ge(w_step, 3 * XD)

                    def body(b, steps):
                        for what, n, new in steps:
                            e = b + new
                            if what == "turn_x":
                                for half in range(2):
                                    dve.wait_ge(xt_high.sem, xt_high.at(e, 2 * n + half))
                                    dve.tensor_tensor(xT[n % 2][1][:, 4 * half:4 * half + 4, :],
                                                      bank_x[half][:, :].rearrange("p (k n) -> p k n", n=P),
                                                      xT[n % 2][0][:, 4 * half:4 * half + 4, :],
                                                      ALU.subtract).then_inc(xt_done.sem, 1)
                            elif what == "embed":
                                dve.wait_ge(em_full.sem, em_full.at(e, n))
                                dve.sem_inc(idle, 1)
                                dve.bn_stats(stats[:, n, :], bank_e[n % 2][:, 0:C]).then_inc(stats_done.sem, 1)
                                dve.wait_ge(stats_done.sem, stats_done.at(e, n))
                                dve.sem_inc(idle, 1)
                                dve.bn_aggr(moments[:, n, :], stats[:, n, :]).then_inc(moments_ready.sem, 1)
                                dve.wait_ge(residual_ready.sem, residual_ready.at(e, n - NT))
                                dve.sem_inc(idle, 1)
                                dve.tensor_copy(h[:, n, :], bank_e[n % 2][:, 0:C]).then_inc(em_done.sem, 1)
                            elif what == "norm":
                                dve.wait_ge(em_done.sem, em_done.at(e, n))
                                dve.wait_ge(lt_full.sem, lt_full.at(e, n // 2 - 2))
                                dve.wait_ge(rstd_ready.sem, rstd_ready.at(e, n))
                                dve.tensor_scalar(ln[:, n, :], h[:, n, :], moments[:, n, 0:1], rstd[:, n:n + 1],
                                                  ALU.subtract, ALU.mult).then_inc(ln_ready.sem, 1)
                            elif what == "turn_ln":
                                dve.wait_ge(lt_high.sem, lt_high.at(e, n))
                                dve.tensor_tensor(lnT[1][:, :, 2 * n * P:2 * (n + 1) * P],
                                                  bank_l.rearrange("p (c n) -> p c n", c=CH),
                                                  lnT[0][:, :, 2 * n * P:2 * (n + 1) * P],
                                                  ALU.subtract).then_inc(lt_done.sem, 1)
                            elif what == "max":
                                max_of_tile(dve, 0, n)
                            elif what == "value":
                                dve.wait_ge(v_full.sem, v_full.at(b, n))
                                dve.tensor_tensor(v_all[:, bass.ds(b * NT + 2 * n, 2), :],
                                                  bank_v.rearrange("p (t c) -> p t c", c=C),
                                                  bv_all[:, :].unsqueeze(1).to_broadcast([P, 2, C]),
                                                  ALU.add).then_inc(v_done.sem, 1)

                    rounds(dve, body)

        v_aug = tk("v_aug", [P, NT, H, 2 * D], F32)
        m_raw = tk("m_raw", [GH, T], F32)
        m_rows = tk("m_rows", [GH, 2, T], F32R)
        probs = [tk(f"probs{i}", [P, GH, 2, T], F32) for i in range(2)]
        heads_t = tk("heads_t", [P, T], F32)
        denom = tk("denom", [P, NT, GH], F32)
        y = tk("y", [P, NT, C], F32)
        yT = tk("yT", [P, CH, T], F32)
        stats = tk("stats2", [P, NT, 6], F32)
        moments = tk("moments2", [P, NT, 2], F32)
        var_eps = tk("var_eps2", [P, NT], F32)
        rstd = tk("rstd2", [P, NT], F32)
        shift = tk("shift", [P, NT], F32)
        minus_shift = tk("minus_shift", [P, NT], F32)
        h = tk("h2", [P, NT, C], F32)
        rows = tk("rows", [P, NT, ROW], F32)
        rowsT = tk("rowsT", [P, CH, T], F32)
        logits = tk("logits", [P, NT, E], F32)
        top8 = tk("top8", [P, NT, 8], F32)
        top_at = tk("top_at", [P, NT, 8], U32)
        top_expert = tk("top_expert", [P, NT, 8], F32)
        hot = [tk(f"hot{i}", [P, NT, E], F32) for i in range(2)]
        sel = tk("sel", [P, NT, E], BF16)
        sel_sum = tk("sel_sum", [P, E], F32)
        gap = tk("gap", [P, NT], F32)
        gap_exp = tk("gap_exp", [P, NT], F32)
        gap_sum = tk("gap_sum", [P, NT], F32)
        picked = [tk(f"picked{i}", [P, NT, E], F32) for i in range(2)]
        rank = tk("rank", [P, 2, NT], F32)
        dropped = tk("dropped", [P, 2, NT], F32)
        slot = tk("slot", [P, 2, NT], F32)
        slot_at = tk("slot_at", [P, 2, NT], U32)

        v_cleared = sem("v_cleared")
        v_copied = signal("v_copied", NG)
        p_full, p_done = signal("p_full", NU), signal("p_done", NU)
        rows_turned = signal("rows_turned", NG)
        rows_out = signal("rows_out", NG)
        m_split = signal("m_split", NG)
        m_loaded = signal("m_loaded", NG, 16 * GH)
        values_done = signal("values_done", NU)
        heads_out = signal("heads_out", NG)
        heads_turned = signal("heads_turned", NG)
        denom_ready = signal("denom_ready", NG)
        y_ready = signal("y_ready", NG)
        y_turned, y_out = signal("y_turned", CH), signal("y_out", CH)
        projected = signal("projected", 2)
        h_ready = signal("h_ready", 2)
        h_stored = [signal(f"h_stored{i}", 1, 16) for i in range(2)]
        moments_ready = signal("moments_ready2", 2)
        var_ready, rstd_ready = signal("var_ready2", 2), signal("rstd_ready2", 2)
        shift_half, shift_ready = signal("shift_half", 2), signal("shift_ready", 2)
        row_ready = signal("row_ready", NT)
        stats_done = signal("stats_done2", NT)
        r_turned, r_out = signal("r_turned", CH), signal("r_out", CH)
        routed, logits_ready = signal("routed", 1), signal("logits_ready", 1)
        VEC = 11
        vec = signal("vec", VEC)
        sel_ready = signal("sel_ready", 1)
        gap_ready, gap_done = signal("gap_ready", 1), signal("gap_done", 1)
        ranked, ranks_out = signal("ranked", 1), signal("ranks_out", 1)
        slot_ready = signal("slot_ready", 1)
        psP, psO, psM = wide, bank[2], bank[3]

        def rounds2(engine, body):
            body(attention_begin())
            with engine.Fori(0, NB - 1) as b:
                body(attention_round(b))
            body(attention_end())

        with nc.Block() as block:
            @block.sync
            def _(sp):
                for s in [m_loaded, *h_stored, w_loaded]:
                    sp.sem_inc(s.sem, s.credit)
                load_weights(sp, 0, 0)

                def body(steps):
                    for what, n, b in steps:
                        if what == "load":
                            sp.wait_ge(p_full.sem, p_full.at(b, 8 * n + 7 - NU))
                            sp.sem_inc(idle, 1)
                            load_stacks(sp, b, n)
                        elif what == "rows":
                            sp.wait_ge(m_split.sem, m_split.at(b, n))
                            for hd in range(GH):
                                sp.dma_start(q_stack[MROW:MROW + 2, n, hd, :].bitcast(F32),
                                             m_rows[hd:hd + 1, :, :].bitcast(F32)).then_inc(m_loaded.sem, 16)
                        elif what == "project":
                            sp.wait_ge(h_ready.sem, h_ready.at(b, n))
                            sp.sem_inc(idle, 1)
                            sp.dma_start(out_tiles[bass.ds(b * NT + 2 * n, 2)].rearrange("n p c -> p n c"),
                                         h[:, 2 * n:2 * n + 2, :]).then_inc(h_stored[n].sem, 16)


                rounds2(sp, body)
                sp.wait_ge(w_split.sem, w_split.at(0, 0))
                load_weights(sp, 0, 1)
                for stored in h_stored:
                    sp.wait_ge(stored.sem, stored.at(NB - 1, 0))

            @block.tensor
            def _(pe):
                for s in (p_full, rows_turned, values_done, heads_turned, y_turned, projected, r_turned,
                          routed, ranked):
                    pe.sem_inc(s.sem, s.credit)
                last_use = [(ranks_out, 0, -1)]

                def psM_after(done, b, event):
                    signal_, batch_, event_ = last_use[0]
                    pe.wait_ge(signal_.sem, signal_.at(batch_, event_))
                    last_use[0] = (done, b, event)

                def body(steps):
                    for what, n, b in steps:
                        if what == "max":
                            max_products(pe, b, n)
                        elif what == "rows":
                            pe.wait_ge(s_done.sem, s_done.at(b, 16 * n + 15))
                            psM_after(rows_out, b, n)
                            for t in range(NT):
                                last = pe.transpose(psM[0:GH, t * P:(t + 1) * P], top_score[n % 2][:, t, :],
                                                    ident[:, :])
                            last.then_inc(rows_turned.sem, 1)
                        elif what == "scores":
                            g, half, hd = n // 8, n % 8 // GH, n % GH
                            if n % 8 == 0:
                                pe.wait_ge(m_loaded.sem, m_loaded.at(b, g))
                            pe.wait_ge(p_done.sem, p_done.at(b, n - 2))
                            for i in range(2):
                                s = 2 * half + i
                                pe.matmul(psP[n % 2][:, i, s * P:(s + 1) * P], ident16[:, :], rel_block[:, :],
                                          start=True, stop=True)
                            for i in range(2):
                                s = 2 * half + i
                                last = pe.matmul(psP[n % 2][:, i, :], k_stack[:, g, hd, s * P:(s + 1) * P],
                                                 q_stack[:, g, hd, :], start=False, stop=True,
                                                 skip_group_check=True)
                            last.then_inc(p_full.sem, 1)
                        elif what == "values":
                            g, half, s, i = n // 8, n // 4, n // 2 % 4, n // 2 % 2
                            columns = slice(n % 2 * (T // 2), (n % 2 + 1) * (T // 2))
                            pe.wait_ge(p_done.sem, p_done.at(b, 4 * half + 3))
                            if n % 8 == 0:
                                pe.wait_ge(v_copied.sem, v_copied.at(b, g))
                                pe.wait_ge(heads_out.sem, heads_out.at(b, g - 1))
                            for hd in range(GH):
                                last = pe.matmul(psO[32 * hd:32 * hd + 32, columns], v_aug[:, s, g * GH + hd, :],
                                                 probs[half % 2][:, hd, i, columns], start=(n % 8 == 0),
                                                 stop=(n % 8 == 7), tile_position=(0, 32 * hd),
                                                 skip_group_check=True)
                            last.then_inc(values_done.sem, 1)
                        elif what == "heads":
                            pe.wait_ge(heads_out.sem, heads_out.at(b, n))
                            psM_after(y_ready, b, n)
                            for t in range(NT):
                                last = pe.transpose(psM[:, t * P:(t + 1) * P], heads_t[:, t * P:(t + 1) * P],
                                                    ident[:, :])
                            last.then_inc(heads_turned.sem, 1)
                        elif what == "turn_y":
                            pe.wait_ge(y_ready.sem, y_ready.at(b, NG - 1))
                            psM_after(y_out, b, n)
                            for t in range(NT):
                                last = pe.transpose(psM[:, t * P:(t + 1) * P], y[:, t, n * P:(n + 1) * P],
                                                    ident[:, :])
                            last.then_inc(y_turned.sem, 1)
                        elif what == "project":
                            pe.wait_ge(y_out.sem, y_out.at(b, CH - 1))
                            psM_after(h_ready, b, n)
                            for t in (2 * n, 2 * n + 1):
                                for c in range(CH):
                                    last = pe.matmul(psM[:, (t % 2) * C:(t % 2 + 1) * C],
                                                     yT[:, c, t * P:(t + 1) * P], wproj[:, c, :],
                                                     start=(c == 0), stop=(c == CH - 1))
                            last.then_inc(projected.sem, 1)
                        elif what == "turn_rows":
                            psM_after(r_out, b, n)
                            for t in range(NT):
                                if n == 0:
                                    pe.wait_ge(row_ready.sem, row_ready.at(b, t))
                                last = pe.transpose(psM[:, t * P:(t + 1) * P], rows[:, t, n * P:(n + 1) * P],
                                                    ident[:, :])
                            last.then_inc(r_turned.sem, 1)
                        elif what == "route":
                            pe.wait_ge(r_out.sem, r_out.at(b, CH - 1))
                            psM_after(logits_ready, b, 0)
                            for t in range(NT):
                                for c in range(CH):
                                    last = pe.matmul(psM[:, t * E:(t + 1) * E], rowsT[:, c, t * P:(t + 1) * P],
                                                     wr[:, c, :], start=(c == 0), stop=(c == CH - 1))
                            last.then_inc(routed.sem, 1)
                        elif what == "rank":
                            pe.wait_ge(sel_ready.sem, sel_ready.at(b, 0))
                            psM_after(ranks_out, b, 0)
                            for t in range(NT):
                                o = psM[:, t * E:(t + 1) * E]
                                pe.matmul(o, before[:, :], sel[:, t, :], start=True, stop=False)
                                for t0 in range(t):
                                    pe.matmul(o, ones[:, :], sel[:, t0, :], start=False, stop=False)
                                last = pe.matmul(o, ones[:, :], run[:, :], start=False, stop=True)
                            last.then_inc(ranked.sem, 1)

                rounds2(pe, body)

            @block.scalar
            def _(act):
                for s in (p_done, rows_out, heads_out, y_out, row_ready, r_out, gap_done):
                    act.sem_inc(s.sem, s.credit)

                def body(steps):
                    for what, n, b in steps:
                        if what == "rows":
                            act.wait_ge(rows_turned.sem, rows_turned.at(b, n))
                            act.wait_ge(m_loaded.sem, m_loaded.at(b, n - 1))
                            act.activation(m_rows[:, 0, :], psM[0:GH, :], ACT.Copy)
                            act.activation(m_raw[:, :], psM[0:GH, :], ACT.Copy).then_inc(rows_out.sem, 1)
                        elif what == "scores":
                            g, half, hd = n // 8, n % 8 // GH, n % GH
                            act.wait_ge(p_full.sem, p_full.at(b, n))
                            if hd == 0:
                                act.wait_ge(values_done.sem, values_done.at(b, n - 5))
                            act.activation(probs[n // GH % 2][:, hd, :, :], psP[n % 2][:, :, :], ACT.Exp,
                                           scale=slope[g * GH + hd]).then_inc(p_done.sem, 1)
                        elif what == "heads_out":
                            act.wait_ge(values_done.sem, values_done.at(b, 8 * n + 7))
                            act.wait_ge(heads_turned.sem, heads_turned.at(b, n - 1))
                            act.activation(heads_t[:, :], psO[:, :], ACT.Copy).then_inc(heads_out.sem, 1)
                        elif what == "turn_y":
                            act.wait_ge(y_turned.sem, y_turned.at(b, n))
                            act.activation(yT[:, n, :], psM[:, :], ACT.Copy).then_inc(y_out.sem, 1)
                        elif what == "norm":
                            if n == 0:
                                act.wait_ge(scattered, b * (2 * NT * 16) + CLEARS * 16)
                            act.wait_ge(shift_ready.sem, shift_ready.at(b, n))
                            for t in (2 * n, 2 * n + 1):
                                act.activation(rows[:, t, 0:C], h[:, t, :], ACT.Identity, bias=minus_shift[:, t:t + 1],
                                               scale=rstd[:, t:t + 1]).then_inc(row_ready.sem, 1)
                        elif what == "turn_rows":
                            act.wait_ge(r_turned.sem, r_turned.at(b, n))
                            act.activation(rowsT[:, n, :], psM[:, :], ACT.Copy).then_inc(r_out.sem, 1)
                        elif what == "rank":
                            act.wait_ge(gap_ready.sem, gap_ready.at(b, 0))
                            act.activation(gap_exp[:, :], gap[:, :], ACT.Exp).then_inc(gap_done.sem, 1)

                rounds2(act, body)

            @block.vector
            def _(dve):
                for s in (w_high, denom_ready, y_ready, h_ready, moments_ready, logits_ready, vec, sel_ready,
                          gap_ready, ranks_out, slot_ready, stats_done):
                    dve.sem_inc(s.sem, s.credit)
                dve.memset(v_aug[:, :, :, D:2 * D], 0.0).then_inc(v_cleared, 1)
                dve.wait_ge(v_cleared, 1)
                dve.memset(v_aug[:, :, :, D:D + 1], 1.0).then_inc(v_cleared, 1)

                def route(b, settle):
                    dve.wait_ge(routed.sem, routed.at(b, 0))
                    dve.tensor_tensor(logits[:, :, :], psM[:, 0:NT * E].rearrange("p (t e) -> p t e", e=E),
                                      br_all[:, :].unsqueeze(1).to_broadcast([P, NT, E]),
                                      ALU.add).then_inc(logits_ready.sem, 1)
                    dve.wait_ge(logits_ready.sem, logits_ready.at(b, 0))
                    dve.sem_inc(idle, 1)
                    for t in range(NT):
                        last = dve.max(top8[:, t, :], logits[:, t, :])
                    settle(last)

                def pick(settle):
                    dve.sem_inc(idle, 1)
                    for t in range(NT):
                        last = dve.max_index(top_at[:, t, :], top8[:, t, :], logits[:, t, :])
                    settle(last)
                    settle(dve.tensor_copy(top_expert[:, :, :], top_at[:, :, :]))

                def choose(b, settle):
                    for i in range(2):
                        last = dve.tensor_tensor(hot[i][:, :, :], numbers[:, :].unsqueeze(1).to_broadcast([P, NT, E]),
                                                 top_expert[:, :, i:i + 1].to_broadcast([P, NT, E]), ALU.is_equal)
                    settle(last)
                    dve.tensor_tensor(sel[:, :, :], hot[0][:, :, :], hot[1][:, :, :],
                                      ALU.add).then_inc(sel_ready.sem, 1)
                    dve.tensor_tensor(gap[:, :], top8[:, :, 1], top8[:, :, 0], ALU.subtract).then_inc(gap_ready.sem, 1)
                    dve.tensor_copy(rows[:, :, FIRST], top_expert[:, :, 0])
                    settle(dve.tensor_copy(rows[:, :, :].bitcast(U32)[:, :, TOKEN], token_id[:, :]))
                    dve.tensor_scalar(token_id[:, :], token_id[:, :], float(T), None, ALU.add)

                def place(b, settle):
                    dve.wait_ge(gap_done.sem, gap_done.at(b, 0))
                    settle(dve.tensor_scalar(gap_sum[:, :], gap_exp[:, :], 1.0, None, ALU.add))
                    settle(dve.reciprocal(rows[:, :, GATE1], gap_sum[:, :]))
                    dve.tensor_tensor(rows[:, :, GATE2], rows[:, :, GATE1], gap_exp[:, :], ALU.mult)
                    dve.wait_ge(ranked.sem, ranked.at(b, 0))
                    ranks = psM[:, 0:NT * E].rearrange("p (t e) -> p t e", e=E)
                    dve.tensor_tensor(picked[0][:, :, :], ranks, hot[0][:, :, :], ALU.mult)
                    dve.tensor_tensor(picked[1][:, :, :], ranks, hot[1][:, :, :], ALU.mult).then_inc(ranks_out.sem, 1)
                    dve.wait_ge(ranks_out.sem, ranks_out.at(b, 0))
                    for i in range(2):
                        last = dve.tensor_reduce(rank[:, i, :], picked[i][:, :, :], AX.X, ALU.add)
                    settle(last)
                    dve.tensor_scalar(dropped[:, :, :], rank[:, :, :], float(CAP), float(2 * E * CAP),
                                      ALU.is_ge, ALU.mult)
                    settle(dve.scalar_tensor_tensor(
                        out=slot[:, :, :], in0=top_expert[:, :, 0:2].rearrange("p t i -> p i t"), scalar=float(CAP),
                        in1=rank[:, :, :], op0=ALU.mult, op1=ALU.add))
                    dve.tensor_tensor(slot_at[:, :, :], slot[:, :, :], dropped[:, :, :],
                                      ALU.add).then_inc(slot_ready.sem, 1)
                    settle(dve.tensor_reduce(sel_sum[:, :], sel[:, :, :].rearrange("p t e -> p e t"), AX.X, ALU.add))
                    dve.tensor_tensor(run[:, :], run[:, :], sel_sum[:, :], ALU.add).then_inc(vec.sem, 1)

                def body(steps):
                    own = [0]
                    for what, n, b in steps:
                        def settle(instruction):
                            instruction.then_inc(vec.sem, 1)
                            dve.wait_ge(vec.sem, vec.at(b, own[0]))
                            own[0] += 1

                        if what == "max":
                            if n % 16 == 0:
                                dve.wait_ge(rows_turned.sem, rows_turned.at(b, n // 16 - 2))
                                dve.sem_inc(idle, 1)
                            max_of_tile(dve, b, n)
                        elif what == "weights":
                            dve.wait_ge(p_full.sem, p_full.at(NB - 1, NU - 1))
                            high_weights(dve, 0, 0, w1_first, w2_first)
                        elif what == "heads":
                            dve.wait_ge(heads_turned.sem, heads_turned.at(b, n))
                            o = psM[:, :].rearrange("p (t h d) -> p t h d", t=NT, h=GH)
                            dve.reciprocal(denom[:, :, :], o[:, :, :, D]).then_inc(denom_ready.sem, 1)
                            dve.wait_ge(denom_ready.sem, denom_ready.at(b, n))
                            if n == 0:
                                dve.wait_ge(y_turned.sem, y_turned.at(b, -1))
                            dve.tensor_tensor(
                                y[:, :, n * GH * D:(n + 1) * GH * D].rearrange("p t (h d) -> p t h d", d=D),
                                o[:, :, :, 0:D], denom[:, :, :].unsqueeze(3).to_broadcast([P, NT, GH, D]),
                                ALU.mult).then_inc(y_ready.sem, 1)
                        elif what == "project":
                            dve.wait_ge(h_stored[n].sem, h_stored[n].at(b, -1))
                            dve.wait_ge(projected.sem, projected.at(b, n))
                            dve.tensor_tensor(h[:, 2 * n:2 * n + 2, :], psM[:, :].rearrange("p (t c) -> p t c", c=C),
                                              residual[:, bass.ds(b * NT + 2 * n, 2), :],
                                              ALU.add).then_inc(h_ready.sem, 1)
                        elif what == "stats":
                            dve.wait_ge(h_ready.sem, h_ready.at(b, n))
                            dve.sem_inc(idle, 1)
                            for t in (2 * n, 2 * n + 1):
                                dve.bn_stats(stats[:, t, :], h[:, t, :]).then_inc(stats_done.sem, 1)
                            for t in (2 * n, 2 * n + 1):
                                dve.wait_ge(stats_done.sem, stats_done.at(b, t))
                                dve.sem_inc(idle, 1)
                                last = dve.bn_aggr(moments[:, t, :], stats[:, t, :])
                            last.then_inc(moments_ready.sem, 1)
                        elif what == "route":
                            own[0] = 0
                            route(b, settle)
                        elif what == "pick":
                            pick(settle)
                        elif what == "choose":
                            choose(b, settle)
                        elif what == "rank":
                            place(b, settle)
                            assert own[0] == VEC - 1, own[0]

                rounds2(dve, body)

            @block.gpsimd
            def _(pool):
                for s in (w_split, v_copied, m_split, var_ready, rstd_ready, shift_half, shift_ready):
                    pool.sem_inc(s.sem, s.credit)
                pool.wait_ge(v_cleared, 2)

                def body(steps):
                    for what, n, b in steps:
                        if what == "copy_v":
                            pool.wait_ge(values_done.sem, values_done.at(b, 8 * n + 7 - NU))
                            pool.sem_inc(idle, 1)
                            pool.tensor_copy(
                                v_aug[:, :, n * GH:(n + 1) * GH, 0:D],
                                v_all[:, bass.ds(b * NT, NT), n * GH * D:(n + 1) * GH * D]
                                .rearrange("p t (h d) -> p t h d", d=D)).then_inc(v_copied.sem, 1)
                        elif what == "rows":
                            pool.wait_ge(rows_out.sem, rows_out.at(b, n))
                            pool.wait_ge(m_loaded.sem, m_loaded.at(b, n - 1))
                            pool.tensor_tensor(m_rows[:, 1, :], m_raw[:, :], m_rows[:, 0, :],
                                               ALU.subtract).then_inc(m_split.sem, 1)
                        elif what == "weights":
                            low_weights(pool, 0, 0, w1_first, w2_first)
                        elif what == "stats":
                            pool.wait_ge(moments_ready.sem, moments_ready.at(b, n))
                            pool.sem_inc(idle, 1)
                            pool.tensor_scalar(var_eps[:, 2 * n:2 * n + 2], moments[:, 2 * n:2 * n + 2, 1], EPS, None,
                                               ALU.add).then_inc(var_ready.sem, 1)
                            pool.wait_ge(var_ready.sem, var_ready.at(b, n))
                            pool.tensor_tensor(rstd[:, 2 * n:2 * n + 2], var_eps[:, 2 * n:2 * n + 2],
                                               power[:, :].to_broadcast([P, 2]), ALU.pow).then_inc(rstd_ready.sem, 1)
                            pool.wait_ge(rstd_ready.sem, rstd_ready.at(b, n))
                            pool.tensor_tensor(shift[:, 2 * n:2 * n + 2], moments[:, 2 * n:2 * n + 2, 0],
                                               rstd[:, 2 * n:2 * n + 2], ALU.mult).then_inc(shift_half.sem, 1)
                            pool.wait_ge(shift_half.sem, shift_half.at(b, n))
                            pool.sem_inc(idle, 1)
                            pool.tensor_scalar(minus_shift[:, 2 * n:2 * n + 2], shift[:, 2 * n:2 * n + 2], -1.0, None,
                                               ALU.mult).then_inc(shift_ready.sem, 1)
                        elif what == "rank":
                            pool.wait_ge(slot_ready.sem, slot_ready.at(b, 0))
                            pool.sem_inc(idle, 1)
                            for i in range(2):
                                for t in range(NT):
                                    pool.indirect_dma_start(
                                        out=slots[:, :],
                                        out_offset=bass.IndirectOffsetOnAxis(ap=slot_at[:, i, t:t + 1], axis=0),
                                        in_=rows[:, t, :], in_offset=None, bounds_check=E * CAP - 1,
                                        oob_is_err=False).then_inc(scattered, 16)

                rounds2(pool, body)
                pool.wait_ge(scattered, (CLEARS + NB * 2 * NT) * 16)
        tokens.close()

        NP = E // 2
        w1_part = [w1_first, [t[:, :, :] for t in two("w1_part", [P, CH, HID], F32R)]]
        w2_part = [w2_first, [t[:, :, :] for t in two("w2_part", [P, KH, C], F32R)]]
        b2_all = two("b2_all", [P, C], F32)
        taken = two("taken", [P, NS, ROW], F32)
        takenT = [two(f"takenT{i}_", [P, CH, CAP], F32R) for i in range(2)]
        act_raw = two("act_raw", [P, CAP], F32)
        hidden = two("hidden", [P, KH, CAP], F32R)
        given = two("given", [P, NS, C], F32)
        number = sb("number", [P, 1], F32)
        gate_parts = two("gate_parts", [P, NS], F32)
        gate = two("gate", [P, NS], F32)

        number_ready = sem("number_ready")
        b2_loaded = [signal(f"b2_loaded{i}", 1, 16) for i in range(2)]
        taken_loaded = [signal(f"taken_loaded{i}", 1, 16) for i in range(2)]
        t_full, t_high, t_done = signal("t_full", 4), signal("t_high", 4), signal("t_done", 4)
        h_full, h_raw = signal("h_full", 2 * KH), signal("h_raw", 2 * KH)
        h_high, h_low = signal("h_high", 2 * KH), signal("h_low", 2 * KH)
        g_full, g_sum, g_ready = signal("g_full", 2 * NS), signal("g_sum", 2 * NS), signal("g_ready", 2 * NS)
        gate_half, gate_ready = signal("gate_half", 2), signal("gate_ready", 2)
        DISPATCHED = (CLEARS + NB * 2 * NT) * 16
        bank_h = [wide[0][:, 0, :], wide[0][:, 1, :]]
        bank_t = [wide[1][:, 0, :], wide[1][:, 1, :]]

        def added(pair, e):
            return pair * (2 * NS * 16) + (DISPATCHED + (e + 1) * NS * 16)

        def all_experts(engine, prepare, run_expert):
            prepare(0, 0)
            with engine.Fori(0, NP - 1) as pair:
                run_expert(pair, 0, lambda: prepare(pair, 1))
                run_expert(pair, 1, lambda: prepare(pair + 1, 0))
            run_expert(NP - 1, 0, lambda: prepare(NP - 1, 1))
            run_expert(NP - 1, 1, lambda: None)

        with nc.Block() as block:
            @block.sync
            def _(sp):
                for s in (*b2_loaded, *taken_loaded):
                    sp.sem_inc(s.sem, s.credit)

                def next_weights(pair, i):
                    sp.wait_ge(w_split.sem, w_split.at(pair, i - 1))
                    sp.sem_inc(idle, 1)
                    load_weights(sp, pair, i)

                def load_rows(pair, i):
                    sp.wait_ge(scattered, added(pair, i - 2))
                    sp.sem_inc(idle, 1)
                    sp.dma_start(taken[i][:, :, :],
                                 slots.rearrange("(e s p) c -> e p s c", p=P, s=NS)[pair * 2 + i]
                                 ).then_inc(taken_loaded[i].sem, 16)
                    sp.dma_start(b2_all[i][:, :],
                                 b2.rearrange("(e o) n -> e o n", o=1)[pair * 2 + i].to_broadcast([P, C])
                                 ).then_inc(b2_loaded[i].sem, 16)

                load_rows(0, 0)
                with sp.Fori(0, NP - 1) as pair:
                    load_rows(pair, 1)
                    next_weights(pair + 1, 0)
                    load_rows(pair + 1, 0)
                    next_weights(pair + 1, 1)
                load_rows(NP - 1, 1)

            @block.tensor
            def _(pe):
                for s in (t_full, h_full, g_full):
                    pe.sem_inc(s.sem, s.credit)

                def prepare(pair, i):
                    pe.wait_ge(taken_loaded[i].sem, taken_loaded[i].at(pair, 0))
                    for c in range(CH):
                        pe.wait_ge(t_done.sem, t_done.at(pair, 2 * i + c - 2))
                        for s in range(NS):
                            last = pe.transpose(bank_t[c][:, s * P:(s + 1) * P],
                                                taken[i][:, s, c * P:(c + 1) * P], ident[:, :])
                        last.then_inc(t_full.sem, 1)

                def run_expert(pair, i, prepare_next):
                    pe.wait_ge(w_split.sem, w_split.at(pair, i))
                    pe.wait_ge(t_done.sem, t_done.at(pair, 2 * i + 1))

                    def first_product(k):
                        pe.wait_ge(h_raw.sem, h_raw.at(pair, KH * i + k - 2))
                        for c in range(CH):
                            last = split_product(
                                pe, bank_h[k % 2], [w1_part[i][j][:, c, k * P:(k + 1) * P] for j in range(2)],
                                [takenT[i][j][:, c, :] for j in range(2)], start=(c == 0), stop=(c == CH - 1))
                        last.then_inc(h_full.sem, 1)

                    def second_product(k):
                        pe.wait_ge(h_low.sem, h_low.at(pair, KH * i + k))
                        for s in range(NS):
                            if k == 0:
                                pe.wait_ge(g_sum.sem, g_sum.at(pair, NS * i + s - NS))
                            last = split_product(
                                pe, bank[s][:, 0:C], [hidden[j][:, k, s * P:(s + 1) * P] for j in range(2)],
                                [w2_part[i][j][:, k, :] for j in range(2)], start=(k == 0), stop=(k == KH - 1))
                            if k == KH - 1:
                                last.then_inc(g_full.sem, 1)

                    for k in range(KH):
                        first_product(k)
                        if k >= 3:
                            second_product(k - 3)
                    second_product(KH - 3)
                    prepare_next()
                    for k in range(KH - 2, KH):
                        second_product(k)

                all_experts(pe, prepare, run_expert)

            @block.scalar
            def _(act):
                for s in (t_high, h_raw, h_high):
                    act.sem_inc(s.sem, s.credit)

                def prepare(pair, i):
                    act.wait_ge(h_full.sem, h_full.at(pair, KH * (i + 1) - 1 - 2 * KH))
                    for c in range(CH):
                        act.wait_ge(t_full.sem, t_full.at(pair, 2 * i + c))
                        act.activation(takenT[i][0][:, c, :], bank_t[c], ACT.Copy).then_inc(t_high.sem, 1)

                def run_expert(pair, i, prepare_next):
                    for k in range(KH + 1):
                        if k < KH:
                            act.wait_ge(h_full.sem, h_full.at(pair, KH * i + k))
                            act.wait_ge(h_low.sem, h_low.at(pair, KH * i + k - 2))
                            act.activation(act_raw[k % 2][:, :], bank_h[k % 2], ACT.Gelu,
                                           bias=b1T[:, bass.ds(pair * (2 * KH) + (i * KH + k), 1)]
                                           ).then_inc(h_raw.sem, 1)
                        if k:
                            act.wait_ge(h_raw.sem, h_raw.at(pair, KH * i + k - 1))
                            if k == 1:
                                act.wait_ge(g_full.sem, g_full.at(pair, NS * i - 1))
                            act.activation(hidden[0][:, k - 1, :], act_raw[(k - 1) % 2][:, :],
                                           ACT.Copy).then_inc(h_high.sem, 1)
                    prepare_next()

                all_experts(act, prepare, run_expert)

            @block.vector
            def _(dve):
                for s in (t_done, h_low, g_sum, g_ready, gate_half, gate_ready):
                    dve.sem_inc(s.sem, s.credit)
                dve.memset(number[:, :], 0.0).then_inc(number_ready, 1)
                dve.wait_ge(number_ready, 1)

                def rows_and_gates(pair, i):
                    for c in range(CH):
                        dve.wait_ge(t_high.sem, t_high.at(pair, 2 * i + c))
                        dve.tensor_tensor(takenT[i][1][:, c, :], bank_t[c], takenT[i][0][:, c, :],
                                          ALU.subtract).then_inc(t_done.sem, 1)
                    for n, (column, test) in enumerate(((GATE1, ALU.is_equal), (GATE2, ALU.not_equal))):
                        last = dve.scalar_tensor_tensor(out=gate_parts[n][:, :], in0=taken[i][:, :, FIRST],
                                                        scalar=number[:, 0:1], in1=taken[i][:, :, column],
                                                        op0=test, op1=ALU.mult)
                    last.then_inc(gate_half.sem, 1)
                    dve.wait_ge(gate_half.sem, gate_half.at(pair, i))
                    dve.tensor_scalar(number[:, :], number[:, :], 1.0, None, ALU.add)
                    dve.tensor_tensor(gate[i][:, :], gate_parts[0][:, :], gate_parts[1][:, :],
                                      ALU.add).then_inc(gate_ready.sem, 1)

                def low_hidden(pair, i, k):
                    dve.wait_ge(h_high.sem, h_high.at(pair, KH * i + k))
                    dve.tensor_tensor(hidden[1][:, k, :], act_raw[k % 2][:, :], hidden[0][:, k, :],
                                      ALU.subtract).then_inc(h_low.sem, 1)

                def give(pair, i):
                    dve.wait_ge(b2_loaded[i].sem, b2_loaded[i].at(pair, 0))
                    dve.wait_ge(scattered, added(pair, i - 2))
                    dve.wait_ge(gate_ready.sem, gate_ready.at(pair, i))
                    for s in range(NS):
                        dve.wait_ge(g_full.sem, g_full.at(pair, NS * i + s))
                        dve.tensor_tensor(given[i][:, s, :], bank[s][:, 0:C], b2_all[i][:, :],
                                          ALU.add).then_inc(g_sum.sem, 1)
                        dve.wait_ge(g_sum.sem, g_sum.at(pair, NS * i + s))
                        dve.tensor_scalar(given[i][:, s, :], given[i][:, s, :], gate[i][:, s:s + 1], None,
                                          ALU.mult).then_inc(g_ready.sem, 1)

                def run_expert(pair, i, next_pair):
                    for k in range(KH):
                        low_hidden(pair, i, k)
                        if k == 1 and next_pair is not None:
                            dve.wait_ge(g_full.sem, g_full.at(pair, NS * i - 1))
                            high_weights(dve, next_pair, 1 - i, w1_part[1 - i], w2_part[1 - i])
                    if next_pair is not None:
                        rows_and_gates(next_pair, 1 - i)
                    give(pair, i)

                rows_and_gates(0, 0)
                with dve.Fori(0, NP - 1) as pair:
                    run_expert(pair, 0, pair)
                    run_expert(pair, 1, pair + 1)
                run_expert(NP - 1, 0, NP - 1)
                run_expert(NP - 1, 1, None)

            @block.gpsimd
            def _(pool):
                def prepare(pair, i):
                    low_weights(pool, pair, i, w1_part[i], w2_part[i])

                def run_expert(pair, i, prepare_next):
                    prepare_next()
                    for s in range(NS):
                        pool.wait_ge(g_ready.sem, g_ready.at(pair, NS * i + s))
                        pool.sem_inc(idle, 1)
                        if s == 0:
                            pool.wait_ge(scattered, added(pair, i - 1))
                            pool.sem_inc(idle, 1)
                        pool.indirect_dma_start(
                            out=out[:, :],
                            out_offset=bass.IndirectOffsetOnAxis(ap=taken[i][:, s, TOKEN:TOKEN + 1].bitcast(U32),
                                                                 axis=0),
                            in_=given[i][:, s, :], in_offset=None, bounds_check=N + CAP - 1, oob_is_err=True,
                            compute_op=ALU.add).then_inc(scattered, 16)

                with pool.Fori(0, NP - 1) as pair:
                    run_expert(pair, 0, lambda: prepare(pair, 1))
                    run_expert(pair, 1, lambda: prepare(pair + 1, 0))
                run_expert(NP - 1, 0, lambda: prepare(NP - 1, 1))
                run_expert(NP - 1, 1, lambda: None)
                pool.wait_ge(scattered, added(NP - 1, 1))


_INS = ["x", "L0_tok_weight", "L0_tok_weighted_sum", "L0_attn_W_qkv", "L0_attn_b_qkv", "L0_attn_W_proj",
        "L0_attn_b_proj", "L0_ffn_Wr", "L0_ffn_br", "L0_ffn_W1", "L0_ffn_b1", "L0_ffn_W2", "L0_ffn_b2"]


def constants():
    import numpy as np

    f = np.float32
    p, t = np.arange(P)[:, None], np.arange(T)
    later = [(t >= P * (s + 1)) for s in range(NT - 1)]
    inside = [(t // P == s) for s in range(NT - 1)]
    q_rows = [w * (P * (s + 1) - t) for s, w in enumerate(later)] + [w * 1 for w in later] + [0 * t, 0 * t]
    k_rows = [w * 1 for w in inside] + [w * (t - P * (s + 1)) for s, w in enumerate(inside)] + [0 * t - 1, 0 * t - 1]
    column = np.arange(2 * T - P)[None, :] - (T - P)
    heads = 8 * np.arange(2)[None, :] + p // D
    return {
        "identity": np.eye(P, dtype=f),
        "earlier": (p < np.arange(P)[None, :]).astype(f),
        "relative": (np.minimum(column - p, 0) * ((column >= 0) & (column < P))).astype(f),
        "relative_block": np.minimum(p - np.arange(P)[None, :], 0).astype(f),
        "stack_rows": np.stack([np.array(q_rows), np.array(k_rows)], 1).astype(f),
        "q_scale": (D**-0.5 / np.array(slopes(), f)[heads]).astype(f),
        "expert_numbers": np.arange(E, dtype=f),
        "token_numbers": (p + P * np.arange(NT)[None, :]).astype(f),
        "empty_numbers": (N + p + P * np.arange(NS)[None, :]).astype(f),
    }


def kernel(**inputs):
    import concourse.bacc as _bacc
    import numpy as _np
    from concourse.bass_utils import run_bass_kernel_spmd as _run

    nc = _bacc.Bacc("TRN2", target_bir_lowering=False, num_devices=1)
    arrays, args = {}, []
    for name, a in [*((k, inputs[k]) for k in _INS), *constants().items()]:
        a = _np.ascontiguousarray(a)
        arrays[f"in_{name}_dram"] = a
        args.append(nc.dram_tensor(f"in_{name}_dram", a.shape, mybir.dt.from_np(a.dtype), kind="ExternalInput").ap())
    args.append(nc.dram_tensor("out_0_dram", (N + CAP, C), F32, kind="ExternalOutput").ap())
    tower(nc, *args)
    r = _run(nc, [arrays], core_ids=[0])
    return _np.asarray(r.results[0]["out_0_dram"])[:N].reshape(NB, T, C)
```

```python
import math
from contextlib import ExitStack

import concourse.bass as bass
from concourse import mybir

F32 = mybir.dt.float32
F32R = mybir.dt.float32r
BF16 = mybir.dt.bfloat16
U32 = mybir.dt.uint32
ALU = mybir.AluOpType
ACT = mybir.ActivationFunctionType
AX = mybir.AxisListType

P = 128
NB, T, C = 4, 512, 256
XD = 4
NT = T // P
CH = C // P
H, D = 16, 16
NG, GH = 4, 4
N = NB * T
E, CAP, HID = 8, 512, 1024
KH = HID // P
NS = CAP // P
ROW = C + 4
TOKEN, FIRST, GATE1, GATE2 = C, C + 1, C + 2, C + 3
EPS = 1e-5
LOWEST = -3.0e38

SPLIT = 4 * D
ALIBI = 2 * (NT - 1)
MROW = P - 2
Q_PARTS, K_PARTS = (0, 1, 0, 1), (0, 0, 1, 1)
NA = NG * NT * GH
NU = NG * 2 * GH
LEAD = 26
MIDDLE = 16


def slopes():
    start = 2.0 ** (-(2.0 ** -(math.log2(H) - 3)))
    return [start * start**i for i in range(H)]


class Signal:

    def __init__(self, semaphore, per, by=1):
        self.sem, self.per, self.by = semaphore, per, by
        self.credit = per * by

    def at(self, batch, event):
        assert -self.per <= event < self.per
        return batch * self.credit + (self.credit + self.by * (event + 1))


def embedding_steps(first, last):
    order = ["turn_x 0 new", "turn_ln 1 old", "turn_x 1 new", "embed 0 new", "qk 0 old", "turn_x 2 new",
             "embed 1 new", "norm 0 new", "qk 1 old", "store 0 old", "turn_x 3 new", "qk 2 old", "store 1 old",
             "embed 2 new", "norm 1 new", "qk 3 old", "store 2 old", "value 0 old", "norm 2 new", "embed 3 new",
             "store 3 old", "value 1 old", "turn_ln 0 new", "norm 3 new"]
    tiles = {"turn_ln": range(0, 2), "qk 0": range(2, 4), "qk 1": range(4, 6), "qk 2": range(6, 8),
             "qk 3": range(8, 10), "value 0": range(10, 13), "value 1": range(13, 16)}
    steps = []
    for step in order:
        what, n, batch = step.split()
        if last and batch == "old":
            steps += [("max", tile, 0) for tile in tiles.get(what, tiles.get(f"{what} {n}", ()))]
        if not (first if batch == "old" else last):
            steps.append((what, int(n), int(batch == "new")))
    return steps


def attention_steps(batch, start, end, first, last):
    steps = []
    after = {5: ("turn_y", 0), 6: ("turn_y", 1), 7: ("project", 0), 8: ("project", 1), 13: ("route", 0),
             15: ("rank", 0)}
    before = {8: ("stats", 0), 9: ("stats", 1), 10: ("norm", 0)}
    between = {10: ("norm", 1), 11: ("turn_rows", 0), 12: ("turn_rows", 1), 14: ("pick", 0), 15: ("gates", 0)}
    ahead = {16: ("load", 0), 17: ("copy_v", 0), 21: ("load", 1), 22: ("copy_v", 1), 25: ("load", 2),
             28: ("copy_v", 2)}
    own = {0: ("load", 3), 6: ("copy_v", 3)}
    for u in range(start, end):
        if u in ahead and not last:
            steps.append((*ahead[u], batch + 1))
        if u in own and not first:
            steps.append((*own[u], batch))
        g, whose = (u // 8 - 1, batch) if u >= 8 else (u // 8 - 1 + NG, batch - 1)
        begun = u >= 8 or not first
        if u % 8 == 4 and begun:
            steps.append(("heads_out", g, whose))
        maxima = [("max", a, batch) if a < NA else ("max", a - NA, batch + 1)
                  for a in (LEAD + 2 * u, LEAD + 2 * u + 1) if a < NA or not last]
        if u in before and not first:
            steps.append((*before[u], batch - 1))
        steps += maxima[:1]
        if u in between and not first:
            steps.append((*between[u], batch - 1))
        steps += [("scores", u, batch)] + maxima[1:]
        if u % 8 == 3:
            if u // 8 + 1 < NG:
                steps.append(("rows", u // 8 + 1, batch))
            elif not last:
                steps.append(("rows", 0, batch + 1))
        if u % 2 and u > 4:
            steps.append(("values", (u - 5) // 2, batch))
        elif u % 2 and not first:
            steps.append(("values", (u - 5) // 2 + 4 * NG, batch - 1))
        if u % 8 == 4 and begun:
            steps.append(("heads", g, whose))
        if u in after and not first:
            steps.append((*after[u], batch - 1))
        if u == 14 and not first:
            steps.append(("choose", 0, batch - 1))
    return steps


def attention_begin():
    steps = [("copy_v", 0, 0), ("rows", 0, 0)] + [("max", a, 0) for a in range(16, LEAD)]
    steps += [("copy_v", g, 0) for g in range(1, NG)]
    return steps + attention_steps(0, 0, MIDDLE, first=True, last=False)


def attention_round(batch):
    return (attention_steps(batch, MIDDLE, NU, first=False, last=False)
            + attention_steps(batch + 1, 0, MIDDLE, first=False, last=False))


def attention_end():
    last = NB - 1
    return (attention_steps(last, MIDDLE, NU, first=False, last=True) + [("weights", 0, 0)]
            + [("values", 4 * NG - 2, last), ("values", 4 * NG - 1, last), ("heads_out", NG - 1, last),
               ("heads", NG - 1, last),
               ("turn_y", 0, last), ("turn_y", 1, last), ("project", 0, last), ("stats", 0, last),
               ("project", 1, last), ("stats", 1, last), ("weights", 1, 0), ("norm", 0, last), ("norm", 1, last),
               ("turn_rows", 0, last), ("turn_rows", 1, last), ("route", 0, last), ("pick", 0, last),
               ("choose", 0, last), ("gates", 0, last), ("rank", 0, last)])


def split_product(pe, out, left, right, start, stop):
    pe.matmul(out, left[0], right[0], start=start, stop=False)
    pe.matmul(out, left[0], right[1], start=False, stop=False)
    return pe.matmul(out, left[1], right[0], start=False, stop=stop)


def tower(nc, x, tok_weight, tok_sum, w_qkv, b_qkv, w_proj, b_proj, w_router, b_router, w1, b1, w2, b2,
          identity, earlier, relative, relative_block, stack_rows, q_scale, expert_numbers, token_numbers,
          empty_numbers, out):
    slope = slopes()
    x_tiles = x.rearrange("b (t p) i d -> (b t) p (i d)", p=P)
    out_tiles = out.rearrange("(n p) c -> n p c", p=P)

    with ExitStack() as whole:
        def sb(name, shape, dt, scope=whole):
            return scope.enter_context(nc.sbuf_tensor(name, shape, dt))

        def two(name, shape, dt, scope=whole):
            return [sb(f"{name}{i}", shape, dt, scope) for i in range(2)]

        def sem(name):
            return whole.enter_context(nc.semaphore(name))

        def signal(name, per, by=1):
            return Signal(sem(name), per, by)

        slots = nc.dram_tensor("slots", [E * CAP, ROW], F32, kind="Internal").ap()
        parts = nc.dram_tensor("parts", [NB, 2, 2, H * D, T], F32, kind="Internal").ap()

        bank = [whole.enter_context(nc.psum_tensor(f"bank{i}", [P, 512], F32)) for i in range(8)]

        idle = sem("idle")
        scattered = sem("scattered")

        ident = sb("ident", [P, P], F32)
        b1T = sb("b1T", [P, E * KH], F32)
        x_tiles_in = sb("x_tiles_in", [P, 2, C * XD], F32)
        h_and_ln = sb("h_and_ln", [P, 2, NT, C], F32)
        w1_raw = x_tiles_in.rearrange("p i n -> p (i n)").rearrange("p (c n) -> p c n", c=CH)
        w2_raw = h_and_ln.rearrange("p i t c -> p (i t) c")
        q_stack = sb("q_stack", [P, NG, GH, T], F32R)
        quarter = q_stack.rearrange("p g h t -> p g (h t)")
        w1_first = [quarter[:, i, :].rearrange("p (c n) -> p c n", c=CH) for i in range(2)]
        w2_first = [quarter[:, 2 + i, :].rearrange("p (k n) -> p k n", n=C) for i in range(2)]
        tokens = whole.enter_context(ExitStack())

        def tk(name, shape, dt):
            return sb(name, shape, dt, tokens)

        masked = [tk(f"masked{i}", [P, T], BF16) for i in range(3)]
        top_score = [tk(f"top_score{i}", [P, NT, GH], F32) for i in range(2)]
        empty = tk("empty", [P, NS, ROW], F32)
        wproj = tk("wproj", [P, CH, C], F32)
        wr = tk("wr", [P, CH, E], F32)
        br_all = tk("br_all", [P, E], F32)
        before = tk("before", [P, P], BF16)
        ones = tk("ones", [P, P], BF16)
        ident16 = tk("ident16", [P, P], BF16)
        rel = tk("rel", [P, 2 * T - P], F32)
        rel_block = tk("rel_block", [P, P], BF16)
        numbers = tk("numbers", [P, E], F32)
        token_id = tk("token_id", [P, NT], F32)
        power = tk("power", [P, 1], F32)
        run = tk("run", [P, E], BF16)
        k_stack = tk("k_stack", [P, NG, GH, T], F32R)
        residual = tk("residual", [P, NB * NT, C], F32)
        v_all = tk("v_all", [P, NB * NT, C], F32)
        rows_placed = sem("rows_placed")
        cleared = [sem("q_cleared"), sem("k_cleared")]
        stack_loaded = [signal(f"stack_loaded{g}", 1, 16 * 8) for g in range(NG)]
        s_full, s_done = signal("s_full", NA), signal("s_done", NA)
        psS = bank[0:3]
        w_loaded = signal("w_loaded", 2, 32)
        w_high, w_split = signal("w_high", 2), signal("w_split", 2)

        def load_stacks(sp, b, g):
            for which, stack, order in ((0, q_stack, Q_PARTS), (1, k_stack, K_PARTS)):
                for i, part in enumerate(order):
                    src = parts[b, which, part, g * GH * D:(g + 1) * GH * D, :]
                    sp.dma_start(stack[i * D:(i + 1) * D, g, :, :].bitcast(F32),
                                 src.rearrange("(h d) t -> d h t", d=D)).then_inc(stack_loaded[g].sem, 16)

        def max_products(pe, b, n, k, since):
            g, t, hd = n // 16, n % 16 // GH, n % GH
            if n % 16 == 0:
                pe.wait_ge(stack_loaded[g].sem, stack_loaded[g].at(b, 0))
            pe.wait_ge(s_done.sem, s_done.at(b, n - since))
            pe.matmul(psS[k % 3][:, :], q_stack[0:MROW, g, hd, t * P:(t + 1) * P],
                      k_stack[0:MROW, g, hd, :], start=True, stop=True).then_inc(s_full.sem, 1)

        def max_of_tile(dve, b, n, k):
            g, t, hd = n // 16, n % 16 // GH, n % GH
            dve.wait_ge(s_full.sem, s_full.at(b, n))
            dve.sem_inc(idle, 1)
            first = T - P - t * P
            dve.tensor_tensor_reduce(masked[k % 3][:, :], psS[k % 3][:, :], rel[:, first:first + T],
                                     1.0, LOWEST, ALU.add, ALU.max,
                                     top_score[g % 2][:, t, hd:hd + 1]).then_inc(s_done.sem, 1)

        def load_weights(sp, pair, i):
            sp.dma_start(w1_raw, w1.rearrange("e (c p) n -> e p c n", p=P)[pair * 2 + i]
                         ).then_inc(w_loaded.sem, 16)
            sp.dma_start(w2_raw, w2.rearrange("e (k p) n -> e p k n", p=P)[pair * 2 + i]
                         ).then_inc(w_loaded.sem, 16)

        def high_weights(dve, pair, i, w1_part, w2_part):
            dve.wait_ge(w_loaded.sem, w_loaded.at(pair, i))
            dve.tensor_copy(w1_part[0], w1_raw)
            dve.tensor_copy(w2_part[0], w2_raw).then_inc(w_high.sem, 1)

        def low_weights_1(pool, pair, i, w1_part):
            pool.wait_ge(w_high.sem, w_high.at(pair, i))
            pool.tensor_tensor(w1_part[1], w1_raw, w1_part[0], ALU.subtract)

        def low_weights_2(pool, w2_part):
            pool.tensor_tensor(w2_part[1], w2_raw, w2_part[0], ALU.subtract).then_inc(w_split.sem, 1)

        with ExitStack() as embedding:
            def em(name, shape, dt):
                return sb(name, shape, dt, embedding)

            ws = em("ws", [P, CH, C], F32)
            b1_rows = em("b1_rows", [E * KH, P], F32)
            before32 = em("before32", [P, P], F32)
            rel_block32 = em("rel_block32", [P, P], F32)
            rows32 = em("rows32", [8, 2, T], F32)
            empty_id = em("empty_id", [P, NS], F32)
            wtok = two("wtok", [P, XD, CH, C], F32R, embedding)
            wqkv32 = em("wqkv32", [P, CH, 3 * C], F32)
            wqkv = two("wqkv", [P, CH, 3 * C], F32R, embedding)
            bv_all = em("bv_all", [P, C], F32)
            bp_all = em("bp_all", [P, C], F32)
            bqk = em("bqk", [P, 4], F32)
            qscale = em("qscale", [P, 2], F32)
            bq_scaled = em("bq_scaled", [P, 2], F32)
            x_tile = [x_tiles_in[:, i, :] for i in range(2)]
            xT = [two(f"xT{i}_", [P, XD * CH, P], F32R, embedding) for i in range(2)]
            h, ln = h_and_ln[:, 0, :, :], h_and_ln[:, 1, :, :]
            stats = em("stats", [P, NT, 6], F32)
            moments = em("moments", [P, NT, 2], F32)
            var_eps = em("var_eps", [P, NT], F32)
            rstd = em("rstd", [P, NT], F32)
            wd = ln.rearrange("p n c -> p (n c)").rearrange("p (c d) -> p c d", d=XD)
            lnT = two("lnT", [P, CH, T], F32R, embedding)
            qk_raw = em("qk_raw", [P, 2, T], F32)
            wtok32 = [qk_raw[:, i, :].rearrange("p (c n) -> p c n", c=CH) for i in range(2)]
            wtok32 += [h[:, i * CH:(i + 1) * CH, :] for i in range(2)]
            qk_part = two("qk_part", [P, 2, T], F32R, embedding)

            first_loaded = sem("first_loaded")
            later_loaded = sem("later_loaded")
            bp_loaded = sem("bp_loaded")
            empty_ready = sem("empty_ready")
            slots_cleared = sem("slots_cleared")
            turned = sem("turned")
            w_product, w_high_part = sem("w_product"), sem("w_high_part")
            bias_ready = sem("bias_ready")
            wtok_ready = sem("wtok_ready")
            wqkv_ready = sem("wqkv_ready")
            x_loaded = [signal(f"x_loaded{i}", NT // 2, 16) for i in range(2)]
            xt_full = signal("xt_full", 2 * NT)
            xt_high = signal("xt_high", 2 * NT)
            xt_done = signal("xt_done", 2 * NT)
            em_full = signal("em_full", NT)
            em_done = signal("em_done", NT)
            stats_done = signal("stats_done", NT)
            moments_ready = signal("moments_ready", NT)
            var_ready = signal("var_ready", NT)
            rstd_ready = signal("rstd_ready", NT)
            ln_ready = signal("ln_ready", NT)
            residual_ready = signal("residual_ready", NT)
            lt_full = signal("lt_full", 2)
            lt_high = signal("lt_high", 2)
            lt_done = signal("lt_done", 2)
            qk_full = signal("qk_full", 4)
            qk_done = signal("qk_done", 4)
            low_ready = signal("low_ready", 4)
            part_stored = [signal(f"part_stored{i}", 2, 32) for i in range(2)]
            v_full = signal("v_full", NT // 2)
            v_done = signal("v_done", NT // 2)
            bank_x, bank_e, bank_q, bank_l, bank_v = bank[0:2], bank[2:4], bank[4:6], bank[6], bank[7]

            first_loads = [
                (ws[:, :, :], tok_sum.rearrange("(h p) i -> p h i", p=P)),
                (ident[:, :], identity),
                (empty_id[:, :], empty_numbers),
                (wd[:, :, :], tok_weight.partition_broadcast(P)),
            ]
            later_loads = [
                (bqk[:, :], b_qkv[0:2 * C].rearrange("(j p) -> p j", p=P)),
                (qscale[:, :], q_scale),
                (bv_all[:, :], b_qkv[2 * C:3 * C].partition_broadcast(P)),
                (wqkv32[:, :, :], w_qkv.rearrange("(h p) n -> p h n", p=P)),
                (b1_rows[:, :], b1.rearrange("e (k p) -> (e k) p", p=P)),
                (before32[:, :], earlier),
                (rel_block32[:, :], relative_block),
                (rel[:, :], relative),
                (rows32[:, :, :], stack_rows),
                (wproj[:, :, :], w_proj.rearrange("(h p) n -> p h n", p=P)),
                (wr[:, :, :], w_router.rearrange("(h p) n -> p h n", p=P)),
                (br_all[:, :], b_router.partition_broadcast(P)),
                (numbers[:, :], expert_numbers.partition_broadcast(P)),
                (token_id[:, :], token_numbers),
            ]

            def rounds(engine, body, then=lambda: None):
                body(-1, embedding_steps(first=True, last=False))
                then()
                with engine.Fori(0, NB - 1) as b:
                    body(b, embedding_steps(first=False, last=False))
                body(NB - 1, embedding_steps(first=False, last=True))

            with nc.Block() as block:
                @block.sync
                def _(sp):
                    for dst, src in first_loads:
                        sp.dma_start(dst, src).then_inc(first_loaded, 16)
                    for s in [*x_loaded, *stack_loaded]:
                        sp.sem_inc(s.sem, s.credit)

                    def constant_rows():
                        sp.wait_ge(later_loaded, 16 * len(later_loads))
                        for half, stack in ((0, q_stack), (1, k_stack)):
                            sp.wait_ge(cleared[half], 1)
                            sp.dma_start(stack[SPLIT:SPLIT + ALIBI, :, :, :].rearrange("p g h t -> p (g h) t")
                                         .bitcast(F32),
                                         rows32[0:ALIBI, half, :].unsqueeze(1).to_broadcast([ALIBI, H, T])
                                         ).then_inc(rows_placed, 16)
                            sp.dma_start(stack[MROW:P, :, :, :].rearrange("p g h t -> p (g h) t").bitcast(F32),
                                         rows32[ALIBI:ALIBI + 2, half, :].unsqueeze(1).to_broadcast([2, H, T])
                                         ).then_inc(rows_placed, 16)

                    def body(b, steps):
                        for what, n, new in steps:
                            if what == "turn_x":
                                sp.wait_ge(xt_full.sem, xt_full.at(b + new, 2 * n - 3))
                                sp.dma_start(x_tile[n % 2], x_tiles[(b + new) * NT + n]
                                             ).then_inc(x_loaded[n % 2].sem, 16)
                                if isinstance(b, int) and n == 1:
                                    with nc.allow_non_contiguous_dma("biases by partition"):
                                        for dst, src in later_loads:
                                            sp.dma_start(dst, src).then_inc(later_loaded, 16)
                            elif what == "embed" and n % 2:
                                sp.wait_ge(empty_ready, 2)
                                sp.dma_start(
                                    slots.rearrange("(k e s p) c -> e k p s c", k=2, p=P, s=NS)[b + new, n // 2],
                                    empty[:, :, :]).then_inc(slots_cleared, 16)

                    rounds(sp, body, constant_rows)
                    sp.wait_ge(slots_cleared, E * 16)
                    for stored in part_stored:
                        sp.wait_ge(stored.sem, stored.at(0, 1))
                    for g in range(NG):
                        load_stacks(sp, 0, g)

                @block.gpsimd
                def _(pool):
                    for s in (var_ready, rstd_ready, residual_ready, low_ready):
                        pool.sem_inc(s.sem, s.credit)
                    pool.wait_ge(bp_loaded, 16)
                    pool.memset(q_stack[SPLIT:P, :, :, :].bitcast(F32), 0.0).then_inc(cleared[0], 1)
                    pool.wait_ge(cleared[0], 1)
                    pool.memset(k_stack[SPLIT:P, :, :, :].bitcast(F32), 0.0).then_inc(cleared[1], 1)
                    pool.wait_ge(empty_ready, 2)
                    pool.dma_start(out[N:N + CAP, :].rearrange("(s p) c -> p s c", p=P),
                                   empty[:, :, 0:C]).then_inc(scattered, 16)
                    pool.wait_ge(cleared[1], 1)

                    def low_qkv():
                        pool.wait_ge(wqkv_ready, 1)
                        pool.tensor_tensor(wqkv[1][:, :, :], wqkv32[:, :, :], wqkv[0][:, :, :],
                                           ALU.subtract).then_inc(wqkv_ready, 1)

                    def body(b, steps):
                        for what, n, new in steps:
                            if what == "embed":
                                e = b + new
                                pool.wait_ge(moments_ready.sem, moments_ready.at(e, n))
                                pool.sem_inc(idle, 1)
                                pool.tensor_scalar(var_eps[:, n:n + 1], moments[:, n, 1:2], EPS, None,
                                                   ALU.add).then_inc(var_ready.sem, 1)
                                pool.wait_ge(var_ready.sem, var_ready.at(e, n))
                                pool.tensor_tensor(rstd[:, n:n + 1], var_eps[:, n:n + 1], power[:, :],
                                                   ALU.pow).then_inc(rstd_ready.sem, 1)
                                pool.wait_ge(em_done.sem, em_done.at(e, n))
                                pool.tensor_tensor(residual[:, bass.ds(e * NT + n, 1), :].rearrange("p o c -> p (o c)"),
                                                   h[:, n, :], bp_all[:, :], ALU.add).then_inc(residual_ready.sem, 1)
                            elif what == "qk":
                                pool.wait_ge(qk_done.sem, qk_done.at(b, n))
                                pool.wait_ge(part_stored[n % 2].sem, part_stored[n % 2].at(b, n // 2 - 1))
                                pool.tensor_tensor(qk_part[1][:, n % 2, :], qk_raw[:, n % 2, :],
                                                   qk_part[0][:, n % 2, :], ALU.subtract).then_inc(low_ready.sem, 1)

                    rounds(pool, body, low_qkv)

                @block.tensor
                def _(pe):
                    for s in (xt_full, em_full, lt_full, qk_full, v_full, s_full):
                        pe.sem_inc(s.sem, s.credit)
                    pe.wait_ge(first_loaded, 16 * len(first_loads))
                    for ih in range(CH):
                        for oh in range(CH):
                            at = ih * C + oh * P
                            last = pe.transpose(bank[2][:, at:at + P], ws[:, oh, ih * P:(ih + 1) * P], ident[:, :])
                    last.then_inc(turned, 1)

                    def body(b, steps):
                        for what, n, new in steps:
                            e = b + new
                            if what == "turn_x":
                                pe.wait_ge(x_loaded[n % 2].sem, x_loaded[n % 2].at(e, n // 2))
                                xv = x_tile[n % 2].rearrange("p (i d) -> p i d", d=XD)
                                for half in range(2):
                                    pe.wait_ge(xt_done.sem, xt_done.at(e, 2 * n + half - 2))
                                    for k in range(4 * half, 4 * half + 4):
                                        d, ih = k // CH, k % CH
                                        last = pe.transpose(bank_x[half][:, (k % 4) * P:(k % 4 + 1) * P],
                                                            xv[:, ih * P:(ih + 1) * P, d], ident[:, :])
                                    last.then_inc(xt_full.sem, 1)
                            elif what == "embed":
                                if isinstance(e, int) and (e, n) == (0, 0):
                                    pe.wait_ge(wtok_ready, 1)
                                pe.wait_ge(xt_done.sem, xt_done.at(e, 2 * n + 1))
                                pe.wait_ge(em_done.sem, em_done.at(e, n - 2))
                                for k in range(XD * CH):
                                    last = split_product(
                                        pe, bank_e[n % 2][:, 0:C], [xT[n % 2][i][:, k, :] for i in range(2)],
                                        [wtok[i][:, k // CH, k % CH, :] for i in range(2)],
                                        start=(k == 0), stop=(k == XD * CH - 1))
                                last.then_inc(em_full.sem, 1)
                            elif what == "turn_ln":
                                pe.wait_ge(lt_done.sem, lt_done.at(e, n - 1))
                                for t in (2 * n, 2 * n + 1):
                                    pe.wait_ge(ln_ready.sem, ln_ready.at(e, t))
                                    for c in range(CH):
                                        at = c * 2 * P + (t % 2) * P
                                        last = pe.transpose(bank_l[:, at:at + P], ln[:, t, c * P:(c + 1) * P],
                                                            ident[:, :])
                                last.then_inc(lt_full.sem, 1)
                            elif what == "qk":
                                pe.wait_ge(wqkv_ready, 2)
                                pe.wait_ge(lt_done.sem, lt_done.at(b, 1))
                                pe.wait_ge(qk_done.sem, qk_done.at(b, n - 2))
                                for c in range(CH):
                                    last = split_product(
                                        pe, bank_q[n % 2][:, :], [wqkv[i][:, c, n * P:(n + 1) * P] for i in range(2)],
                                        [lnT[i][:, c, :] for i in range(2)], start=(c == 0), stop=(c == CH - 1))
                                last.then_inc(qk_full.sem, 1)
                            elif what == "max":
                                if n == 0:
                                    pe.wait_ge(xt_done.sem, xt_done.at(NB - 1, 2 * NT - 1))
                                    pe.wait_ge(em_done.sem, em_done.at(NB - 1, NT - 1))
                                    pe.wait_ge(rows_placed, 4 * 16)
                                max_products(pe, 0, n, n, 3)
                            elif what == "value":
                                pe.wait_ge(v_done.sem, v_done.at(b, n - 1))
                                for t in (2 * n, 2 * n + 1):
                                    for c in range(CH):
                                        last = split_product(
                                            pe, bank_v[:, (t % 2) * C:(t % 2 + 1) * C],
                                            [lnT[i][:, c, t * P:(t + 1) * P] for i in range(2)],
                                            [wqkv[i][:, c, 2 * C:3 * C] for i in range(2)],
                                            start=(c == 0), stop=(c == CH - 1))
                                last.then_inc(v_full.sem, 1)

                    rounds(pe, body)
                    pe.wait_ge(v_done.sem, v_done.at(NB - 1, 1))
                    pe.wait_ge(later_loaded, 16 * len(later_loads))
                    pe.transpose(bank_v[:, 0:E * KH], b1_rows[:, :],
                                 ident[0:E * KH, 0:E * KH]).then_inc(turned, 1)

                @block.scalar
                def _(act):
                    for s in (xt_high, lt_high, qk_done, *part_stored):
                        act.sem_inc(s.sem, s.credit)
                    act.dma_start(bp_all[:, :], b_proj.partition_broadcast(P)).then_inc(bp_loaded, 16)
                    for d in range(XD):
                        act.wait_ge(w_product, d + 1)
                        act.activation(wtok[0][:, d, :, :], wtok32[d], ACT.Copy).then_inc(w_high_part, 1)

                    def body(b, steps):
                        for what, n, new in steps:
                            e = b + new
                            if what == "turn_x":
                                act.wait_ge(em_full.sem, em_full.at(e, n - 2))
                                for half in range(2):
                                    act.wait_ge(xt_full.sem, xt_full.at(e, 2 * n + half))
                                    act.activation(xT[n % 2][0][:, 4 * half:4 * half + 4, :],
                                                   bank_x[half][:, :].rearrange("p (k n) -> p k n", n=P),
                                                   ACT.Copy).then_inc(xt_high.sem, 1)
                            elif what == "turn_ln":
                                act.wait_ge(v_full.sem, v_full.at(e, -1))
                                act.wait_ge(lt_full.sem, lt_full.at(e, n))
                                act.activation(lnT[0][:, :, 2 * n * P:2 * (n + 1) * P],
                                               bank_l.rearrange("p (c n) -> p c n", c=CH),
                                               ACT.Copy).then_inc(lt_high.sem, 1)
                            elif what == "qk":
                                act.wait_ge(qk_full.sem, qk_full.at(b, n))
                                act.wait_ge(part_stored[n % 2].sem, part_stored[n % 2].at(b, n // 2 - 1))
                                scale = qscale[:, n:n + 1] if n < 2 else 1.0
                                bias = bq_scaled[:, n:n + 1] if n < 2 else bqk[:, n:n + 1]
                                act.activation(qk_part[0][:, n % 2, :], bank_q[n % 2][:, :], ACT.Identity, bias=bias,
                                               scale=scale)
                                act.activation(qk_raw[:, n % 2, :], bank_q[n % 2][:, :], ACT.Identity, bias=bias,
                                               scale=scale).then_inc(qk_done.sem, 1)

                            elif what == "store":
                                act.wait_ge(low_ready.sem, low_ready.at(b, n))
                                act.sem_inc(idle, 1)
                                for part in range(2):
                                    dst = parts[b, n // 2, part, (n % 2) * P:(n % 2 + 1) * P, :]
                                    act.dma_start(dst, qk_part[part][:, n % 2, :].bitcast(F32)
                                                  ).then_inc(part_stored[n % 2].sem, 16)

                    rounds(act, body)
                    for i in range(2):
                        act.wait_ge(part_stored[i].sem, part_stored[i].at(NB - 1, 1))
                    act.wait_ge(rows_placed, 4 * 16)

                @block.vector
                def _(dve):
                    for s in (xt_done, em_done, stats_done, moments_ready, ln_ready, lt_done, v_done, s_done):
                        dve.sem_inc(s.sem, s.credit)
                    dve.memset(empty[:, :, :], 0.0).then_inc(empty_ready, 1)
                    dve.memset(ones[:, :], 1.0)
                    dve.memset(run[:, :], 0.0)
                    dve.memset(power[:, :], -0.5)
                    dve.wait_ge(first_loaded, 16 * len(first_loads))
                    dve.wait_ge(empty_ready, 1)
                    dve.tensor_copy(empty[:, :, :].bitcast(U32)[:, :, TOKEN], empty_id[:, :]).then_inc(empty_ready, 1)
                    dve.wait_ge(turned, 1)
                    sums = bank[2][:, :].rearrange("p (i o) -> p i o", i=CH)
                    for d in range(XD):
                        by = wd[:, :, d].unsqueeze(1).to_broadcast([P, CH, C])
                        dve.tensor_tensor(wtok32[d], sums, by, ALU.mult).then_inc(w_product, 1)
                    for d in range(XD):
                        dve.wait_ge(w_high_part, d + 1)
                        last = dve.tensor_tensor(wtok[1][:, d, :, :], wtok32[d], wtok[0][:, d, :, :], ALU.subtract)
                    last.then_inc(wtok_ready, 1)

                    def high_qkv():
                        dve.wait_ge(later_loaded, 16 * len(later_loads))
                        dve.tensor_copy(wqkv[0][:, :, :], wqkv32[:, :, :]).then_inc(wqkv_ready, 1)
                        dve.tensor_tensor(bq_scaled[:, :], bqk[:, 0:2], qscale[:, :], ALU.mult).then_inc(bias_ready, 1)
                    def body(b, steps):
                        for what, n, new in steps:
                            e = b + new
                            if what == "turn_x":
                                for half in range(2):
                                    dve.wait_ge(xt_high.sem, xt_high.at(e, 2 * n + half))
                                    dve.tensor_tensor(xT[n % 2][1][:, 4 * half:4 * half + 4, :],
                                                      bank_x[half][:, :].rearrange("p (k n) -> p k n", n=P),
                                                      xT[n % 2][0][:, 4 * half:4 * half + 4, :],
                                                      ALU.subtract).then_inc(xt_done.sem, 1)
                            elif what == "embed":
                                dve.wait_ge(em_full.sem, em_full.at(e, n))
                                dve.sem_inc(idle, 1)
                                dve.bn_stats(stats[:, n, :], bank_e[n % 2][:, 0:C]).then_inc(stats_done.sem, 1)
                                dve.wait_ge(stats_done.sem, stats_done.at(e, n))
                                dve.sem_inc(idle, 1)
                                dve.bn_aggr(moments[:, n, :], stats[:, n, :]).then_inc(moments_ready.sem, 1)
                                dve.wait_ge(residual_ready.sem, residual_ready.at(e, n - NT))
                                dve.sem_inc(idle, 1)
                                dve.tensor_copy(h[:, n, :], bank_e[n % 2][:, 0:C]).then_inc(em_done.sem, 1)
                            elif what == "norm":
                                dve.wait_ge(em_done.sem, em_done.at(e, n))
                                dve.wait_ge(lt_full.sem, lt_full.at(e, n // 2 - 2))
                                dve.wait_ge(rstd_ready.sem, rstd_ready.at(e, n))
                                dve.tensor_scalar(ln[:, n, :], h[:, n, :], moments[:, n, 0:1], rstd[:, n:n + 1],
                                                  ALU.subtract, ALU.mult).then_inc(ln_ready.sem, 1)
                            elif what == "turn_ln":
                                dve.wait_ge(lt_high.sem, lt_high.at(e, n))
                                dve.tensor_tensor(lnT[1][:, :, 2 * n * P:2 * (n + 1) * P],
                                                  bank_l.rearrange("p (c n) -> p c n", c=CH),
                                                  lnT[0][:, :, 2 * n * P:2 * (n + 1) * P],
                                                  ALU.subtract).then_inc(lt_done.sem, 1)
                            elif what == "max":
                                max_of_tile(dve, 0, n, n)
                            elif what == "value":
                                dve.wait_ge(v_full.sem, v_full.at(b, n))
                                dve.tensor_tensor(v_all[:, bass.ds(b * NT + 2 * n, 2), :],
                                                  bank_v.rearrange("p (t c) -> p t c", c=C),
                                                  bv_all[:, :].unsqueeze(1).to_broadcast([P, 2, C]),
                                                  ALU.add).then_inc(v_done.sem, 1)

                    rounds(dve, body, high_qkv)
                    dve.tensor_copy(before[:, :], before32[:, :])
                    dve.tensor_copy(ident16[:, :], ident[:, :])
                    dve.tensor_copy(rel_block[:, :], rel_block32[:, :])
                    dve.wait_ge(turned, 2)
                    dve.tensor_copy(b1T[:, :], bank_v[:, 0:E * KH])

        v_aug = tk("v_aug", [P, NT, H, 2 * D], F32)
        m_raw = tk("m_raw", [GH, T], F32)
        m_rows = tk("m_rows", [GH, 2, T], F32R)
        probs = [tk(f"probs{i}", [P, GH, 2, T], F32) for i in range(2)]
        heads_t = tk("heads_t", [P, T], F32)
        denom = tk("denom", [P, NT, GH], F32)
        y = tk("y", [P, NT, C], F32)
        yT = tk("yT", [P, CH, T], F32)
        stats = tk("stats2", [P, NT, 6], F32)
        moments = tk("moments2", [P, NT, 2], F32)
        var_eps = tk("var_eps2", [P, NT], F32)
        rstd = tk("rstd2", [P, NT], F32)
        shift = tk("shift", [P, NT], F32)
        minus_shift = tk("minus_shift", [P, NT], F32)
        h = tk("h2", [P, NT, C], F32)
        rows = tk("rows", [P, NT, ROW], F32)
        rowsT = tk("rowsT", [P, CH, T], F32)
        logits = tk("logits", [P, NT, E], F32)
        top8 = tk("top8", [P, NT, 8], F32)
        top_at = tk("top_at", [P, NT, 8], U32)
        top_expert = tk("top_expert", [P, NT, 8], F32)
        hot = [tk(f"hot{i}", [P, NT, E], F32) for i in range(2)]
        sel = tk("sel", [P, NT, E], BF16)
        sel_sum = tk("sel_sum", [P, E], F32)
        gap = tk("gap", [P, NT], F32)
        gap_exp = tk("gap_exp", [P, NT], F32)
        gap_sum = tk("gap_sum", [P, NT], F32)
        picked = [tk(f"picked{i}", [P, NT, E], F32) for i in range(2)]
        rank = tk("rank", [P, 2, NT], F32)
        dropped = tk("dropped", [P, 2, NT], F32)
        slot = tk("slot", [P, 2, NT], F32)
        slot_at = tk("slot_at", [P, 2, NT], U32)

        v_cleared = sem("v_cleared")
        v_copied = signal("v_copied", NG)
        p_full, p_done = signal("p_full", 2 * NU), signal("p_done", 2 * NU)
        rows_turned = signal("rows_turned", NG)
        rows_out = signal("rows_out", NG)
        m_split = signal("m_split", NG)
        m_loaded = signal("m_loaded", NG, 16 * GH)
        values_done = signal("values_done", 4 * NG)
        heads_out = signal("heads_out", NG)
        heads_turned = signal("heads_turned", NG)
        denom_ready = signal("denom_ready", NG)
        y_ready = signal("y_ready", NG)
        y_turned, y_out = signal("y_turned", CH), signal("y_out", CH)
        projected = signal("projected", 2)
        h_ready = signal("h_ready", 2)
        h_stored = [signal(f"h_stored{i}", 1, 16) for i in range(2)]
        moments_ready = signal("moments_ready2", 2)
        var_ready, rstd_ready = signal("var_ready2", 2), signal("rstd_ready2", 2)
        shift_half, shift_ready = signal("shift_half", 2), signal("shift_ready", 2)
        row_ready = signal("row_ready", NT)
        stats_done = signal("stats_done2", NT)
        r_turned, r_out = signal("r_turned", CH), signal("r_out", CH)
        routed, logits_ready = signal("routed", 1), signal("logits_ready", 1)
        VEC = 11
        vec = signal("vec", VEC)
        sel_ready = signal("sel_ready", 1)
        gap_ready, gap_done = signal("gap_ready", 1), signal("gap_done", 1)
        ranked, ranks_out = signal("ranked", 1), signal("ranks_out", 1)
        slot_ready = signal("slot_ready", 1)
        psO, psP, psM = bank[3], bank[4:7], bank[7]

        def side_bank(b, n):
            return psP[0] if isinstance(b, int) and b == NB - 1 and n == 1 else psM

        def numbered(steps):
            counts = {}
            for what, n, b in steps:
                yield what, n, b, counts.get(what, 0)
                counts[what] = counts.get(what, 0) + 1

        def since(k):
            return min(k + 1, 3)

        def rounds2(engine, body):
            body(attention_begin())
            with engine.Fori(0, NB - 1) as b:
                body(attention_round(b))
            body(attention_end())

        with nc.Block() as block:
            @block.sync
            def _(sp):
                for s in [m_loaded, *h_stored, w_loaded]:
                    sp.sem_inc(s.sem, s.credit)
                load_weights(sp, 0, 0)

                def body(steps):
                    for what, n, b, _ in numbered(steps):
                        if what == "load":
                            sp.wait_ge(p_full.sem, p_full.at(b, 16 * n + 15 - 2 * NU))
                            sp.sem_inc(idle, 1)
                            load_stacks(sp, b, n)
                        elif what == "rows":
                            sp.wait_ge(m_split.sem, m_split.at(b, n))
                            for hd in range(GH):
                                sp.dma_start(q_stack[MROW:MROW + 2, n, hd, :].bitcast(F32),
                                             m_rows[hd:hd + 1, :, :].bitcast(F32)).then_inc(m_loaded.sem, 16)
                        elif what == "project":
                            sp.wait_ge(h_ready.sem, h_ready.at(b, n))
                            sp.sem_inc(idle, 1)
                            sp.dma_start(out_tiles[bass.ds(b * NT + 2 * n, 2)].rearrange("n p c -> p n c"),
                                         h[:, 2 * n:2 * n + 2, :]).then_inc(h_stored[n].sem, 16)

                rounds2(sp, body)
                sp.wait_ge(w_split.sem, w_split.at(0, 0))
                load_weights(sp, 0, 1)
                for stored in h_stored:
                    sp.wait_ge(stored.sem, stored.at(NB - 1, 0))

            @block.tensor
            def _(pe):
                for s in (p_full, rows_turned, values_done, heads_turned, y_turned, projected, r_turned,
                          routed, ranked):
                    pe.sem_inc(s.sem, s.credit)
                last_use = {False: (ranks_out, 0, -1), True: (p_done, NB - 1, 2 * NU - 1)}

                def psM_after(done, b, event, beside=False):
                    signal_, batch_, event_ = last_use[beside]
                    pe.wait_ge(signal_.sem, signal_.at(batch_, event_))
                    last_use[beside] = (done, b, event)

                def body(steps):
                    for what, n, b, k in numbered(steps):
                        if what == "max":
                            max_products(pe, b, n, k, since(k))
                        elif what == "rows":
                            pe.wait_ge(s_done.sem, s_done.at(b, 16 * n + 15))
                            psM_after(rows_out, b, n)
                            for t in range(NT):
                                last = pe.transpose(psM[0:GH, t * P:(t + 1) * P], top_score[n % 2][:, t, :],
                                                    ident[:, :])
                            last.then_inc(rows_turned.sem, 1)
                        elif what == "scores":
                            g, half, hd = n // 8, n % 8 // GH, n % GH
                            if n % 8 == 0:
                                pe.wait_ge(m_loaded.sem, m_loaded.at(b, g))
                            for i in range(2):
                                s, out_bank = 2 * half + i, psP[(2 * k + i) % 3]
                                pe.wait_ge(p_done.sem, p_done.at(b, 2 * n + i - since(2 * k + i)))
                                pe.matmul(out_bank[:, s * P:(s + 1) * P], ident16[:, :], rel_block[:, :],
                                          start=True, stop=True)
                            for i in range(2):
                                s, out_bank = 2 * half + i, psP[(2 * k + i) % 3]
                                pe.matmul(out_bank[:, :], k_stack[:, g, hd, s * P:(s + 1) * P],
                                          q_stack[:, g, hd, :], start=False, stop=True,
                                          skip_group_check=True).then_inc(p_full.sem, 1)
                        elif what == "values":
                            g, half, s, i = n // 4, n // 2, n % 4, n % 2
                            pe.wait_ge(p_done.sem, p_done.at(b, 8 * half + 7))
                            if s == 0:
                                pe.wait_ge(v_copied.sem, v_copied.at(b, g))
                                pe.wait_ge(heads_out.sem, heads_out.at(b, g - 1))
                            for hd in range(GH):
                                last = pe.matmul(psO[32 * hd:32 * hd + 32, :], v_aug[:, s, g * GH + hd, :],
                                                 probs[half % 2][:, hd, i, :], start=(s == 0), stop=(s == NT - 1),
                                                 tile_position=(0, 32 * hd))
                            last.then_inc(values_done.sem, 1)
                        elif what == "heads":
                            pe.wait_ge(heads_out.sem, heads_out.at(b, n))
                            psM_after(y_ready, b, n)
                            for t in range(NT):
                                last = pe.transpose(psM[:, t * P:(t + 1) * P], heads_t[:, t * P:(t + 1) * P],
                                                    ident[:, :])
                            last.then_inc(heads_turned.sem, 1)
                        elif what == "turn_y":
                            pe.wait_ge(y_ready.sem, y_ready.at(b, NG - 1))
                            psM_after(y_out, b, n, side_bank(b, n) is not psM)
                            for t in range(NT):
                                last = pe.transpose(side_bank(b, n)[:, t * P:(t + 1) * P], y[:, t, n * P:(n + 1) * P],
                                                    ident[:, :])
                            last.then_inc(y_turned.sem, 1)
                        elif what == "project":
                            pe.wait_ge(y_out.sem, y_out.at(b, CH - 1))
                            psM_after(h_ready, b, n, side_bank(b, n) is not psM)
                            for t in (2 * n, 2 * n + 1):
                                for c in range(CH):
                                    last = pe.matmul(side_bank(b, n)[:, (t % 2) * C:(t % 2 + 1) * C],
                                                     yT[:, c, t * P:(t + 1) * P], wproj[:, c, :],
                                                     start=(c == 0), stop=(c == CH - 1))
                            last.then_inc(projected.sem, 1)
                        elif what == "turn_rows":
                            psM_after(r_out, b, n, side_bank(b, n) is not psM)
                            for t in range(NT):
                                if n == 0:
                                    pe.wait_ge(row_ready.sem, row_ready.at(b, t))
                                last = pe.transpose(side_bank(b, n)[:, t * P:(t + 1) * P],
                                                    rows[:, t, n * P:(n + 1) * P], ident[:, :])
                            last.then_inc(r_turned.sem, 1)
                        elif what == "route":
                            pe.wait_ge(r_out.sem, r_out.at(b, CH - 1))
                            psM_after(logits_ready, b, 0)
                            for t in range(NT):
                                for c in range(CH):
                                    last = pe.matmul(psM[:, t * E:(t + 1) * E], rowsT[:, c, t * P:(t + 1) * P],
                                                     wr[:, c, :], start=(c == 0), stop=(c == CH - 1))
                            last.then_inc(routed.sem, 1)
                        elif what == "rank":
                            pe.wait_ge(sel_ready.sem, sel_ready.at(b, 0))
                            psM_after(ranks_out, b, 0)
                            for t in range(NT):
                                o = psM[:, t * E:(t + 1) * E]
                                pe.matmul(o, before[:, :], sel[:, t, :], start=True, stop=False)
                                for t0 in range(t):
                                    pe.matmul(o, ones[:, :], sel[:, t0, :], start=False, stop=False)
                                last = pe.matmul(o, ones[:, :], run[:, :], start=False, stop=True)
                            last.then_inc(ranked.sem, 1)

                rounds2(pe, body)

            @block.scalar
            def _(act):
                for s in (p_done, rows_out, heads_out, y_out, row_ready, r_out, gap_done):
                    act.sem_inc(s.sem, s.credit)

                def body(steps):
                    for what, n, b, k in numbered(steps):
                        if what == "rows":
                            act.wait_ge(rows_turned.sem, rows_turned.at(b, n))
                            act.wait_ge(m_loaded.sem, m_loaded.at(b, n - 1))
                            act.activation(m_rows[:, 0, :], psM[0:GH, :], ACT.Copy)
                            act.activation(m_raw[:, :], psM[0:GH, :], ACT.Copy).then_inc(rows_out.sem, 1)
                        elif what == "scores":
                            g, half, hd = n // 8, n % 8 // GH, n % GH
                            if hd == 0:
                                act.wait_ge(values_done.sem, values_done.at(b, 2 * (n // GH) - 3))
                            for i in range(2):
                                act.wait_ge(p_full.sem, p_full.at(b, 2 * n + i))
                                act.activation(probs[n // GH % 2][:, hd, i, :], psP[(2 * k + i) % 3][:, :], ACT.Exp,
                                               scale=slope[g * GH + hd]).then_inc(p_done.sem, 1)
                        elif what == "heads_out":
                            act.wait_ge(values_done.sem, values_done.at(b, 4 * n + 3))
                            act.wait_ge(heads_turned.sem, heads_turned.at(b, n - 1))
                            act.activation(heads_t[:, :], psO[:, :], ACT.Copy).then_inc(heads_out.sem, 1)
                        elif what == "turn_y":
                            act.wait_ge(y_turned.sem, y_turned.at(b, n))
                            act.activation(yT[:, n, :], side_bank(b, n)[:, :], ACT.Copy).then_inc(y_out.sem, 1)
                        elif what == "norm":
                            if n == 0:
                                act.wait_ge(scattered, b * (2 * NT * 16) + 16)
                            act.wait_ge(shift_ready.sem, shift_ready.at(b, n))
                            for t in (2 * n, 2 * n + 1):
                                act.activation(rows[:, t, 0:C], h[:, t, :], ACT.Identity, bias=minus_shift[:, t:t + 1],
                                               scale=rstd[:, t:t + 1]).then_inc(row_ready.sem, 1)
                        elif what == "turn_rows":
                            act.wait_ge(r_turned.sem, r_turned.at(b, n))
                            act.activation(rowsT[:, n, :], side_bank(b, n)[:, :], ACT.Copy).then_inc(r_out.sem, 1)
                        elif what == "choose":
                            act.wait_ge(gap_ready.sem, gap_ready.at(b, 0))
                            act.activation(gap_exp[:, :], gap[:, :], ACT.Exp).then_inc(gap_done.sem, 1)

                rounds2(act, body)

            @block.vector
            def _(dve):
                for s in (w_high, denom_ready, y_ready, h_ready, moments_ready, logits_ready, vec, sel_ready,
                          gap_ready, ranks_out, slot_ready, stats_done):
                    dve.sem_inc(s.sem, s.credit)
                dve.memset(v_aug[:, :, :, D:2 * D], 0.0).then_inc(v_cleared, 1)
                dve.wait_ge(v_cleared, 1)
                dve.memset(v_aug[:, :, :, D:D + 1], 1.0).then_inc(v_cleared, 1)

                def route(b, settle):
                    dve.wait_ge(routed.sem, routed.at(b, 0))
                    dve.tensor_tensor(logits[:, :, :], psM[:, 0:NT * E].rearrange("p (t e) -> p t e", e=E),
                                      br_all[:, :].unsqueeze(1).to_broadcast([P, NT, E]),
                                      ALU.add).then_inc(logits_ready.sem, 1)
                    dve.wait_ge(logits_ready.sem, logits_ready.at(b, 0))
                    dve.sem_inc(idle, 1)
                    for t in range(NT):
                        last = dve.max(top8[:, t, :], logits[:, t, :])
                    settle(last)

                def pick(settle):
                    dve.sem_inc(idle, 1)
                    for t in range(NT):
                        last = dve.max_index(top_at[:, t, :], top8[:, t, :], logits[:, t, :])
                    settle(last)
                    settle(dve.tensor_copy(top_expert[:, :, :], top_at[:, :, :]))

                def choose(b, settle):
                    for i in range(2):
                        last = dve.tensor_tensor(hot[i][:, :, :], numbers[:, :].unsqueeze(1).to_broadcast([P, NT, E]),
                                                 top_expert[:, :, i:i + 1].to_broadcast([P, NT, E]), ALU.is_equal)
                    settle(last)
                    dve.tensor_tensor(sel[:, :, :], hot[0][:, :, :], hot[1][:, :, :],
                                      ALU.add).then_inc(sel_ready.sem, 1)
                    dve.tensor_tensor(gap[:, :], top8[:, :, 1], top8[:, :, 0], ALU.subtract).then_inc(gap_ready.sem, 1)
                    dve.tensor_copy(rows[:, :, FIRST], top_expert[:, :, 0])
                    settle(dve.tensor_copy(rows[:, :, :].bitcast(U32)[:, :, TOKEN], token_id[:, :]))
                    dve.tensor_scalar(token_id[:, :], token_id[:, :], float(T), None, ALU.add)

                def gates(b, settle):
                    dve.wait_ge(gap_done.sem, gap_done.at(b, 0))
                    settle(dve.tensor_scalar(gap_sum[:, :], gap_exp[:, :], 1.0, None, ALU.add))
                    settle(dve.reciprocal(rows[:, :, GATE1], gap_sum[:, :]))
                    dve.tensor_tensor(rows[:, :, GATE2], rows[:, :, GATE1], gap_exp[:, :], ALU.mult)

                def place(b, settle):
                    dve.wait_ge(ranked.sem, ranked.at(b, 0))
                    ranks = psM[:, 0:NT * E].rearrange("p (t e) -> p t e", e=E)
                    dve.tensor_tensor(picked[0][:, :, :], ranks, hot[0][:, :, :], ALU.mult)
                    dve.tensor_tensor(picked[1][:, :, :], ranks, hot[1][:, :, :], ALU.mult).then_inc(ranks_out.sem, 1)
                    dve.wait_ge(ranks_out.sem, ranks_out.at(b, 0))
                    for i in range(2):
                        last = dve.tensor_reduce(rank[:, i, :], picked[i][:, :, :], AX.X, ALU.add)
                    settle(last)
                    dve.tensor_scalar(dropped[:, :, :], rank[:, :, :], float(CAP), float(2 * E * CAP),
                                      ALU.is_ge, ALU.mult)
                    settle(dve.scalar_tensor_tensor(
                        out=slot[:, :, :], in0=top_expert[:, :, 0:2].rearrange("p t i -> p i t"), scalar=float(CAP),
                        in1=rank[:, :, :], op0=ALU.mult, op1=ALU.add))
                    dve.tensor_tensor(slot_at[:, :, :], slot[:, :, :], dropped[:, :, :],
                                      ALU.add).then_inc(slot_ready.sem, 1)
                    settle(dve.tensor_reduce(sel_sum[:, :], sel[:, :, :].rearrange("p t e -> p e t"), AX.X, ALU.add))
                    dve.tensor_tensor(run[:, :], run[:, :], sel_sum[:, :], ALU.add).then_inc(vec.sem, 1)

                def body(steps):
                    own = [0]
                    for what, n, b, k in numbered(steps):
                        def settle(instruction):
                            instruction.then_inc(vec.sem, 1)
                            dve.wait_ge(vec.sem, vec.at(b, own[0]))
                            own[0] += 1

                        if what == "max":
                            if n % 16 == 0:
                                dve.wait_ge(rows_turned.sem, rows_turned.at(b, n // 16 - 2))
                                dve.sem_inc(idle, 1)
                            max_of_tile(dve, b, n, k)
                        elif what == "weights" and n == 0:
                            dve.wait_ge(p_full.sem, p_full.at(NB - 1, 2 * NU - 1))
                            high_weights(dve, 0, 0, w1_first, w2_first)
                        elif what == "heads":
                            dve.wait_ge(heads_turned.sem, heads_turned.at(b, n))
                            o = psM[:, :].rearrange("p (t h d) -> p t h d", t=NT, h=GH)
                            dve.reciprocal(denom[:, :, :], o[:, :, :, D]).then_inc(denom_ready.sem, 1)
                            dve.wait_ge(denom_ready.sem, denom_ready.at(b, n))
                            if n == 0:
                                dve.wait_ge(y_turned.sem, y_turned.at(b, -1))
                            dve.tensor_tensor(
                                y[:, :, n * GH * D:(n + 1) * GH * D].rearrange("p t (h d) -> p t h d", d=D),
                                o[:, :, :, 0:D], denom[:, :, :].unsqueeze(3).to_broadcast([P, NT, GH, D]),
                                ALU.mult).then_inc(y_ready.sem, 1)
                        elif what == "project":
                            dve.wait_ge(h_stored[n].sem, h_stored[n].at(b, -1))
                            dve.wait_ge(projected.sem, projected.at(b, n))
                            dve.tensor_tensor(h[:, 2 * n:2 * n + 2, :],
                                              side_bank(b, n)[:, :].rearrange("p (t c) -> p t c", c=C),
                                              residual[:, bass.ds(b * NT + 2 * n, 2), :],
                                              ALU.add).then_inc(h_ready.sem, 1)
                        elif what == "stats":
                            dve.wait_ge(h_ready.sem, h_ready.at(b, n))
                            dve.sem_inc(idle, 1)
                            for t in (2 * n, 2 * n + 1):
                                dve.bn_stats(stats[:, t, :], h[:, t, :]).then_inc(stats_done.sem, 1)
                            for t in (2 * n, 2 * n + 1):
                                dve.wait_ge(stats_done.sem, stats_done.at(b, t))
                                dve.sem_inc(idle, 1)
                                last = dve.bn_aggr(moments[:, t, :], stats[:, t, :])
                            last.then_inc(moments_ready.sem, 1)
                        elif what == "route":
                            own[0] = 0
                            route(b, settle)
                        elif what == "pick":
                            pick(settle)
                        elif what == "choose":
                            choose(b, settle)
                        elif what == "gates":
                            gates(b, settle)
                        elif what == "rank":
                            place(b, settle)
                            assert own[0] == VEC - 1, own[0]

                rounds2(dve, body)

            @block.gpsimd
            def _(pool):
                for s in (w_split, v_copied, m_split, var_ready, rstd_ready, shift_half, shift_ready):
                    pool.sem_inc(s.sem, s.credit)
                pool.wait_ge(v_cleared, 2)

                def body(steps):
                    for what, n, b, _ in numbered(steps):
                        if what == "copy_v":
                            pool.wait_ge(values_done.sem, values_done.at(b, 4 * n + 3 - 4 * NG))
                            pool.sem_inc(idle, 1)
                            pool.tensor_copy(
                                v_aug[:, :, n * GH:(n + 1) * GH, 0:D],
                                v_all[:, bass.ds(b * NT, NT), n * GH * D:(n + 1) * GH * D]
                                .rearrange("p t (h d) -> p t h d", d=D)).then_inc(v_copied.sem, 1)
                        elif what == "rows":
                            pool.wait_ge(rows_out.sem, rows_out.at(b, n))
                            pool.wait_ge(m_loaded.sem, m_loaded.at(b, n - 1))
                            pool.tensor_tensor(m_rows[:, 1, :], m_raw[:, :], m_rows[:, 0, :],
                                               ALU.subtract).then_inc(m_split.sem, 1)
                        elif what == "weights":
                            if n == 0:
                                low_weights_1(pool, 0, 0, w1_first)
                            else:
                                low_weights_2(pool, w2_first)
                        elif what == "stats":
                            pool.wait_ge(moments_ready.sem, moments_ready.at(b, n))
                            pool.sem_inc(idle, 1)
                            pool.tensor_scalar(var_eps[:, 2 * n:2 * n + 2], moments[:, 2 * n:2 * n + 2, 1], EPS, None,
                                               ALU.add).then_inc(var_ready.sem, 1)
                            pool.wait_ge(var_ready.sem, var_ready.at(b, n))
                            pool.tensor_tensor(rstd[:, 2 * n:2 * n + 2], var_eps[:, 2 * n:2 * n + 2],
                                               power[:, :].to_broadcast([P, 2]), ALU.pow).then_inc(rstd_ready.sem, 1)
                            pool.wait_ge(rstd_ready.sem, rstd_ready.at(b, n))
                            pool.tensor_tensor(shift[:, 2 * n:2 * n + 2], moments[:, 2 * n:2 * n + 2, 0],
                                               rstd[:, 2 * n:2 * n + 2], ALU.mult).then_inc(shift_half.sem, 1)
                            pool.wait_ge(shift_half.sem, shift_half.at(b, n))
                            pool.sem_inc(idle, 1)
                            pool.tensor_scalar(minus_shift[:, 2 * n:2 * n + 2], shift[:, 2 * n:2 * n + 2], -1.0, None,
                                               ALU.mult).then_inc(shift_ready.sem, 1)
                        elif what == "rank":
                            pool.wait_ge(slot_ready.sem, slot_ready.at(b, 0))
                            pool.sem_inc(idle, 1)
                            for i in range(2):
                                for t in range(NT):
                                    pool.indirect_dma_start(
                                        out=slots[:, :],
                                        out_offset=bass.IndirectOffsetOnAxis(ap=slot_at[:, i, t:t + 1], axis=0),
                                        in_=rows[:, t, :], in_offset=None, bounds_check=E * CAP - 1,
                                        oob_is_err=False).then_inc(scattered, 16)

                rounds2(pool, body)
                pool.wait_ge(scattered, (1 + NB * 2 * NT) * 16)
        tokens.close()

        NP = E // 2
        w1_part = [w1_first, [t[:, :, :] for t in two("w1_part", [P, CH, HID], F32R)]]
        w2_part = [w2_first, [t[:, :, :] for t in two("w2_part", [P, KH, C], F32R)]]
        b2_all = two("b2_all", [P, C], F32)
        taken = two("taken", [P, NS, ROW], F32)
        takenT = [two(f"takenT{i}_", [P, CH, CAP], F32R) for i in range(2)]
        act_raw = two("act_raw", [P, CAP], F32)
        hidden = two("hidden", [P, KH, CAP], F32R)
        given = two("given", [P, NS, C], F32)
        number = sb("number", [P, 1], F32)
        gate_parts = two("gate_parts", [P, NS], F32)
        gate = two("gate", [P, NS], F32)

        number_ready = sem("number_ready")
        b2_loaded = [signal(f"b2_loaded{i}", 1, 16) for i in range(2)]
        taken_loaded = [signal(f"taken_loaded{i}", 1, 16) for i in range(2)]
        t_full, t_high, t_done = signal("t_full", 4), signal("t_high", 4), signal("t_done", 4)
        h_full, h_raw = signal("h_full", 2 * KH), signal("h_raw", 2 * KH)
        h_high, h_low = signal("h_high", 2 * KH), signal("h_low", 2 * KH)
        g_full, g_sum, g_ready = signal("g_full", 2 * NS), signal("g_sum", 2 * NS), signal("g_ready", 2 * NS)
        gate_half, gate_ready = signal("gate_half", 2), signal("gate_ready", 2)
        DISPATCHED = (1 + NB * 2 * NT) * 16
        bank_h = [bank[4][:, :], bank[5][:, :]]
        bank_t = [bank[6][:, :], bank[7][:, :]]

        def added(pair, e):
            return pair * (2 * NS * 16) + (DISPATCHED + (e + 1) * NS * 16)

        def all_experts(engine, prepare, run_expert):
            prepare(0, 0)
            with engine.Fori(0, NP - 1) as pair:
                run_expert(pair, 0, lambda: prepare(pair, 1))
                run_expert(pair, 1, lambda: prepare(pair + 1, 0))
            run_expert(NP - 1, 0, lambda: prepare(NP - 1, 1))
            run_expert(NP - 1, 1, lambda: None)

        with nc.Block() as block:
            @block.sync
            def _(sp):
                for s in (*b2_loaded, *taken_loaded):
                    sp.sem_inc(s.sem, s.credit)

                def next_weights(pair, i):
                    sp.wait_ge(w_split.sem, w_split.at(pair, i - 1))
                    sp.sem_inc(idle, 1)
                    load_weights(sp, pair, i)

                def load_rows(pair, i):
                    sp.wait_ge(scattered, added(pair, i - 2))
                    sp.sem_inc(idle, 1)
                    sp.dma_start(taken[i][:, :, :],
                                 slots.rearrange("(e s p) c -> e p s c", p=P, s=NS)[pair * 2 + i]
                                 ).then_inc(taken_loaded[i].sem, 16)
                    sp.dma_start(b2_all[i][:, :],
                                 b2.rearrange("(e o) n -> e o n", o=1)[pair * 2 + i].to_broadcast([P, C])
                                 ).then_inc(b2_loaded[i].sem, 16)

                load_rows(0, 0)
                with sp.Fori(0, NP - 1) as pair:
                    load_rows(pair, 1)
                    next_weights(pair + 1, 0)
                    load_rows(pair + 1, 0)
                    next_weights(pair + 1, 1)
                load_rows(NP - 1, 1)

            @block.tensor
            def _(pe):
                for s in (t_full, h_full, g_full):
                    pe.sem_inc(s.sem, s.credit)

                def prepare(pair, i):
                    pe.wait_ge(taken_loaded[i].sem, taken_loaded[i].at(pair, 0))
                    for c in range(CH):
                        pe.wait_ge(t_done.sem, t_done.at(pair, 2 * i + c - 2))
                        for s in range(NS):
                            last = pe.transpose(bank_t[c][:, s * P:(s + 1) * P],
                                                taken[i][:, s, c * P:(c + 1) * P], ident[:, :])
                        last.then_inc(t_full.sem, 1)

                def run_expert(pair, i, prepare_next):
                    pe.wait_ge(w_split.sem, w_split.at(pair, i))
                    pe.wait_ge(t_done.sem, t_done.at(pair, 2 * i + 1))

                    def first_product(k):
                        pe.wait_ge(h_raw.sem, h_raw.at(pair, KH * i + k - 2))
                        for c in range(CH):
                            last = split_product(
                                pe, bank_h[k % 2], [w1_part[i][j][:, c, k * P:(k + 1) * P] for j in range(2)],
                                [takenT[i][j][:, c, :] for j in range(2)], start=(c == 0), stop=(c == CH - 1))
                        last.then_inc(h_full.sem, 1)

                    def second_product(k):
                        pe.wait_ge(h_low.sem, h_low.at(pair, KH * i + k))
                        for s in range(NS):
                            if k == 0:
                                pe.wait_ge(g_sum.sem, g_sum.at(pair, NS * i + s - NS))
                            last = split_product(
                                pe, bank[s][:, 0:C], [hidden[j][:, k, s * P:(s + 1) * P] for j in range(2)],
                                [w2_part[i][j][:, k, :] for j in range(2)], start=(k == 0), stop=(k == KH - 1))
                            if k == KH - 1:
                                last.then_inc(g_full.sem, 1)

                    for k in range(KH):
                        first_product(k)
                        if k >= 3:
                            second_product(k - 3)
                    second_product(KH - 3)
                    prepare_next()
                    for k in range(KH - 2, KH):
                        second_product(k)

                all_experts(pe, prepare, run_expert)

            @block.scalar
            def _(act):
                for s in (t_high, h_raw, h_high):
                    act.sem_inc(s.sem, s.credit)

                def prepare(pair, i):
                    act.wait_ge(h_full.sem, h_full.at(pair, KH * (i + 1) - 1 - 2 * KH))
                    for c in range(CH):
                        act.wait_ge(t_full.sem, t_full.at(pair, 2 * i + c))
                        act.activation(takenT[i][0][:, c, :], bank_t[c], ACT.Copy).then_inc(t_high.sem, 1)

                def run_expert(pair, i, prepare_next):
                    for k in range(KH + 1):
                        if k < KH:
                            act.wait_ge(h_full.sem, h_full.at(pair, KH * i + k))
                            act.wait_ge(h_low.sem, h_low.at(pair, KH * i + k - 2))
                            act.activation(act_raw[k % 2][:, :], bank_h[k % 2], ACT.Gelu,
                                           bias=b1T[:, bass.ds(pair * (2 * KH) + (i * KH + k), 1)]
                                           ).then_inc(h_raw.sem, 1)
                        if k:
                            act.wait_ge(h_raw.sem, h_raw.at(pair, KH * i + k - 1))
                            if k == 1:
                                act.wait_ge(g_full.sem, g_full.at(pair, NS * i - 1))
                            act.activation(hidden[0][:, k - 1, :], act_raw[(k - 1) % 2][:, :],
                                           ACT.Copy).then_inc(h_high.sem, 1)
                    prepare_next()

                all_experts(act, prepare, run_expert)

            @block.vector
            def _(dve):
                for s in (t_done, h_low, g_sum, g_ready, gate_half, gate_ready):
                    dve.sem_inc(s.sem, s.credit)
                dve.memset(number[:, :], 0.0).then_inc(number_ready, 1)
                dve.wait_ge(number_ready, 1)

                def rows_and_gates(pair, i):
                    for c in range(CH):
                        dve.wait_ge(t_high.sem, t_high.at(pair, 2 * i + c))
                        dve.tensor_tensor(takenT[i][1][:, c, :], bank_t[c], takenT[i][0][:, c, :],
                                          ALU.subtract).then_inc(t_done.sem, 1)
                    for n, (column, test) in enumerate(((GATE1, ALU.is_equal), (GATE2, ALU.not_equal))):
                        last = dve.scalar_tensor_tensor(out=gate_parts[n][:, :], in0=taken[i][:, :, FIRST],
                                                        scalar=number[:, 0:1], in1=taken[i][:, :, column],
                                                        op0=test, op1=ALU.mult)
                    last.then_inc(gate_half.sem, 1)
                    dve.wait_ge(gate_half.sem, gate_half.at(pair, i))
                    dve.tensor_scalar(number[:, :], number[:, :], 1.0, None, ALU.add)
                    dve.tensor_tensor(gate[i][:, :], gate_parts[0][:, :], gate_parts[1][:, :],
                                      ALU.add).then_inc(gate_ready.sem, 1)

                def low_hidden(pair, i, k):
                    dve.wait_ge(h_high.sem, h_high.at(pair, KH * i + k))
                    dve.tensor_tensor(hidden[1][:, k, :], act_raw[k % 2][:, :], hidden[0][:, k, :],
                                      ALU.subtract).then_inc(h_low.sem, 1)

                def give(pair, i):
                    dve.wait_ge(b2_loaded[i].sem, b2_loaded[i].at(pair, 0))
                    dve.wait_ge(scattered, added(pair, i - 2))
                    dve.wait_ge(gate_ready.sem, gate_ready.at(pair, i))
                    for s in range(NS):
                        dve.wait_ge(g_full.sem, g_full.at(pair, NS * i + s))
                        dve.tensor_tensor(given[i][:, s, :], bank[s][:, 0:C], b2_all[i][:, :],
                                          ALU.add).then_inc(g_sum.sem, 1)
                        dve.wait_ge(g_sum.sem, g_sum.at(pair, NS * i + s))
                        dve.tensor_scalar(given[i][:, s, :], given[i][:, s, :], gate[i][:, s:s + 1], None,
                                          ALU.mult).then_inc(g_ready.sem, 1)

                def run_expert(pair, i, next_pair):
                    for k in range(KH):
                        low_hidden(pair, i, k)
                        if k == 1 and next_pair is not None:
                            dve.wait_ge(g_full.sem, g_full.at(pair, NS * i - 1))
                            high_weights(dve, next_pair, 1 - i, w1_part[1 - i], w2_part[1 - i])
                    if next_pair is not None:
                        rows_and_gates(next_pair, 1 - i)
                    give(pair, i)

                rows_and_gates(0, 0)
                with dve.Fori(0, NP - 1) as pair:
                    run_expert(pair, 0, pair)
                    run_expert(pair, 1, pair + 1)
                run_expert(NP - 1, 0, NP - 1)
                run_expert(NP - 1, 1, None)

            @block.gpsimd
            def _(pool):
                def prepare(pair, i):
                    low_weights_1(pool, pair, i, w1_part[i])
                    low_weights_2(pool, w2_part[i])

                def run_expert(pair, i, prepare_next):
                    prepare_next()
                    for s in range(NS):
                        pool.wait_ge(g_ready.sem, g_ready.at(pair, NS * i + s))
                        pool.sem_inc(idle, 1)
                        if s == 0:
                            pool.wait_ge(scattered, added(pair, i - 1))
                            pool.sem_inc(idle, 1)
                        pool.indirect_dma_start(
                            out=out[:, :],
                            out_offset=bass.IndirectOffsetOnAxis(ap=taken[i][:, s, TOKEN:TOKEN + 1].bitcast(U32),
                                                                 axis=0),
                            in_=given[i][:, s, :], in_offset=None, bounds_check=N + CAP - 1, oob_is_err=True,
                            compute_op=ALU.add).then_inc(scattered, 16)

                with pool.Fori(0, NP - 1) as pair:
                    run_expert(pair, 0, lambda: prepare(pair, 1))
                    run_expert(pair, 1, lambda: prepare(pair + 1, 0))
                run_expert(NP - 1, 0, lambda: prepare(NP - 1, 1))
                run_expert(NP - 1, 1, lambda: None)
                pool.wait_ge(scattered, added(NP - 1, 1))


_INS = ["x", "L0_tok_weight", "L0_tok_weighted_sum", "L0_attn_W_qkv", "L0_attn_b_qkv", "L0_attn_W_proj",
        "L0_attn_b_proj", "L0_ffn_Wr", "L0_ffn_br", "L0_ffn_W1", "L0_ffn_b1", "L0_ffn_W2", "L0_ffn_b2"]


def constants():
    import numpy as np

    f = np.float32
    p, t = np.arange(P)[:, None], np.arange(T)
    later = [(t >= P * (s + 1)) for s in range(NT - 1)]
    inside = [(t // P == s) for s in range(NT - 1)]
    q_rows = [w * (P * (s + 1) - t) for s, w in enumerate(later)] + [w * 1 for w in later] + [0 * t, 0 * t]
    k_rows = [w * 1 for w in inside] + [w * (t - P * (s + 1)) for s, w in enumerate(inside)] + [0 * t - 1, 0 * t - 1]
    column = np.arange(2 * T - P)[None, :] - (T - P)
    heads = 8 * np.arange(2)[None, :] + p // D
    return {
        "identity": np.eye(P, dtype=f),
        "earlier": (p < np.arange(P)[None, :]).astype(f),
        "relative": (np.minimum(column - p, 0) * ((column >= 0) & (column < P))).astype(f),
        "relative_block": np.minimum(p - np.arange(P)[None, :], 0).astype(f),
        "stack_rows": np.stack([np.array(q_rows), np.array(k_rows)], 1).astype(f),
        "q_scale": (D**-0.5 / np.array(slopes(), f)[heads]).astype(f),
        "expert_numbers": np.arange(E, dtype=f),
        "token_numbers": (p + P * np.arange(NT)[None, :]).astype(f),
        "empty_numbers": (N + p + P * np.arange(NS)[None, :]).astype(f),
    }


def kernel(**inputs):
    import concourse.bacc as _bacc
    import numpy as _np
    from concourse.bass_utils import run_bass_kernel_spmd as _run

    nc = _bacc.Bacc("TRN2", target_bir_lowering=False, num_devices=1)
    arrays, args = {}, []
    for name, a in [*((k, inputs[k]) for k in _INS), *constants().items()]:
        a = _np.ascontiguousarray(a)
        arrays[f"in_{name}_dram"] = a
        args.append(nc.dram_tensor(f"in_{name}_dram", a.shape, mybir.dt.from_np(a.dtype), kind="ExternalInput").ap())
    args.append(nc.dram_tensor("out_0_dram", (N + CAP, C), F32, kind="ExternalOutput").ap())
    tower(nc, *args)
    r = _run(nc, [arrays], core_ids=[0])
    return _np.asarray(r.results[0]["out_0_dram"])[:N].reshape(NB, T, C)
```
